# Optimizing a Trainium2 kernel written in Bass

```python
import numpy as np
import jax
import jax.numpy as jnp

def _softmax(x, axis=-1):
    return jax.nn.softmax(x, axis=axis)

def _gelu(x):
    return jax.nn.gelu(x, approximate=True)

def _silu(x):
    return jax.nn.silu(x)

def _sigmoid(x):
    return jax.nn.sigmoid(x)

def _layernorm(x, axis=-1, eps=1e-05):
    m = jnp.mean(x, axis=axis, keepdims=True)
    v = jnp.var(x, axis=axis, keepdims=True)
    return (x - m) / jnp.sqrt(v + eps)

def _scatter_add(tgt, idx, src, axis=0):
    return tgt.at[idx].add(src)

def _segment_sum(src, seg, n):
    return jax.ops.segment_sum(src, seg, n)
kernel_name = 'mk_vit_tower_d2_tok_img1024_r4_329e6b'

def setup_inputs(seed: int=0):
    np.random.seed(seed)
    _w = jnp.asarray

    def _rec_inputs():
        import jax
        import jax.numpy as jnp
        _rk = jax.random.key(seed)
        x = -0.00016672 + 0.999947 * jax.random.normal(jax.random.fold_in(_rk, 1), (32, 3, 96, 96), jnp.float32)
        return x
    x = _rec_inputs()

    def _L0_tok_setup():
        import jax, jax.numpy as jnp
        import numpy as np
        B, C, H, W = (64, 3, 96, 96)
        P = 16
        NP = H // P * (W // P)
        PD = C * P * P
        ED = 256
        NCLS = 1

        def _layernorm(x, g, b, eps=1e-05):
            mu = jnp.mean(x, axis=-1, keepdims=True)
            var = jnp.mean(jnp.square(x - mu), axis=-1, keepdims=True)
            return (x - mu) * jax.lax.rsqrt(var + eps) * g + b
        key = jax.random.key(seed)
        ks = jax.random.split(key, 8)
        x = jax.random.normal(ks[0], (B, C, H, W), dtype=jnp.float32)
        ln1_g = jnp.ones((PD,), jnp.float32)
        ln1_b = jnp.zeros((PD,), jnp.float32)
        W_proj = jax.random.normal(ks[1], (PD, ED), jnp.float32) / np.sqrt(PD)
        b_proj = jnp.zeros((ED,), jnp.float32)
        ln2_g = jnp.ones((ED,), jnp.float32)
        ln2_b = jnp.zeros((ED,), jnp.float32)
        cls_token = jax.random.normal(ks[2], (1, NCLS, ED), jnp.float32)
        pos_emb = jax.random.normal(ks[3], (1, NP + NCLS, ED), jnp.float32)
        return {'x': x, 'ln1_g': ln1_g, 'ln1_b': ln1_b, 'W_proj': W_proj, 'b_proj': b_proj, 'ln2_g': ln2_g, 'ln2_b': ln2_b, 'cls_token': cls_token, 'pos_emb': pos_emb}
    _L0_tok_all = _L0_tok_setup()
    _L0_tok_in = {k: v for k, v in _L0_tok_all.items() if k in ('ln1_g', 'ln1_b', 'W_proj', 'b_proj', 'ln2_g', 'ln2_b', 'cls_token', 'pos_emb')}
    del _L0_tok_all

    def _L0_attn_setup():
        import jax, jax.numpy as jnp
        import numpy as np
        NUM_HEADS = 16
        TOP_K = 128
        LN_EPS = 1e-05

        def layernorm(x, w, b):
            mu = jnp.mean(x, axis=-1, keepdims=True)
            var = jnp.mean((x - mu) ** 2, axis=-1, keepdims=True)
            return (x - mu) * jax.lax.rsqrt(var + LN_EPS) * w + b

        def top_k_activation(x, k):
            n = x.shape[-1]
            if k >= n:
                return x
            vals, idx = jax.lax.top_k(x, k)
            flat = x.reshape(-1, n)
            rows = jnp.arange(flat.shape[0])[:, None]
            out = jnp.zeros_like(flat).at[rows, idx.reshape(-1, k)].set(vals.reshape(-1, k))
            return out.reshape(x.shape)
        key = jax.random.key(seed)
        ks = jax.random.split(key, 8)
        B, S, H = (2, 512, 256)
        hd = H // NUM_HEADS
        return {'x': jax.random.normal(ks[0], (B, S, H), dtype=jnp.float32), 'W_Q': jax.random.normal(ks[1], (H, H), dtype=jnp.float32) * 0.02, 'W_K': jax.random.normal(ks[2], (H, H), dtype=jnp.float32) * 0.02, 'W_V': jax.random.normal(ks[3], (H, H), dtype=jnp.float32) * 0.02, 'W_O': jax.random.normal(ks[4], (H, H), dtype=jnp.float32) * 0.02, 'q_ln_w': jnp.ones((hd,), dtype=jnp.float32), 'q_ln_b': jnp.zeros((hd,), dtype=jnp.float32), 'k_ln_w': jnp.ones((hd,), dtype=jnp.float32), 'k_ln_b': jnp.zeros((hd,), dtype=jnp.float32), 'sparse_W_V': jax.random.normal(ks[5], (NUM_HEADS, hd, TOP_K), dtype=jnp.float32) * 0.02, 'sparse_W_O': jax.random.normal(ks[6], (NUM_HEADS, TOP_K, hd), dtype=jnp.float32) * 0.02}
    _L0_attn_all = _L0_attn_setup()
    _L0_attn_in = {k: v for k, v in _L0_attn_all.items() if k in ('W_Q', 'W_K', 'W_V', 'W_O', 'q_ln_w', 'q_ln_b', 'k_ln_w', 'k_ln_b', 'sparse_W_V', 'sparse_W_O')}
    del _L0_attn_all

    def _L0_ffn_setup():
        import jax, jax.numpy as jnp
        import numpy as np
        NUM_EXPERTS = 8
        N_EMBD = 256
        D_FF = 4 * N_EMBD
        B, S = (4, 512)
        key = jax.random.key(seed)
        ks = jax.random.split(key, 6)
        x = jax.random.normal(ks[0], (B, S, N_EMBD), dtype=jnp.float32)
        gate_w = jax.random.normal(ks[1], (N_EMBD, NUM_EXPERTS), dtype=jnp.float32) * 0.02
        w1 = jax.random.normal(ks[2], (NUM_EXPERTS, N_EMBD, D_FF), dtype=jnp.float32) * 0.02
        b1 = jnp.zeros((NUM_EXPERTS, D_FF), dtype=jnp.float32)
        w2 = jax.random.normal(ks[3], (NUM_EXPERTS, D_FF, N_EMBD), dtype=jnp.float32) * 0.02
        b2 = jnp.zeros((NUM_EXPERTS, N_EMBD), dtype=jnp.float32)
        return {'x': x, 'gate_w': gate_w, 'w1': w1, 'b1': b1, 'w2': w2, 'b2': b2}
    _L0_ffn_all = _L0_ffn_setup()
    _L0_ffn_in = {k: v for k, v in _L0_ffn_all.items() if k in ('gate_w', 'w1', 'b1', 'w2', 'b2')}
    del _L0_ffn_all

    def _L1_attn_setup():
        import jax, jax.numpy as jnp
        import numpy as np
        import math
        D_MODEL, N_HEADS, D_K, D_C, D_HR = (256, 8, 128, 32, 32)
        B, S = (4, 512)
        key = jax.random.key(seed)
        ks = jax.random.split(key, 17)

        def lin(k, fan_in, fan_out):
            lim = 1.0 / math.sqrt(fan_in)
            kw, kb = jax.random.split(k)
            W = jax.random.uniform(kw, (fan_in, fan_out), jnp.float32, -lim, lim)
            b = jax.random.uniform(kb, (fan_out,), jnp.float32, -lim, lim)
            return (W, b)
        W_DQ, b_DQ = lin(ks[0], D_MODEL, D_C)
        W_UQ, b_UQ = lin(ks[1], D_C, N_HEADS * D_K)
        W_DKV, b_DKV = lin(ks[2], D_MODEL, D_C)
        W_UK, b_UK = lin(ks[3], D_C, N_HEADS * D_K)
        W_UV, b_UV = lin(ks[4], D_C, N_HEADS * D_K)
        W_QR, b_QR = lin(ks[5], D_C, N_HEADS * D_HR)
        W_KR, b_KR = lin(ks[6], D_MODEL, D_HR)
        W_O, b_O = lin(ks[7], N_HEADS * D_K, D_MODEL)
        h_t = jax.random.normal(ks[8], (B, S, D_MODEL), jnp.float32)
        return {'h_t': h_t, 'W_DQ': W_DQ, 'b_DQ': b_DQ, 'W_UQ': W_UQ, 'b_UQ': b_UQ, 'W_DKV': W_DKV, 'b_DKV': b_DKV, 'W_UK': W_UK, 'b_UK': b_UK, 'W_UV': W_UV, 'b_UV': b_UV, 'W_QR': W_QR, 'b_QR': b_QR, 'W_KR': W_KR, 'b_KR': b_KR, 'W_O': W_O, 'b_O': b_O}
    _L1_attn_all = _L1_attn_setup()
    _L1_attn_in = {k: v for k, v in _L1_attn_all.items() if k in ('W_DQ', 'b_DQ', 'W_UQ', 'b_UQ', 'W_DKV', 'b_DKV', 'W_UK', 'b_UK', 'W_UV', 'b_UV', 'W_QR', 'b_QR', 'W_KR', 'b_KR', 'W_O', 'b_O')}
    del _L1_attn_all

    def _L1_ffn_setup():
        import jax, jax.numpy as jnp
        import numpy as np
        B, S, H = (2, 512, 256)
        N, F, SF, K = (16, 256, 1024, 1)
        key = jax.random.key(seed)
        ks = jax.random.split(key, 7)
        std = 0.02
        return {'hidden_states': jax.random.normal(ks[0], (B, S, H), dtype=jnp.float32), 'router_w': jax.random.normal(ks[1], (N, H), dtype=jnp.float32) * std, 'gate_up_proj': jax.random.normal(ks[2], (N, H, 2 * F), dtype=jnp.float32) * std, 'down_proj': jax.random.normal(ks[3], (N, F, H), dtype=jnp.float32) * std, 'shared_gate_w': jax.random.normal(ks[4], (SF, H), dtype=jnp.float32) * std, 'shared_up_w': jax.random.normal(ks[5], (SF, H), dtype=jnp.float32) * std, 'shared_down_w': jax.random.normal(ks[6], (H, SF), dtype=jnp.float32) * std}
    _L1_ffn_all = _L1_ffn_setup()
    _L1_ffn_in = {k: v for k, v in _L1_ffn_all.items() if k in ('router_w', 'gate_up_proj', 'down_proj', 'shared_gate_w', 'shared_up_w', 'shared_down_w')}
    del _L1_ffn_all
    return {'x': x, 'L0_tok_ln1_g': _L0_tok_in['ln1_g'], 'L0_tok_ln1_b': _L0_tok_in['ln1_b'], 'L0_tok_W_proj': _L0_tok_in['W_proj'], 'L0_tok_b_proj': _L0_tok_in['b_proj'], 'L0_tok_ln2_g': _L0_tok_in['ln2_g'], 'L0_tok_ln2_b': _L0_tok_in['ln2_b'], 'L0_tok_cls_token': _L0_tok_in['cls_token'], 'L0_tok_pos_emb': _L0_tok_in['pos_emb'], 'L0_attn_W_Q': _L0_attn_in['W_Q'], 'L0_attn_W_K': _L0_attn_in['W_K'], 'L0_attn_W_V': _L0_attn_in['W_V'], 'L0_attn_W_O': _L0_attn_in['W_O'], 'L0_attn_q_ln_w': _L0_attn_in['q_ln_w'], 'L0_attn_q_ln_b': _L0_attn_in['q_ln_b'], 'L0_attn_k_ln_w': _L0_attn_in['k_ln_w'], 'L0_attn_k_ln_b': _L0_attn_in['k_ln_b'], 'L0_attn_sparse_W_V': _L0_attn_in['sparse_W_V'], 'L0_attn_sparse_W_O': _L0_attn_in['sparse_W_O'], 'L0_ffn_gate_w': _L0_ffn_in['gate_w'], 'L0_ffn_w1': _L0_ffn_in['w1'], 'L0_ffn_b1': _L0_ffn_in['b1'], 'L0_ffn_w2': _L0_ffn_in['w2'], 'L0_ffn_b2': _L0_ffn_in['b2'], 'L1_attn_W_DQ': _L1_attn_in['W_DQ'], 'L1_attn_b_DQ': _L1_attn_in['b_DQ'], 'L1_attn_W_UQ': _L1_attn_in['W_UQ'], 'L1_attn_b_UQ': _L1_attn_in['b_UQ'], 'L1_attn_W_DKV': _L1_attn_in['W_DKV'], 'L1_attn_b_DKV': _L1_attn_in['b_DKV'], 'L1_attn_W_UK': _L1_attn_in['W_UK'], 'L1_attn_b_UK': _L1_attn_in['b_UK'], 'L1_attn_W_UV': _L1_attn_in['W_UV'], 'L1_attn_b_UV': _L1_attn_in['b_UV'], 'L1_attn_W_QR': _L1_attn_in['W_QR'], 'L1_attn_b_QR': _L1_attn_in['b_QR'], 'L1_attn_W_KR': _L1_attn_in['W_KR'], 'L1_attn_b_KR': _L1_attn_in['b_KR'], 'L1_attn_W_O': _L1_attn_in['W_O'], 'L1_attn_b_O': _L1_attn_in['b_O'], 'L1_ffn_router_w': _L1_ffn_in['router_w'], 'L1_ffn_gate_up_proj': _L1_ffn_in['gate_up_proj'], 'L1_ffn_down_proj': _L1_ffn_in['down_proj'], 'L1_ffn_shared_gate_w': _L1_ffn_in['shared_gate_w'], 'L1_ffn_shared_up_w': _L1_ffn_in['shared_up_w'], 'L1_ffn_shared_down_w': _L1_ffn_in['shared_down_w']}

def reference(x, L0_tok_ln1_g, L0_tok_ln1_b, L0_tok_W_proj, L0_tok_b_proj, L0_tok_ln2_g, L0_tok_ln2_b, L0_tok_cls_token, L0_tok_pos_emb, L0_attn_W_Q, L0_attn_W_K, L0_attn_W_V, L0_attn_W_O, L0_attn_q_ln_w, L0_attn_q_ln_b, L0_attn_k_ln_w, L0_attn_k_ln_b, L0_attn_sparse_W_V, L0_attn_sparse_W_O, L0_ffn_gate_w, L0_ffn_w1, L0_ffn_b1, L0_ffn_w2, L0_ffn_b2, L1_attn_W_DQ, L1_attn_b_DQ, L1_attn_W_UQ, L1_attn_b_UQ, L1_attn_W_DKV, L1_attn_b_DKV, L1_attn_W_UK, L1_attn_b_UK, L1_attn_W_UV, L1_attn_b_UV, L1_attn_W_QR, L1_attn_b_QR, L1_attn_W_KR, L1_attn_b_KR, L1_attn_W_O, L1_attn_b_O, L1_ffn_router_w, L1_ffn_gate_up_proj, L1_ffn_down_proj, L1_ffn_shared_gate_w, L1_ffn_shared_up_w, L1_ffn_shared_down_w):
    import jax
    import jax.numpy as jnp

    def _L0_tok_ref(x, ln1_g, ln1_b, W_proj, b_proj, ln2_g, ln2_b, cls_token, pos_emb):
        import jax, jax.numpy as jnp
        import numpy as np
        B, C, H, W = (64, 3, 96, 96)
        P = 16
        NP = H // P * (W // P)
        PD = C * P * P
        ED = 256
        NCLS = 1

        def _layernorm(x, g, b, eps=1e-05):
            mu = jnp.mean(x, axis=-1, keepdims=True)
            var = jnp.mean(jnp.square(x - mu), axis=-1, keepdims=True)
            return (x - mu) * jax.lax.rsqrt(var + eps) * g + b
        b = x.shape[0]
        h, w = (H // P, W // P)
        patches = x.reshape(b, C, h, P, w, P)
        patches = patches.transpose(0, 2, 4, 3, 5, 1).reshape(b, h * w, P * P * C)
        z = _layernorm(patches, ln1_g, ln1_b)
        z = jnp.einsum('bnp,pe->bne', z, W_proj) + b_proj
        z = _layernorm(z, ln2_g, ln2_b)
        cls = jnp.broadcast_to(cls_token, (b, NCLS, ED))
        z = jnp.concatenate([cls, z], axis=1)
        z = z + pos_emb
        return z

    def _L0_attn_ref(x, W_Q, W_K, W_V, W_O, q_ln_w, q_ln_b, k_ln_w, k_ln_b, sparse_W_V, sparse_W_O):
        import jax, jax.numpy as jnp
        import numpy as np
        NUM_HEADS = 16
        TOP_K = 128
        LN_EPS = 1e-05

        def layernorm(x, w, b):
            mu = jnp.mean(x, axis=-1, keepdims=True)
            var = jnp.mean((x - mu) ** 2, axis=-1, keepdims=True)
            return (x - mu) * jax.lax.rsqrt(var + LN_EPS) * w + b

        def top_k_activation(x, k):
            n = x.shape[-1]
            if k >= n:
                return x
            vals, idx = jax.lax.top_k(x, k)
            flat = x.reshape(-1, n)
            rows = jnp.arange(flat.shape[0])[:, None]
            out = jnp.zeros_like(flat).at[rows, idx.reshape(-1, k)].set(vals.reshape(-1, k))
            return out.reshape(x.shape)
        B, S, H = x.shape
        nh = sparse_W_V.shape[0]
        hd = H // nh

        def split_heads(t):
            return t.reshape(B, S, nh, hd).transpose(0, 2, 1, 3)
        Q = split_heads(jnp.einsum('bsd,od->bso', x, W_Q))
        K = split_heads(jnp.einsum('bsd,od->bso', x, W_K))
        V = split_heads(jnp.einsum('bsd,od->bso', x, W_V))
        Q = layernorm(Q, q_ln_w, q_ln_b)
        K = layernorm(K, k_ln_w, k_ln_b)
        scores = jnp.einsum('bhqd,bhkd->bhqk', Q, K) / jnp.sqrt(jnp.float32(hd))
        attn = jax.nn.softmax(scores, axis=-1)
        context = jnp.einsum('bhqk,bhkd->bhqd', attn, V)
        context_flat = context.transpose(0, 2, 1, 3).reshape(B * nh, S, hd)
        v_weights = sparse_W_V.mean(axis=2)
        z = jnp.einsum('bnd,hd->bhn', context_flat, v_weights)
        z_sparse = top_k_activation(z, TOP_K)
        o_weights = sparse_W_O.mean(axis=1)
        y_flat = jnp.einsum('bhn,hd->bnd', z_sparse, o_weights)
        y = y_flat.reshape(B, nh, S, hd).transpose(0, 2, 1, 3).reshape(B, S, H)
        y = jnp.einsum('bsd,od->bso', y, W_O)
        return y

    def _L0_ffn_ref(x, gate_w, w1, b1, w2, b2):
        import jax, jax.numpy as jnp
        import numpy as np
        NUM_EXPERTS = 8
        N_EMBD = 256
        D_FF = 4 * N_EMBD
        B, S = (4, 512)
        Bb, Ss, D = x.shape
        x_flat = x.reshape(-1, D)
        router_logits = x_flat @ gate_w
        router_probs = jax.nn.softmax(router_logits, axis=-1)
        expert_idx = jnp.argmax(router_probs, axis=-1)
        expert_w = jnp.take_along_axis(router_probs, expert_idx[:, None], axis=1)[:, 0]
        out = jnp.zeros_like(x_flat)
        for e in range(NUM_EXPERTS):
            h = jax.nn.gelu(x_flat @ w1[e] + b1[e], approximate=False)
            y = h @ w2[e] + b2[e]
            sel = expert_idx == e
            out = out + jnp.where(sel, expert_w, 0.0)[:, None] * y
        return out.reshape(Bb, Ss, D)

    def _L1_attn_ref(h_t, W_DQ, b_DQ, W_UQ, b_UQ, W_DKV, b_DKV, W_UK, b_UK, W_UV, b_UV, W_QR, b_QR, W_KR, b_KR, W_O, b_O):
        import jax, jax.numpy as jnp
        import numpy as np
        import math
        D_MODEL, N_HEADS, D_K, D_C, D_HR = (256, 8, 128, 32, 32)
        B, S = (4, 512)
        b, s, _ = h_t.shape
        c_q = h_t @ W_DQ + b_DQ
        c_kv = h_t @ W_DKV + b_DKV
        q_c = (c_q @ W_UQ + b_UQ).reshape(b, s, N_HEADS, D_K).transpose(0, 2, 1, 3)
        k_c = (c_kv @ W_UK + b_UK).reshape(b, s, N_HEADS, D_K).transpose(0, 2, 1, 3)
        v_c = (c_kv @ W_UV + b_UV).reshape(b, s, N_HEADS, D_K).transpose(0, 2, 1, 3)
        q_r = (c_q @ W_QR + b_QR).reshape(b, s, N_HEADS, D_HR).transpose(0, 2, 1, 3)
        k_r = (h_t @ W_KR + b_KR)[:, None, :, :]
        k_r = jnp.broadcast_to(k_r, (b, N_HEADS, s, D_HR))
        q = jnp.concatenate([q_c, q_r], axis=-1)
        k = jnp.concatenate([k_c, k_r], axis=-1)
        scale = 1.0 / math.sqrt(D_K + D_HR)
        scores = jnp.einsum('bhsd,bhtd->bhst', q, k) * scale
        attn = jax.nn.softmax(scores, axis=-1)
        o = jnp.einsum('bhst,bhtd->bhsd', attn, v_c)
        o = o.transpose(0, 2, 1, 3).reshape(b, s, N_HEADS * D_K)
        return o @ W_O + b_O

    def _L1_ffn_ref(hidden_states, router_w, gate_up_proj, down_proj, shared_gate_w, shared_up_w, shared_down_w):
        import jax, jax.numpy as jnp
        import numpy as np
        B, S, H = (2, 512, 256)
        N, F, SF, K = (16, 256, 1024, 1)
        b, s, h = hidden_states.shape
        hidden = hidden_states.reshape(-1, h)
        t = hidden.shape[0]
        logits = hidden @ router_w.T
        top_vals, top_idx = jax.lax.top_k(logits, K)
        scores = jnp.full_like(logits, -jnp.inf)
        scores = scores.at[jnp.arange(t)[:, None], top_idx].set(top_vals)
        scores = jax.nn.sigmoid(scores.astype(jnp.float32)).astype(hidden.dtype)
        routed_in = hidden[None, :, :] * scores.T[:, :, None]
        gate_up = jnp.einsum('nth,nhf->ntf', routed_in, gate_up_proj)
        gate, up = jnp.split(gate_up, 2, axis=-1)
        routed_out = jnp.einsum('ntf,nfh->nth', up * jax.nn.silu(gate), down_proj)
        expert_sum = routed_out.sum(axis=0)
        shared = jax.nn.silu(hidden @ shared_gate_w.T) * (hidden @ shared_up_w.T) @ shared_down_w.T
        return (shared + expert_sum).reshape(b, s, h)
    h = _L0_tok_ref(x, L0_tok_ln1_g, L0_tok_ln1_b, L0_tok_W_proj, L0_tok_b_proj, L0_tok_ln2_g, L0_tok_ln2_b, L0_tok_cls_token, L0_tok_pos_emb)
    h = h + _L0_attn_ref(_layernorm(h, axis=-1), L0_attn_W_Q, L0_attn_W_K, L0_attn_W_V, L0_attn_W_O, L0_attn_q_ln_w, L0_attn_q_ln_b, L0_attn_k_ln_w, L0_attn_k_ln_b, L0_attn_sparse_W_V, L0_attn_sparse_W_O)
    h = h + _L0_ffn_ref(_layernorm(h, axis=-1), L0_ffn_gate_w, L0_ffn_w1, L0_ffn_b1, L0_ffn_w2, L0_ffn_b2)
    h = h + _L1_attn_ref(_layernorm(h, axis=-1), L1_attn_W_DQ, L1_attn_b_DQ, L1_attn_W_UQ, L1_attn_b_UQ, L1_attn_W_DKV, L1_attn_b_DKV, L1_attn_W_UK, L1_attn_b_UK, L1_attn_W_UV, L1_attn_b_UV, L1_attn_W_QR, L1_attn_b_QR, L1_attn_W_KR, L1_attn_b_KR, L1_attn_W_O, L1_attn_b_O)
    h = h + _L1_ffn_ref(_layernorm(h, axis=-1), L1_ffn_router_w, L1_ffn_gate_up_proj, L1_ffn_down_proj, L1_ffn_shared_gate_w, L1_ffn_shared_up_w, L1_ffn_shared_down_w)
    return h

_drawn_inputs = setup_inputs


def setup_inputs(seed=0):
    import zlib

    import numpy as np

    out = dict(_drawn_inputs(seed))
    spreads = {'L0_tok_ln1_g': (1.0, 0.2),
     'L0_tok_ln1_b': (0.0, 0.1),
     'L0_tok_b_proj': (0.0, 0.1),
     'L0_tok_ln2_g': (1.0, 0.2),
     'L0_tok_ln2_b': (0.0, 0.1),
     'L0_attn_q_ln_w': (1.0, 0.6),
     'L0_attn_q_ln_b': (0.0, 0.8),
     'L0_attn_k_ln_w': (1.0, 0.6),
     'L0_attn_k_ln_b': (0.0, 2.0),
     'L0_ffn_b1': (0.0, 0.8),
     'L0_ffn_b2': (0.0, 0.589)}
    factors = {'L0_attn_W_Q': 8.0,
     'L0_attn_W_K': 8.0,
     'L0_attn_W_V': 8.0,
     'L0_attn_W_O': 8.0,
     'L0_attn_sparse_W_V': 8.0,
     'L0_attn_sparse_W_O': 8.0,
     'L0_ffn_gate_w': 3.01,
     'L0_ffn_w1': 3.847,
     'L0_ffn_w2': 3.565,
     'L1_attn_W_DQ': 8.0,
     'L1_attn_b_DQ': 8.0,
     'L1_attn_W_UQ': 8.0,
     'L1_attn_b_UQ': 8.0,
     'L1_attn_b_DKV': 7.859,
     'L1_attn_W_UK': 8.0,
     'L1_attn_b_UK': 64.0,
     'L1_attn_W_QR': 8.0,
     'L1_attn_b_QR': 8.0,
     'L1_attn_W_KR': 8.0,
     'L1_attn_b_KR': 64.0,
     'L1_attn_b_O': 4.398,
     'L1_ffn_router_w': 8.0,
     'L1_ffn_gate_up_proj': 8.0,
     'L1_ffn_down_proj': 8.0,
     'L1_ffn_shared_gate_w': 8.0,
     'L1_ffn_shared_up_w': 8.0,
     'L1_ffn_shared_down_w': 8.0}
    for name, (base, spread) in spreads.items():
        noise = np.random.default_rng([zlib.crc32(name.encode()), seed]).standard_normal(out[name].shape)
        drawn = base * np.exp(spread * noise) if base else spread * noise
        out[name] = jnp.asarray(drawn.astype(out[name].dtype))
    for name, factor in factors.items():
        out[name] = (out[name] * factor).astype(out[name].dtype)
    return out
```

```python
import concourse.bass as bass
from concourse import mybir
from contextlib import ExitStack

F32 = mybir.dt.float32
BF16 = mybir.dt.bfloat16
I32 = mybir.dt.int32
U32 = mybir.dt.uint32
ALU = mybir.AluOpType
ACT = mybir.ActivationFunctionType
AX = mybir.AxisListType

P = 128
B, C, HW, PS = 32, 3, 96, 16
G = HW // PS
ED = 256
KC = ED // P
PD = C * PS * PS
PC = PD // P
NP = G * G
S = NP + 1
TOK = B * S
NT = 10
QP = 64
PAIRS = B // 2
EPS = 1e-5

H0, HD0 = 16, 16
E0, FF0, NT0 = 8, 1024, 17
H1, DK, DC = 8, 128, 32
E1, FF1, NT1, SF = 16, 256, 25, 1024

assert NT0 == (TOK + E0 * (P - 1)) // P and NT1 == (TOK + E1 * (P - 1)) // P
BLOCKS = [(0, 512), (512, 512), (1024, TOK - 1024)]


class Chain:

    def __init__(self, engine, sem, per=None):
        self.engine, self.sem, self.per, self.base, self.n = engine, sem, per, 0, 0

    def at(self, i):
        assert self.n in (0, self.per), (self.n, self.per)
        self.base, self.n = i * self.per, 0

    def did(self, ins):
        ins.then_inc(self.sem, 1)
        self.n += 1

    def wait(self):
        self.engine.wait_ge(self.sem, self.base + self.n)


def pipelined(engine, n, *stages):
    longest = max(delay for _, delay in stages)

    def step(at, r=None):
        for f, delay in stages:
            i = at - delay
            if r is not None:
                f(r * 2 + i, i % 2, r + i // 2)
            elif 0 <= i < n:
                f(i, i % 2, i // 2)

    first = (longest + 3) // 2
    for at in range(2 * first):
        step(at)
    with engine.Fori(first, n // 2) as r:
        step(0, r)
        step(1, r)
    for at in range(2 * (n // 2), n + longest):
        step(at)


def vit_tower(nc, a, out):
    ctx = ExitStack()
    with ctx:
        def sb(name, shape, dt=F32):
            return ctx.enter_context(nc.sbuf_tensor(name, shape, dt))[:]

        def sem(name):
            return ctx.enter_context(nc.semaphore(name))

        sorted_x = [nc.dram_tensor("sorted_x0", (NT0 * P, ED), F32, kind="Internal").ap(),
                    nc.dram_tensor("sorted_x1", (NT1 * P, ED), F32, kind="Internal").ap()]
        sorted_y = [nc.dram_tensor("sorted_y0", (NT0 * P, ED), F32, kind="Internal").ap(),
                    nc.dram_tensor("sorted_y1", (NT1 * P, ED), F32, kind="Internal").ap()]

        shuffled = nc.dram_tensor("shuffled", (HD0, S * H0, B), F32, kind="Internal").ap()

        h = sb("h", [P, NT, ED])
        xn = sb("xn", [P, NT, ED])
        xT = sb("xT", [P, KC, NT * P])
        ident = sb("ident", [P, P])
        block16 = sb("block16", [P, 8, 16])
        centre = sb("centre", [P, P])
        average = sb("average", [P, P])
        ones_row = sb("ones_row", [1, P])
        before = sb("before", [P, P], BF16)
        ones16 = sb("ones16", [P, P], BF16)
        iota_e = sb("iota_e", [P, 17 * 2])
        thresholds = sb("thresholds", [P, NT])
        lower_e = sb("lower_e", [P, E1, E1])
        eps_col = sb("eps_col", [P, 1])
        stats = sb("stats", [P, NT, 3, 6])
        meanvar = sb("meanvar", [P, NT, 2])
        sd = sb("sd", [P, NT])
        rstd = sb("rstd", [P, NT])

        logits = sb("logits", [P, NT, E1])
        top = sb("top", [P, NT])
        first = sb("first", [P, NT])
        mask = sb("mask", [P, NT, E1])
        onehot = sb("onehot", [P, NT, E1], BF16)
        weight = sb("weight", [P, NT])
        counts_over = sb("counts_over", [P, E1, NT])
        tiles_e = sb("tiles_e", [P, E1])
        base_e = sb("base_e", [P, E1])
        end_e = sb("end_e", [P, E1])
        base_tmp = sb("base_tmp", [P, E1, E1])
        slot_f = sb("slot_f", [P, NT])
        slot = sb("slot", [P, 2, NT], I32)
        tile_cmp = sb("tile_cmp", [1, NT1, E1])
        tile_e_f = sb("tile_e_f", [1, NT1])
        tile_e = sb("tile_e", [1, 2, NT1], I32)
        onehot_f = sb("onehot_f", [P, NT, E0])

        gate_w0 = sb("gate_w0", [P, KC, E0])
        router1 = sb("router1", [E1, ED])
        routerT1 = sb("routerT1", [P, KC, E1])
        b1T = sb("b1T", [P, E0, FF0 // P])
        b2 = sb("b2", [E0, ED])
        b1_rows = sb("b1_rows", [E0 * FF0 // P, P])
        q_w = sb("q_w", [P, 1])
        q_b = sb("q_b", [P, 1])
        k_w = sb("k_w", [P, 1])
        k_b = sb("k_b", [P, 1])
        k_of = sb("k_of", [P, 4])
        down_u = sb("down_u", [P, KC, P])
        down_k = sb("down_k", [P, KC, P])
        bias_u = sb("bias_u", [P, 1])
        bias_k = sb("bias_k", [P, 1])
        keyT = sb("keyT", [P, H1 // 2, P])
        valO = sb("valO", [P, 2, ED])
        bias_o = sb("bias_o", [P, ED])

        KB = 256
        R1, R2, R3, RE = 0, 64 * KB, 96 * KB, 156 * KB
        arena = sb("arena", [P, RE])
        arena_ap = arena[:, :]

        class Area:

            def __init__(self, start, end):
                self.next, self.end = start, end

            def take(self, *shape):
                n = 1
                for x in shape:
                    n *= x
                v = arena_ap[:, self.next:self.next + n]
                self.next += n
                assert self.next <= self.end, (self.next, self.end)
                if len(shape) == 1:
                    return v
                names = "abcd"[:len(shape)]
                return v.rearrange(f"p ({' '.join(names)}) -> p {' '.join(names)}",
                                   **{c: s for c, s in zip(names, shape)})

        w1 = arena_ap[:, R1:R1 + E0 * KC * FF0]
        w2 = arena_ap[:, R2:R2 + E0 * FF0 // P * ED]
        gate_up = arena_ap[:, R1:R1 + E1 * KC * 2 * FF1]
        down = arena_ap[:, R2:R2 + E1 * FF1 // P * ED]

        wx = Area(R2 - 8 * KB, R2)
        qT, kT, vT, woe = (wx.take(KC, ED) for _ in range(4))

        prep = Area(R2, R3)
        wq_raw, wk_raw, wv_raw, wo_raw = (prep.take(KC, ED) for _ in range(4))
        uk_raw, uq_raw, uv_raw = (prep.take(H1 * DK) for _ in range(3))
        qr_raw = prep.take(H1, P)
        ukT = prep.take(H1, P)
        uqT = prep.take(H1, DC + 1)
        uvT = prep.take(H1, DC + 1)
        rawsq = Area(R2 + 8 * KB, R3)
        raw = rawsq.take(2, 512)
        sq = rawsq.take(2, 512)

        emb = Area(R3, RE)
        x_a = emb.take(C, PS, HW)
        wo1_raw = emb.take(H1, ED)
        sparse_v = emb.take(16, P)
        sparse_o = emb.take(P, 16)
        woT = emb.take(KC, ED)
        b_o = emb.take(ED)
        tiled_v, tiled_o, blockM = (emb.take(P) for _ in range(3))
        sv_w, so_w = emb.take(16), emb.take(16)
        emb1 = Area(R1, R2 - 8 * KB)
        x_b = emb1.take(C, PS, HW // 2)
        patch = emb1.take(2, PD)
        patchT = emb1.take(2, PC, P)
        w_proj = emb1.take(PC, ED)
        wg_proj = emb1.take(PC, ED)
        ln1_g, ln1_b = emb1.take(PC), emb1.take(PC)
        b_proj, bias_z, ln2_g, ln2_b = (emb1.take(ED) for _ in range(4))
        zero = emb1.take(8 * ED)

        at0 = Area(R3, RE)
        qn = at0.take(KC, B, S)
        kn = at0.take(KC, B, S)
        ctxT = at0.take(KC, S * B)
        q_ring = at0.take(2, KC, 2, 2 * QP)
        k_ring = [at0.take(KC, 2, 4, S) for _ in range(2)]
        xv = at0.take(2, KC, 2 * QP)
        v_ring = at0.take(2, 2, ED)
        yT = qn.rearrange("p c b n -> p c (b n)")
        p_ring = at0.take(2, 16, QP)
        pT = [at0.take(16, S) for _ in range(2)]
        mx = at0.take(2, 16)
        sm = at0.take(2, 16)

        moe = Area(R3 + 32 * KB, RE)
        onehotT = moe.take(NT, P)
        rows_in = moe.take(2, ED)
        rowsT = moe.take(2, KC, P)
        hid = moe.take(2, FF0)
        hidT = moe.take(2, FF0 // P, P)
        rows_out = moe.take(2, ED)

        at1 = Area(R3, RE)
        lat_u = at1.take(B, QP)
        lat_k = at1.take(B * S)
        keys = at1.take(H1 // 2, B * S)
        ctx1T = at1.take(2, NT * P)
        lat_v = at1.take(2, 2, 2 * DC)
        u_ring = at1.take(2, 2, 2 * QP)
        lk_ring = at1.take(2, 2 * QP)
        p1_ring = at1.take(2, 8, QP)
        pT1 = [at1.take(4, 2, S) for _ in range(2)]
        mx1 = at1.take(2, 8)
        sm1 = at1.take(2, 8)

        sh = Area(R3, R3 + 24 * KB)
        gT = sh.take(KC, SF)
        upT = sh.take(KC, SF)
        dT = sh.take(SF // P, ED)
        sh2 = Area(R3 + 24 * KB, RE)
        sT = sh2.take(SF // P, 512)
        sg = sh2.take(2, 512)
        g_raw = sh2.take(SF // P, ED)
        up_raw = sh2.take(SF // P, ED)
        d_raw = Area(R3 + 24 * KB, RE).take(KC, SF)

        psum = ctx.enter_context(nc.psum_tensor("psum", [P, 8 * 512], F32))

        def bank(b, n=1):
            return psum[:, 512 * b:512 * (b + n)]

        x = a["x"]
        loads = {}
        loads["x_a"] = [(x_a[32 * r:32 * r + 32, :, :, :].rearrange("p c i w -> p c (i w)"),
                         x[:, :, PS * r:PS * (r + 1), :].rearrange("b c i w -> b c (i w)")) for r in range(4)]
        loads["x_b"] = [(x_b[64 * wh + 32 * r:64 * wh + 32 * r + 32, c, :, :],
                         x[:, c, PS * (4 + r):PS * (5 + r), 48 * wh:48 * wh + 48])
                        for wh in range(2) for r in range(2) for c in range(C)]
        wp = a["L0_tok_W_proj"].rearrange("(f c) e -> c f e", c=C)
        g1 = a["L0_tok_ln1_g"].rearrange("(f c o) -> c f o", c=C, o=1)
        b1_ = a["L0_tok_ln1_b"].rearrange("(f c o) -> c f o", c=C, o=1)
        loads["proj"] = [(w_proj[:, 2 * c + k, :], wp[c, P * k:P * k + P, :]) for c in range(C) for k in range(2)] + [
            (ln1_g[:, 2 * c + k:2 * c + k + 1], g1[c, P * k:P * k + P, :]) for c in range(C) for k in range(2)] + [
            (ln1_b[:, 2 * c + k:2 * c + k + 1], b1_[c, P * k:P * k + P, :]) for c in range(C) for k in range(2)] + [
            (b_proj[0:1, :], a["L0_tok_b_proj"].rearrange("(o e) -> o e", o=1)),
            (b_o[0:1, :], a["L1_attn_b_O"].rearrange("(o e) -> o e", o=1)),
            (ln2_g, a["L0_tok_ln2_g"].rearrange("(o e) -> o e", o=1).broadcast_to((P, ED))),
            (ln2_b, a["L0_tok_ln2_b"].rearrange("(o e) -> o e", o=1).broadcast_to((P, ED)))]
        pos = a["L0_tok_pos_emb"]

        def token_runs():
            for j in range(4):
                yield 0, G, j, 1 + G * j
            for j in range(4):
                yield G, G // 2, j, 1 + G * (4 + j % 2) + G // 2 * (j // 2)

        loads["pos"] = [(h[32 * j:32 * j + 32, t + u, :], pos[0, n + u:n + u + 1, :].broadcast_to((32, ED)))
                        for t, nt, j, n in token_runs() for u in range(nt)]
        cls_pos = xn[0:32, NT - 1, :]
        loads["cls"] = [(h[0:32, NT - 1, :], pos[0, 0:1, :].broadcast_to((32, ED))),
                        (cls_pos, a["L0_tok_cls_token"][0, 0:1, :].broadcast_to((32, ED)))]

        def rows(name):
            return a[name].rearrange("(k p) e -> p k e", p=P)
        loads["attn0"] = [(wq_raw, rows("L0_attn_W_Q")), (wk_raw, rows("L0_attn_W_K")),
                          (wv_raw, rows("L0_attn_W_V")), (wo_raw, rows("L0_attn_W_O")),
                          (sparse_v[0:H0], a["L0_attn_sparse_W_V"]), (sparse_o[0:H0], a["L0_attn_sparse_W_O"])]

        def head_col(name):
            v = a[name].rearrange("(d o) -> d o", o=1)
            return v
        loads["small"] = [(d[16 * r:16 * r + 16, :], head_col(n)) for d, n in (
            (q_w, "L0_attn_q_ln_w"), (q_b, "L0_attn_q_ln_b"), (k_w, "L0_attn_k_ln_w"), (k_b, "L0_attn_k_ln_b"))
            for r in range(8)]
        loads["small"] += [(gate_w0, rows("L0_ffn_gate_w")), (router1, a["L1_ffn_router_w"]), (b2, a["L0_ffn_b2"])]
        loads["small"] += [(b1_rows[:], a["L0_ffn_b1"].rearrange("e (c p) -> (e c) p", p=P))]
        row = lambda name: a[name].rearrange("(o e) -> o e", o=1)
        col = lambda name: a[name].rearrange("(d o) -> d o", o=1)
        loads["attn1"] = [
            (down_u[:, :, 0:DC], rows("L1_attn_W_DQ")), (down_u[:, :, 64:64 + DC], rows("L1_attn_W_DQ")),
            (down_k[:, :, 0:DC], rows("L1_attn_W_DKV")), (down_k[:, :, DC:2 * DC], rows("L1_attn_W_KR")),
            (bias_u[0:DC, :], col("L1_attn_b_DQ")), (bias_u[64:64 + DC, :], col("L1_attn_b_DQ")),
            (bias_k[0:DC, :], col("L1_attn_b_DKV")), (bias_k[DC:2 * DC, :], col("L1_attn_b_KR")),
            (uk_raw[0:DC, :], a["L1_attn_W_UK"]), (uk_raw[64:65, :], row("L1_attn_b_UK")),
            (uq_raw[0:DC, :], a["L1_attn_W_UQ"]), (uq_raw[DC:DC + 1, :], row("L1_attn_b_UQ")),
            (uv_raw[0:DC, :], a["L1_attn_W_UV"]), (uv_raw[DC:DC + 1, :], row("L1_attn_b_UV")),
            (qr_raw[0:DC, :, DC:2 * DC], a["L1_attn_W_QR"].rearrange("c (h r) -> c h r", h=H1)),
            (qr_raw[DC:DC + 1, :, DC:2 * DC], row("L1_attn_b_QR").rearrange("o (h r) -> o h r", h=H1)),
            (wo1_raw, rows("L1_attn_W_O"))]
        w1v = w1.rearrange("p (e k f) -> p e k f", e=E0, k=KC)
        w2v = w2.rearrange("p (e c n) -> p e c n", e=E0, n=ED)
        W1 = a["L0_ffn_w1"].rearrange("e (k p) f -> p e k f", p=P)
        W2 = a["L0_ffn_w2"].rearrange("e (c p) n -> p e c n", p=P)
        loads["w1"] = [(w1v[:, e], W1[:, e]) for e in range(E0)]
        loads["w2"] = [(w2v[:, e], W2[:, e]) for e in range(E0)]
        guv = gate_up.rearrange("p (e k f) -> p e k f", e=E1, k=KC)
        dv = down.rearrange("p (e c n) -> p e c n", e=E1, n=ED)
        GU = a["L1_ffn_gate_up_proj"].rearrange("e (k p) f -> p e k f", p=P)
        DN = a["L1_ffn_down_proj"].rearrange("e (c p) n -> p e c n", p=P)
        loads["gate_up"] = [(guv[:, e], GU[:, e]) for e in range(E1)]
        loads["down"] = [(dv[:, 2 * e:2 * e + 2], DN[:, 2 * e:2 * e + 2]) for e in range(E1 // 2)]
        loads["shared"] = [(g_raw, rows("L1_ffn_shared_gate_w")), (up_raw, rows("L1_ffn_shared_up_w")),
                           (d_raw, rows("L1_ffn_shared_down_w"))]
        load_sem = {name: sem(f"ld_{name}") for name in loads}

        def arrived(engine, name, n=None):
            engine.wait_ge(load_sem[name], 16 * (len(loads[name]) if n is None else n))

        (prep_zeroed, consts_ready, averages_ready, prep_mm, prep_out, tiled_ready, folded, ln1_stats, ln1_sd,
         patch_ready, patch_mm, patchT_ready, z_mm, z_taken, ln2_stats, ln2_sd, pos_ready, embedded,
         ln_stats, ln_sd, xn_ready, xT_mm, xT_ready,
         qk_mm, sq_ready, var_mm, sd_ready, qk_norm, khead_ready, at0_zeroed,
         xv_ready, v_mm, v_ready, q_ready, k_ready, s_mm, s_taken, p_exp, p_sum, p_norm, t_mm, pT_ready, c_mm,
         c_taken, o_mm, o_taken, gathered,
         logits_mm, top_ready, gate_ready, onehot_ready, rank_mm, slots_ready, zero_stored, scattered, ohT_mm, ohT_ready,
         bias2_mm,
         lat_mm, lat_ready, keys_mm, keys_ready, at1_zeroed, u_ready, lk_ready, lv_mm, lv_ready,
         s1_mm, s1_taken, p1_exp, p1_sum, p1_norm, t1_mm, pT1_ready, c1_mm, c1_taken, o1_mm, bias_added,
         w_mm, w_ready, shg_mm, shu_mm, silu_ready, sT_ready, sho_mm, sho_taken, stored, xscaled) = [sem(n) for n in """
         prep_zeroed consts_ready averages_ready prep_mm prep_out tiled_ready folded ln1_stats ln1_sd
         patch_ready patch_mm patchT_ready z_mm z_taken ln2_stats ln2_sd pos_ready embedded
         ln_stats ln_sd xn_ready xT_mm xT_ready
         qk_mm sq_ready var_mm sd_ready qk_norm khead_ready at0_zeroed
         xv_ready v_mm v_ready q_ready k_ready s_mm s_taken p_exp p_sum p_norm t_mm pT_ready c_mm
         c_taken o_mm o_taken gathered
         logits_mm top_ready gate_ready onehot_ready rank_mm slots_ready zero_stored scattered ohT_mm ohT_ready
         bias2_mm
         lat_mm lat_ready keys_mm keys_ready at1_zeroed u_ready lk_ready lv_mm lv_ready
         s1_mm s1_taken p1_exp p1_sum p1_norm t1_mm pT1_ready c1_mm c1_taken o1_mm bias_added
         w_mm w_ready shg_mm shu_mm silu_ready sT_ready sho_mm sho_taken stored xscaled""".split()]
        rows_loaded = [[sem(f"rows_loaded{l}{s}") for s in range(2)] for l in range(2)]
        rows_mm = [sem(f"rows_mm{l}") for l in range(2)]
        rowsT_ready = [sem(f"rowsT_ready{l}") for l in range(2)]
        hid_mm = [sem(f"hid_mm{l}") for l in range(2)]
        hid_ready = [sem(f"hid_ready{l}") for l in range(2)]
        hidT_mm = [sem(f"hidT_mm{l}") for l in range(2)]
        hidT_ready = [sem(f"hidT_ready{l}") for l in range(2)]
        y_mm = [sem(f"y_mm{l}") for l in range(2)]
        y_ready = [sem(f"y_ready{l}") for l in range(2)]
        y_stored = [[sem(f"y_stored{l}{s}") for s in range(2)] for l in range(2)]
        experts_done = sem("experts_done")
        spread, reshuffled, tile_order = sem("spread"), sem("reshuffled"), sem("tile_order")

        def to_tiles(c):
            y = yT[:, c, :].rearrange("p (n b) -> p n b", b=B)
            o = ctxT[:, c, :].rearrange("p (n b) -> p n b", b=B)
            yield (o[:, 0:4 * G, :].rearrange("p (t j) b -> p t j b", j=4),
                   y[:, 1:1 + 4 * G, :].rearrange("p (j t) b -> p t j b", j=4))
            late_o = o[:, 4 * G:6 * G, :].rearrange("p (u w r) b -> p w u r b", w=2, r=2)
            late_y = y[:, 1 + 4 * G:1 + 6 * G, :].rearrange("p (r w u) b -> p w u r b", r=2, w=2)
            for w in range(2):
                yield late_o[:, w], late_y[:, w]
            yield o[:, S - 1, :], y[:, 0, :]
        silu1 = sem("silu1")

        QK = [(which, c, n) for which in range(2) for c in range(KC) for n in range(len(BLOCKS))]
        SH = [(n, f) for n in range(len(BLOCKS)) for f in range(SF // P)]
        SCALE0, SCALE1 = HD0 ** -0.5, (DK + DC) ** -0.5
        PREP = ["q", "k", "v", "woT", "router", "b1", "uk0", "uk1", "uq", "keyT", "uv", "valO", "bias_o",
                "mix", "woe"]
        NCUT = 9
        e_of = [E0, E1]
        nt_of = [NT0, NT1]

        block = ctx.enter_context(nc.Block())

        @block.sync
        def _(sp):
            def load(name, part=slice(None)):
                with nc.allow_non_contiguous_dma(reason="columns of a few vectors"):
                    for dst, src in loads[name][part]:
                        sp.dma_start(dst, src).then_inc(load_sem[name], 16)

            load("x_a")
            load("proj")
            load("x_b")
            sp.wait_ge(prep_zeroed, 1)
            load("pos")
            load("cls")
            load("attn0")
            load("attn1")
            load("small")
            for l in range(2):
                zx = sorted_x[l].rearrange("(n p) e -> p n e", p=P)
                for n in range(0, nt_of[l], 8):
                    m = min(8, nt_of[l] - n)
                    sp.dma_start(zx[:, n:n + m, :], zero[:, 0:m * ED].rearrange("p (n e) -> p n e", e=ED))\
                      .then_inc(zero_stored, 16)
            sp.wait_ge(zero_stored, 16 * 7)
            sp.wait_ge(embedded, 1)
            load("w1", slice(0, E0 - 1))
            sp.wait_ge(qk_norm, len(QK))
            load("w2", slice(0, E0 // 2))
            sp.wait_ge(c_taken, PAIRS)
            for hd in range(H0):
                r = HD0 * (hd % 8)
                sp.dma_start(shuffled.rearrange("d (q h) b -> h d q b", h=H0)[hd],
                             ctxT[r:r + HD0, hd // 8, :].rearrange("p (q b) -> p q b", b=B)).then_inc(spread, 16)
            sp.wait_ge(spread, 16 * H0)
            for hd in range(H0):
                r = HD0 * (hd % 8)
                sp.dma_start(yT[r:r + HD0, hd // 8, :], shuffled[:, S * hd:S * hd + S, :]
                             .rearrange("d q b -> d (q b)")).then_inc(reshuffled, 16)
            sp.wait_ge(o_mm, NT)
            load("w1", slice(E0 - 1, E0))
            load("w2", slice(E0 // 2, E0))

            def experts(l):
                xs = sorted_x[l].rearrange("(t p) e -> p t e", p=P)

                def front(i, s, k):
                    sp.wait_ge(rows_mm[l], i)
                    sp.dma_start(rows_in[:, s:s + 1, :], xs[:, bass.ds(i, 1), :]).then_inc(rows_loaded[l][s], 16)

                sp.wait_ge(scattered, 16 * NT * (l + 1))
                pipelined(sp, nt_of[l], (front, 0))

            experts(0)
            sp.wait_ge(y_mm[0], NT0 + 1)
            sp.wait_ge(gathered, 16 * NT)
            load("gate_up")
            load("down")
            sp.wait_ge(o1_mm, NT)
            load("shared", slice(0, 2))
            load("shared", slice(2, 3))
            sp.wait_ge(sho_mm, NT)
            experts(1)
            sp.wait_ge(experts_done, 1)
            n = 0
            for t, nt, j, tok in token_runs():
                sp.dma_start(out[:, tok:tok + nt, :], h[32 * j:32 * j + 32, t:t + nt, :]).then_inc(stored, 16)
                n += 1
            sp.dma_start(out[:, 0, :], h[0:32, NT - 1, :]).then_inc(stored, 16)
            sp.wait_ge(stored, 16 * (n + 1))

        @block.gpsimd
        def _(pool):
            ch = Chain(pool, sem("pool_chain"))

            def zeroed(*views):
                for v in views:
                    ch.did(pool.memset(v, 0.0))

            zeroed(keyT[:], down_u[:], down_k[:], bias_u[:], bias_k[:], uk_raw, uq_raw, uv_raw, qr_raw, zero,
                   h[:, NT - 1, :])
            ch.wait()
            for v, at in ((bias_u, DC), (bias_u, 64 + DC), (bias_k, 2 * DC)):
                ch.did(pool.affine_select(out=v[:], in_=v[:], pattern=[[0, 1]], compare_op=ALU.not_equal,
                                          fill=1.0, base=-at, channel_multiplier=1))
                ch.wait()
            pool.memset(ones_row[:], 1.0).then_inc(prep_zeroed, 1)

            def select(v, pattern, op, fill, base, mult):
                ch.did(pool.affine_select(out=v, in_=v, pattern=pattern, compare_op=op, fill=fill, base=base,
                                          channel_multiplier=mult))
                ch.wait()
            ch.did(pool.memset(ident[:], 0.0))
            ch.did(pool.memset(block16[:], 1.0))
            ch.did(pool.memset(ones16[:], 1.0))
            ch.did(pool.memset(before[:], 1.0))
            ch.did(pool.memset(lower_e[:], 1.0))
            ch.did(pool.memset(eps_col[:], EPS))
            ch.wait()
            select(ident[:], [[-1, P]], ALU.not_equal, 1.0, 0, 1)
            select(block16[:], [[-16, 8], [0, 16]], ALU.is_ge, 0.0, 0, 1)
            select(block16[:], [[16, 8], [0, 16]], ALU.is_ge, 0.0, 15, -1)
            select(before[:], [[1, P]], ALU.is_gt, 0.0, 0, -1)
            select(lower_e[:], [[1, E1], [-1, E1]], ALU.is_gt, 0.0, 0, 0)
            ch.did(pool.iota(iota_e[:], pattern=[[1, 34]], base=0, channel_multiplier=0,
                             allow_small_or_imprecise_dtypes=True))
            ch.did(pool.iota(thresholds[:], pattern=[[P, NT]], base=0, channel_multiplier=0,
                             allow_small_or_imprecise_dtypes=True))
            ch.wait()
            pool.sem_inc(consts_ready, 1)

            arrived(pool, "pos")
            arrived(pool, "proj")
            hp = h[:, 0:NCUT, :]
            pool.tensor_tensor(out=hp, in0=hp, in1=ln2_b.rearrange("p (o e) -> p o e", o=1)
                               .broadcast_to((P, NCUT, ED)), op=ALU.add).then_inc(pos_ready, 1)
            arrived(pool, "cls")
            pool.tensor_tensor(out=h[0:32, NT - 1, :], in0=h[0:32, NT - 1, :], in1=cls_pos, op=ALU.add)\
                .then_inc(pos_ready, 1)

            pool.wait_ge(embedded, 1)
            pool.wait_ge(prep_out, 1 + len(PREP))
            for v in (q_ring, xv, v_ring, p_ring):
                last = pool.memset(v, 0.0)
                ch.did(last)
            ch.wait()
            pool.sem_inc(at0_zeroed, 1)

            pool.wait_ge(qk_norm, len(QK))
            pool.wait_ge(khead_ready, 2)
            ln_tok = xT.rearrange("p k (n b) -> p k b n", b=B)

            def front(i, s, k):
                pool.wait_ge(v_mm, i)
                for k in range(KC):
                    ins = pool.tensor_copy(xv[:, s, k, :].rearrange("p (j n) -> p j n", j=2)[:, :, 0:S],
                                           ln_tok[:, k, bass.ds(i * 2, 2), 0:S])
                    ins.then_inc(xv_ready, 1)
                pool.wait_ge(s_mm, i)
                for c in range(KC):
                    pool.tensor_tensor(
                        out=k_ring[s][:, c],
                        in0=kn[:, c, bass.ds(i * 2, 2), :].rearrange("p j (o n) -> p j o n", o=1)
                        .broadcast_to((P, 2, 4, S)),
                        in1=k_of[:].rearrange("p (o h q) -> p o h q", o=1, q=1).broadcast_to((P, 2, 4, S)),
                        op=ALU.mult).then_inc(k_ready, 1)

            def back(i, s, k):
                pool.wait_ge(p_sum, i + 1)
                pv = p_ring[:, s, :, 0:S]
                pool.tensor_tensor(out=pv, in0=pv, in1=sm[:, s, :].rearrange("p (g o) -> p g o", o=1)
                                   .broadcast_to((P, 16, S)), op=ALU.mult).then_inc(p_norm, 1)

            pipelined(pool, PAIRS, (front, 0), (back, 1))

            def scatter(l):
                pool.wait_ge(slots_ready, l + 1)
                pool.wait_ge(zero_stored, 16 * 7)
                for t in range(NT):
                    n = P if t < NT - 1 else B
                    pool.indirect_dma_start(
                        out=sorted_x[l], out_offset=bass.IndirectOffsetOnAxis(
                            ap=slot[0:n, l, t:t + 1].bitcast(U32), axis=0),
                        in_=xn[0:n, t, :], in_offset=None).then_inc(scattered, 16)

            def store_rows(l):
                ys = sorted_y[l].rearrange("(t p) e -> p t e", p=P)

                def store(i, s, k):
                    pool.wait_ge(y_ready[l], i + 1)
                    pool.dma_start(ys[:, bass.ds(i, 1), :], rows_out[:, s:s + 1, :]).then_inc(y_stored[l][s], 16)

                pipelined(pool, nt_of[l], (store, 0))

            def gather(l):
                for s in range(2):
                    pool.wait_ge(y_stored[l][s], 16 * ((nt_of[l] + 1 - s) // 2))
                pool.wait_ge(scattered, 16 * NT * (l + 1))
                for t in range(NT):
                    n = P if t < NT - 1 else B
                    pool.indirect_dma_start(
                        out=xn[0:n, t, :], out_offset=None, in_=sorted_y[l],
                        in_offset=bass.IndirectOffsetOnAxis(ap=slot[0:n, l, t:t + 1].bitcast(U32), axis=0))\
                        .then_inc(gathered, 16)

            scatter(0)
            store_rows(0)
            gather(0)

            pool.wait_ge(y_mm[0], NT0 + 1)
            pool.wait_ge(bias2_mm, NT)
            for v in (lat_u, lat_v, u_ring, lk_ring, p1_ring, ctx1T):
                ch.did(pool.memset(v, 0.0))
            ch.wait()
            pool.sem_inc(at1_zeroed, 1)
            pool.wait_ge(lat_ready, 6)

            pool.sem_inc(p1_norm, 1)

            def front1(i, s, k):
                pool.wait_ge(s1_mm, i)
                for half in range(2):
                    r = slice(64 * half, 64 * half + 64)
                    if half == 0:
                        pool.wait_ge(lk_ready, i)
                        pool.wait_ge(p1_norm, i)
                    pool.tensor_copy(u_ring[r, s, :, QP * half:QP * half + QP],
                                     lat_u[r, bass.ds(i * 2, 2), :]).then_inc(u_ready, 1)
                pool.wait_ge(lv_mm, i)
                pool.wait_ge(u_ready, i * 2 + 2)
                pool.tensor_copy(lk_ring[:, s, :].rearrange("p (j n) -> p j n", j=2)[:, :, 0:S],
                                 lat_k.rearrange("p (b n) -> p b n", n=S)[:, bass.ds(i * 2, 2), :])\
                    .then_inc(lk_ready, 1)

            def back1(i, s, k):
                pool.wait_ge(p1_sum, i + 1)
                pool.wait_ge(lk_ready, i + 1)
                pv = p1_ring[:, s, :, 0:S]
                pool.tensor_tensor(out=pv, in0=pv, in1=sm1[:, s, :].rearrange("p (g o) -> p g o", o=1)
                                   .broadcast_to((P, 8, S)), op=ALU.mult).then_inc(p1_norm, 1)

            pipelined(pool, PAIRS, (front1, 0), (back1, 1))
            scatter(1)
            store_rows(1)
            gather(1)

        @block.scalar
        def _(act):
            def evacuated(sems, dst, src, **kw):
                ins = act.activation(dst, src, ACT.Copy)
                ins.then_inc(sems, 1)

            act.wait_ge(prep_mm, 1)
            evacuated(prep_out, bias_z, bank(6)[:, 0:ED])

            def ln1_deviation(n, t0, t1):
                act.wait_ge(ln1_stats, n + 1)
                act.activation(sd[:, t0:t1], meanvar[:, t0:t1, 1], ACT.Sqrt, bias=eps_col[:, 0:1])\
                   .then_inc(ln1_sd, 1)

            ln1_deviation(0, 0, G)
            for t in range(NCUT):
                act.wait_ge(patch_mm, t + 1)
                if t >= 2:
                    act.wait_ge(z_mm, t - 1)
                act.activation(patchT[:, t % 2].rearrange("p c n -> p (c n)"),
                               bank(2 * (t % 2), 2)[:, 0:PD], ACT.Copy).then_inc(patchT_ready, 1)
                if t == G - 1:
                    ln1_deviation(1, G, NCUT)
            act.wait_ge(ln2_stats, 1)
            act.activation(sd[:, 0:NCUT], meanvar[:, 0:NCUT, 1], ACT.Sqrt, bias=eps_col[:, 0:1]).then_inc(ln2_sd, 1)

            def layernorm(n):
                act.wait_ge(ln_stats, n + 1)
                act.activation(sd[:, :], meanvar[:, :, 1], ACT.Sqrt, bias=eps_col[:, 0:1]).then_inc(ln_sd, 1)
                for t in range(NT):
                    act.wait_ge(xT_mm, NT * n + t + 1)
                    act.activation(xT[:, :, P * t:P * t + P],
                                   bank(t % 4)[:, 0:KC * P].rearrange("p (k n) -> p k n", k=KC),
                                   ACT.Copy).then_inc(xT_ready, 1)

            pb = lambda n: bank(7 - n % 2)
            for n, what in enumerate(PREP):
                if what == "mix":
                    continue
                act.wait_ge(prep_mm, n + 2)
                src = pb(n)
                two = lambda v: v.rearrange("p k e -> p (k e)")
                if what in ("q", "k", "v", "woT", "woe"):
                    dst = {"q": qT, "k": kT, "v": vT, "woT": woT, "woe": woe}[what]
                    evacuated(prep_out, two(dst), src)
                elif what == "router":
                    evacuated(prep_out, two(routerT1[:]), src[:, 0:KC * E1])
                elif what == "b1":
                    evacuated(prep_out, two(b1T[:]), src[:, 0:E0 * FF0 // P])
                elif what in ("uk0", "uk1"):
                    m = 4 * (what == "uk1")
                    evacuated(prep_out, two(ukT[:, m:m + 4, :]), src)
                elif what in ("uq", "uv"):
                    evacuated(prep_out, two(uqT if what == "uq" else uvT), src[:, 0:H1 * (DC + 1)])
                elif what == "keyT":
                    evacuated(prep_out, keyT[:].rearrange("p a (r n) -> p (a r) n", r=2)[:, :, 0:DC + 1],
                              src[:, 0:H1 * (DC + 1)].rearrange("p (g n) -> p g n", g=H1))
                elif what == "valO":
                    evacuated(prep_out, two(valO[:]), src)
                elif what == "bias_o":
                    evacuated(prep_out, bias_o[:], src[:, 0:ED])

            layernorm(0)
            def sd_of(v):
                n = BLOCKS[QK[v][2]][1]
                act.wait_ge(var_mm, v + 1)
                act.activation(sq[:, v % 2, 0:n], bank(2 + v % 2)[:, 0:n], ACT.Sqrt, bias=eps_col[:, 0:1])\
                   .then_inc(sd_ready, 1)

            for v, (_, _, blk) in enumerate(QK):
                n = BLOCKS[blk][1]
                act.wait_ge(qk_mm, v + 1)
                if v >= 2:
                    act.wait_ge(qk_norm, v - 1)
                act.activation(raw[:, v % 2, 0:n], bank(v % 2)[:, 0:n], ACT.Copy).then_inc(sq_ready, 1)
                act.activation(sq[:, v % 2, 0:n], bank(v % 2)[:, 0:n], ACT.Square).then_inc(sq_ready, 1)
                if v:
                    sd_of(v - 1)
            sd_of(len(QK) - 1)

            act.wait_ge(qk_norm, len(QK))
            act.activation(kn, kn, ACT.Identity, scale=k_w[:, 0:1], bias=k_b[:, 0:1]).then_inc(khead_ready, 1)
            act.wait_ge(at0_zeroed, 1)

            def front(i, s, k):
                act.wait_ge(s_mm, i)
                for half in range(2):
                    r = slice(64 * half, 64 * half + 64)
                    act.activation(q_ring[r, s, :, :, QP * half:QP * half + S],
                                   qn[r, :, bass.ds(i * 2, 2), :], ACT.Identity,
                                   scale=q_w[r, 0:1], bias=q_b[r, 0:1]).then_inc(q_ready, 1)
                act.wait_ge(v_mm, i + 2)
                act.wait_ge(c_mm, i)
                for half in range(2):
                    for j in range(2):
                        cols = lambda v: v.rearrange("p (g two d) -> p g two d", two=2, d=HD0)[:, :, half, :]
                        act.activation(cols(v_ring[64 * half:64 * half + 64, s, j, :]),
                                       cols(bank(6)[64 * j:64 * j + 64, 0:ED]), ACT.Copy).then_inc(v_ready, 1)

            def exps(i, s, k):
                act.wait_ge(s_taken, i + 2)
                pv = p_ring[:, s, :, 0:S]
                act.activation(pv, pv, ACT.Exp, scale=SCALE0).then_inc(p_exp, 1)

            def back(i, s, k):
                act.wait_ge(t_mm, i + 2)
                act.wait_ge(c_mm, i)
                act.activation(pT[s], bank(4, 2).rearrange("p (g n) -> p g n", n=QP)[:, :, 0:S], ACT.Copy)\
                   .then_inc(pT_ready, 1)

            pipelined(act, PAIRS, (back, 2), (front, 0), (exps, 0))
            act.wait_ge(reshuffled, 16 * H0)
            for dst, src in to_tiles(0):
                act.activation(dst, src, ACT.Copy).then_inc(tile_order, 1)
            layernorm(1)
            act.wait_ge(top_ready, 1)
            act.activation(logits[:, :, 0:E0], logits[:, :, 0:E0], ACT.Exp).then_inc(gate_ready, 1)
            for n in range(3):
                act.wait_ge(ohT_mm, n + 1)
                m = min(4, NT - 4 * n)
                act.activation(onehotT[0:E0, 4 * n:4 * n + m, :].rearrange("p t n -> p (t n)"),
                               bank(5 + n)[0:E0, 0:P * m], ACT.Copy).then_inc(ohT_ready, 1)

            act.wait_ge(slots_ready, 1)

            def xfront(i, s, k):
                act.wait_ge(rows_mm[0], i + 2)
                act.activation(rowsT[:, s], bank(0)[:, 0:KC * P].rearrange("p (k n) -> p k n", k=KC), ACT.Copy)\
                   .then_inc(rowsT_ready[0], 1)

            def xback(i, s, k):
                e = act.value_load(tile_e[0:1, 0, bass.ds(i, 1)], min_val=0, max_val=E0 - 1)
                act.wait_ge(hidT_mm[0], i + 2)
                act.wait_ge(y_mm[0], i)
                b1f = b1T[:, :, :].rearrange("p e c -> p (e c)")
                for c in range(FF0 // P):
                    act.activation(hidT[:, s, c, :], bank(4, 2)[:, P * c:P * c + P], ACT.Gelu,
                                   bias=b1f[:, bass.ds(e * (FF0 // P) + c, 1)]).then_inc(hidT_ready[0], 1)

            pipelined(act, NT0, (xfront, 0), (xback, 2))
            layernorm(2)

            act.wait_ge(at1_zeroed, 1)
            v = 0
            for which in range(2):
                for c0, n in BLOCKS:
                    act.wait_ge(lat_mm, v + 1)
                    if which == 0:
                        dst = lat_u.rearrange("p b n -> p n b")[:, c0 // B:(c0 + n) // B, :]
                    else:
                        dst = lat_k.rearrange("p (b n) -> p n b", n=S)[:, c0 // B:(c0 + n) // B, :]
                    act.activation(dst, bank(v % 2)[:, 0:n].rearrange("p (n b) -> p n b", b=B), ACT.Identity,
                                   bias=(bias_k if which else bias_u)[:, 0:1]).then_inc(lat_ready, 1)
                    v += 1
            for v in range(12):
                c0, n = BLOCKS[v % 3]
                act.wait_ge(keys_mm, v + 1)
                act.activation(keys[:, v // 3, c0:c0 + n], bank(2 + v % 2)[:, 0:n], ACT.Copy).then_inc(keys_ready, 1)

            def front1(i, s, k):
                act.wait_ge(lv_mm, i + 2)
                act.wait_ge(c1_mm, i)
                for half in range(2):
                    for j in range(2):
                        act.activation(lat_v[64 * half:64 * half + 64, s, j, DC * half:DC * half + DC],
                                       bank(6)[64 * j:64 * j + 64, 0:DC], ACT.Copy).then_inc(lv_ready, 1)

            def exps1(i, s, k):
                act.wait_ge(s1_taken, i + 2)
                pv = p1_ring[:, s, :, 0:S]
                act.activation(pv, pv, ACT.Exp, scale=SCALE1).then_inc(p1_exp, 1)

            def back1(i, s, k):
                act.wait_ge(t1_mm, i + 2)
                act.wait_ge(c1_mm, i)
                act.activation(pT1[s], bank(4).rearrange("p (g r n) -> p g r n", g=4, n=QP)[:, :, :, 0:S], ACT.Copy)\
                   .then_inc(pT1_ready, 1)

            pipelined(act, PAIRS, (back1, 2), (front1, 0), (exps1, 0))
            layernorm(3)
            act.wait_ge(top_ready, 2)
            act.activation(weight[:], top[:], ACT.Sigmoid).then_inc(gate_ready, 1)

            for v in range(12):
                act.wait_ge(w_mm, v + 1)
                if v < 8:
                    dst = (gT if v < 4 else upT)[:, v % 4 // 2, 512 * (v % 2):512 * (v % 2) + 512]
                else:
                    dst = dT[:, 2 * (v - 8):2 * (v - 8) + 2, :].rearrange("p c e -> p (c e)")
                act.activation(dst, bank(v % 2), ACT.Copy).then_inc(w_ready, 1)
            for v, (blk, f) in enumerate(SH):
                n = BLOCKS[blk][1]
                act.wait_ge(shg_mm, v + 1)
                if v >= 2:
                    act.wait_ge(sT_ready, v - 1)
                act.activation(sg[:, v % 2, 0:n], bank(v % 2)[:, 0:n], ACT.Silu).then_inc(silu_ready, 1)

            act.wait_ge(slots_ready, 2)

            def xfront1(i, s, k):
                act.wait_ge(rows_mm[1], i + 2)
                act.activation(rowsT[:, s], bank(0)[:, 0:KC * P].rearrange("p (k n) -> p k n", k=KC), ACT.Copy)\
                   .then_inc(rowsT_ready[1], 1)

            def xsilu1(i, s, k):
                act.wait_ge(hid_mm[1], i + 1)
                act.wait_ge(hid_ready[1], i)
                act.activation(hid[:, s, 0:FF1], bank(2 + s)[:, 0:FF1], ACT.Silu).then_inc(silu1, 1)

            def xback1(i, s, k):
                act.wait_ge(hidT_mm[1], i + 2)
                act.wait_ge(y_mm[1], i)
                act.activation(hidT[:, s, 0:2, :].rearrange("p c n -> p (c n)"), bank(4)[:, 0:2 * P], ACT.Copy)\
                   .then_inc(hidT_ready[1], 1)

            pipelined(act, NT1, (xfront1, 0), (xback1, 2), (xsilu1, 1))

        @block.vector
        def _(dve):
            ch = Chain(dve, sem("dve_chain"))

            def wide(v, n):
                return v.rearrange("p (g o) -> p g o", o=1).broadcast_to((v.shape[0], v.shape[1], n))

            def over(v, n):
                return v.rearrange("p (o g) -> p o g", o=1).broadcast_to((v.shape[0], n, v.shape[1]))

            for credit in (hid_ready[1], s_taken, s1_taken):
                dve.sem_inc(credit, 1)
            dve.wait_ge(consts_ready, 1)
            blk = block16[:, :, :].rearrange("p j i -> p (j i)")
            ch.did(dve.tensor_scalar(average[:], blk, 1.0 / HD0, None, ALU.mult))
            ch.wait()
            dve.tensor_tensor(out=centre[:], in0=ident[:], in1=average[:], op=ALU.subtract).then_inc(averages_ready, 1)

            def patch_of(t):
                return x_a[:, :, :, PS * t:PS * t + PS] if t < G else x_b[:, :, :, PS * (t - G):PS * (t - G) + PS]

            def ln1(t0, t1):
                for t in range(t0, t1):
                    for c in range(C):
                        ch.did(dve.bn_stats(stats[:, t, c, :], patch_of(t)[:, c]))
                ch.wait()
                for t in range(t0, t1):
                    last = dve.bn_aggr(meanvar[:, t, :], stats[:, t, :, :].rearrange("p c s -> p (c s)"))
                last.then_inc(ln1_stats, 1)

            arrived(dve, "x_a")
            ln1(0, G)
            arrived(dve, "proj")
            for c in range(PC):
                last = dve.tensor_scalar(wg_proj[:, c, :], w_proj[:, c, :], ln1_g[:, c:c + 1], None, ALU.mult)
            last.then_inc(folded, 1)
            dve.wait_ge(ln1_sd, 1)
            ch.did(dve.reciprocal(rstd[:, 0:G], sd[:, 0:G]))
            ch.wait()

            def norm1(t):
                if t >= 2:
                    dve.wait_ge(patch_mm, t - 1)
                dve.tensor_scalar(patch[:, t % 2].rearrange("p (c i w) -> p c i w", c=C, i=PS), patch_of(t),
                                  meanvar[:, t, 0:1], rstd[:, t:t + 1], ALU.subtract, ALU.mult).then_inc(patch_ready, 1)

            def take_z(t):
                dve.wait_ge(z_mm, t + 1)
                if t == 0:
                    dve.wait_ge(prep_out, 1)
                dve.tensor_tensor(out=xn[:, t, :], in0=bank(4 + t % 2)[:, 0:ED], in1=bias_z, op=ALU.add)\
                   .then_inc(z_taken, 1)

            norm1(0)
            for t in range(1, NCUT):
                if t == G:
                    arrived(dve, "x_b")
                    ln1(G, NCUT)
                    dve.wait_ge(ln1_sd, 2)
                    ch.did(dve.reciprocal(rstd[:, G:NCUT], sd[:, G:NCUT]))
                    ch.wait()
                norm1(t)
                take_z(t - 1)
            take_z(NCUT - 1)
            dve.wait_ge(z_taken, NCUT)
            for t in range(NCUT):
                ch.did(dve.bn_stats(stats[:, t, 0, :], xn[:, t, :]))
            ch.wait()
            for t in range(NCUT):
                last = dve.bn_aggr(meanvar[:, t, :], stats[:, t, 0, :])
            last.then_inc(ln2_stats, 1)

            arrived(dve, "attn0")
            ch.did(dve.tensor_reduce(sv_w[0:H0, :], sparse_v[0:H0], axis=AX.X, op=ALU.add))
            ch.did(dve.tensor_reduce(so_w[0:H0, :], sparse_o[0:H0].rearrange("p k d -> p d k"), axis=AX.X, op=ALU.add))
            ch.wait()
            for dst, src in ((tiled_v, sv_w), (tiled_o, so_w)):
                last = dve.tensor_copy(dst[0:H0, :].rearrange("p (r d) -> p r d", d=HD0), over(src[0:H0, :], 8))
            last.then_inc(tiled_ready, 1)

            dve.wait_ge(ln2_sd, 1)
            ch.did(dve.reciprocal(rstd[:, 0:NCUT], sd[:, 0:NCUT]))
            ch.wait()
            for t in range(NCUT):
                ch.did(dve.tensor_scalar(xn[:, t, :], xn[:, t, :], meanvar[:, t, 0:1], rstd[:, t:t + 1],
                                         ALU.subtract, ALU.mult))
            ch.wait()
            dve.wait_ge(pos_ready, 2)
            for t in range(NCUT):
                ch.did(dve.tensor_tensor(out=xn[:, t, :], in0=xn[:, t, :], in1=ln2_g, op=ALU.mult))
            ch.wait()
            for t in range(NCUT):
                last = dve.tensor_tensor(out=h[:, t, :], in0=h[:, t, :], in1=xn[:, t, :], op=ALU.add)
                ch.did(last)
            ch.wait()
            dve.sem_inc(embedded, 1)

            arrived(dve, "small")
            dve.tensor_tensor(out=k_of[:], in0=block16[:, 0:4, 0], in1=block16[:, 4:8, 0], op=ALU.add)\
               .then_inc(khead_ready, 1)

            def layernorm(n):
                for t in range(NT):
                    ch.did(dve.bn_stats(stats[:, t, 0, :], h[:, t, :]))
                ch.wait()
                for t in range(NT):
                    last = dve.bn_aggr(meanvar[:, t, :], stats[:, t, 0, :])
                last.then_inc(ln_stats, 1)
                dve.wait_ge(ln_sd, n + 1)
                ch.did(dve.reciprocal(rstd[:], sd[:]))
                ch.wait()
                for t in range(NT):
                    dve.tensor_scalar(xn[:, t, :], h[:, t, :], meanvar[:, t, 0:1], rstd[:, t:t + 1],
                                      ALU.subtract, ALU.mult).then_inc(xn_ready, 1)

            dve.wait_ge(prep_mm, 1 + PREP.index("mix") + 1)
            dve.scalar_tensor_tensor(out=blockM, in0=bank(7 - PREP.index("mix") % 2)[:, 0:P], scalar=1.0 / (P * P),
                                     in1=blk, op0=ALU.mult, op1=ALU.mult).then_inc(prep_out, 1)

            layernorm(0)
            for v, (which, c, bl) in enumerate(QK):
                c0, n = BLOCKS[bl]
                dve.wait_ge(sd_ready, v + 1)
                ch.did(dve.reciprocal(sq[:, v % 2, 0:n], sq[:, v % 2, 0:n]))
                ch.wait()
                dst = (kn if which else qn)[:, c].rearrange("p b n -> p n b")[:, c0 // B:(c0 + n) // B, :]
                if v == 0:
                    dve.wait_ge(embedded, 1)
                r3 = raw[:, v % 2, 0:n].rearrange("p (n b) -> p n b", b=B)
                s3 = sq[:, v % 2, 0:n].rearrange("p (n b) -> p n b", b=B)
                if which:
                    dve.tensor_tensor(out=dst, in0=r3, in1=s3, op=ALU.mult).then_inc(qk_norm, 1)
                    continue
                seq = qn[:, c].rearrange("p b n -> p n b")
                parts = []
                n0 = c0 // B
                for t in range(n0 // 4, (n0 + n // B) // 4):
                    q0 = 4 * t - n0
                    if t < G:
                        parts.append((seq[:, 1 + t:1 + t + 3 * G + 1:G, :], q0, 4))
                    else:
                        for j1 in range(2):
                            at = 1 + 4 * G + G // 2 * j1 + t - G
                            parts.append((seq[:, at:at + G + 1:G, :], q0 + 2 * j1, 2))
                if n0 + n // B == S:
                    parts.append((seq[:, 0:1, :], S - 1 - n0, 1))
                for q, (d, q0, m) in enumerate(parts):
                    ins = dve.tensor_tensor(out=d, in0=r3[:, q0:q0 + m, :], in1=s3[:, q0:q0 + m, :], op=ALU.mult)
                ins.then_inc(qk_norm, 1)

            chf = Chain(dve, sem("dve_chain_max0"), 1)
            chs = Chain(dve, sem("dve_chain_sum0"), 1)
            dve.wait_ge(at0_zeroed, 1)

            def fmax(i, s, k):
                chf.at(i)
                dve.wait_ge(s_mm, i + 2)
                sc = bank(2 * s, 2).rearrange("p (j n) -> p j n", j=2)[:, :, 0:8 * S]\
                    .rearrange("p j (g n) -> p j g n", n=S)
                chf.did(dve.tensor_reduce(mx[:, s, :], sc, axis=AX.X, op=ALU.max))
                chf.wait()
                dve.wait_ge(t_mm, i)
                dve.tensor_tensor(out=p_ring[:, s, :, 0:S].rearrange("p (j g) n -> p j g n", j=2), in0=sc,
                                  in1=mx[:, s, :].rearrange("p (j g o) -> p j g o", j=2, o=1)
                                  .broadcast_to((P, 2, 8, S)), op=ALU.subtract).then_inc(s_taken, 1)

            def fctx(i, s, k):
                dve.wait_ge(c_mm, i + 2)
                dve.tensor_copy(ctxT.rearrange("p c (n b) -> p c b n", b=B)[:, :, bass.ds(i * 2, 2), :],
                                bank(7)[:, 0:4 * S].rearrange("p (c j n) -> p c j n", c=2, j=2)).then_inc(c_taken, 1)

            def fsum(i, s, k):
                chs.at(i)
                dve.wait_ge(p_exp, i + 1)
                chs.did(dve.tensor_reduce(sm[:, s, :], p_ring[:, s, :, 0:S], axis=AX.X, op=ALU.add))
                chs.wait()
                dve.reciprocal(sm[:, s, :], sm[:, s, :]).then_inc(p_sum, 1)

            pipelined(dve, PAIRS, (fmax, 0), (fctx, 2), (fsum, 0))

            def add_heads(base, n_done):
                for t in range(NT):
                    dve.wait_ge(base, t + 1)
                    m = P if t < NT - 1 else B
                    ins = dve.tensor_tensor(out=h[0:m, t, :], in0=h[0:m, t, :], in1=bank(t % 4)[0:m, 0:ED],
                                            op=ALU.add)
                    ins.then_inc(o_taken, 1)
                dve.wait_ge(o_taken, n_done)

            dve.wait_ge(reshuffled, 16 * H0)
            for dst, src in to_tiles(1):
                dve.tensor_copy(dst, src).then_inc(tile_order, 1)
            add_heads(o_mm, NT)
            layernorm(1)

            def route(l):
                E, nt = e_of[l], nt_of[l]
                lg, mk, oh = logits[:, :, 0:E], mask[:, :, 0:E], onehot[:, :, 0:E]
                dve.wait_ge(logits_mm, l + 1)
                ch.did(dve.tensor_copy(lg, bank(4)[:, 0:NT * E].rearrange("p (t e) -> p t e", e=E)))
                ch.wait()
                ch.did(dve.tensor_reduce(top[:], lg, axis=AX.X, op=ALU.max))
                ch.wait()
                if l:
                    dve.sem_inc(top_ready, 1)
                ch.did(dve.tensor_tensor(out=mk, in0=lg, in1=wide(top[:], E), op=ALU.is_equal))
                ch.wait()
                if l == 0:
                    dve.tensor_tensor(out=lg, in0=lg, in1=wide(top[:], E), op=ALU.subtract).then_inc(top_ready, 1)
                ch.did(dve.scalar_tensor_tensor(out=mk, in0=mk, scalar=-64.0, in1=over(iota_e[:, 0:E], NT),
                                                op0=ALU.mult, op1=ALU.add))
                ch.wait()
                ch.did(dve.tensor_reduce(first[:], mk, axis=AX.X, op=ALU.min))
                ch.wait()
                ch.did(dve.tensor_tensor(out=oh, in0=mk, in1=wide(first[:], E), op=ALU.is_equal))
                ch.wait()
                ch.did(dve.memset(onehot[32:64, NT - 1, 0:E], 0.0))
                ch.did(dve.memset(onehot[64:128, NT - 1, 0:E], 0.0))
                ch.wait()
                if l == 0:
                    ch.did(dve.tensor_copy(onehot_f[:], oh))
                    ch.wait()
                dve.sem_inc(onehot_ready, 1)
                dve.wait_ge(gate_ready, l + 1)
                if l == 0:
                    ch.did(dve.tensor_reduce(weight[:], lg, axis=AX.X, op=ALU.add))
                    ch.wait()
                    ch.did(dve.reciprocal(weight[:], weight[:]))
                else:
                    for t in range(NT):
                        ch.did(dve.tensor_scalar(xn[:, t, :], xn[:, t, :], weight[:, t:t + 1], None, ALU.mult))
                ch.wait()
                dve.wait_ge(rank_mm, l + 1)
                rank = bank(5)[:, 0:NT * E].rearrange("p (t e) -> p t e", e=E)
                over_e, tl, bs, en = counts_over[:, 0:E, :], tiles_e[:, 0:E], base_e[:, 0:E], end_e[:, 0:E]
                ch.did(dve.tensor_tensor(out=over_e, in0=wide(bank(6)[:, 0:E], NT), in1=over(thresholds[:], E),
                                         op=ALU.is_gt))
                ch.wait()
                ch.did(dve.tensor_reduce(tl, over_e, axis=AX.X, op=ALU.add))
                ch.wait()
                ch.did(dve.tensor_tensor(out=base_tmp[:, 0:E, 0:E], in0=lower_e[:, 0:E, 0:E], in1=over(tl, E),
                                         op=ALU.mult))
                ch.wait()
                ch.did(dve.tensor_reduce(bs, base_tmp[:, 0:E, 0:E], axis=AX.X, op=ALU.add))
                ch.wait()
                ch.did(dve.tensor_tensor(out=en, in0=bs, in1=tl, op=ALU.add))
                ch.did(dve.scalar_tensor_tensor(out=mk, in0=over(bs, NT), scalar=float(P), in1=rank,
                                                op0=ALU.mult, op1=ALU.add))
                ch.wait()
                ch.did(dve.tensor_tensor(out=mk, in0=mk, in1=oh, op=ALU.mult))
                ch.did(dve.tensor_tensor(out=tile_cmp[0:1, 0:nt, 0:E - 1], in0=wide(iota_e[0:1, 0:nt], E - 1),
                                         in1=over(end_e[0:1, 0:E - 1], nt), op=ALU.is_ge))
                ch.wait()
                ch.did(dve.tensor_reduce(slot_f[:], mk, axis=AX.X, op=ALU.add))
                ch.did(dve.tensor_reduce(tile_e_f[0:1, 0:nt], tile_cmp[0:1, 0:nt, 0:E - 1], axis=AX.X, op=ALU.add))
                ch.wait()
                ch.did(dve.tensor_copy(slot[:, l, :], slot_f[:]))
                ch.did(dve.tensor_copy(tile_e[0:1, l, 0:nt], tile_e_f[0:1, 0:nt]))
                ch.wait()
                dve.sem_inc(slots_ready, 1)

            route(0)

            def take_hid0(i, s, k):
                dve.wait_ge(hidT_mm[0], i)
                for half in range(2):
                    dve.wait_ge(hid_mm[0], i * 2 + half + 1)
                    dve.tensor_copy(hid[:, s, 512 * half:512 * half + 512], bank(2 + half)).then_inc(hid_ready[0], 1)

            def take_y(l):
                def body(i, s, k):
                    dve.wait_ge(y_mm[l], i + 2)
                    dve.wait_ge(y_stored[l][s], k * 16)
                    dve.tensor_copy(rows_out[:, s, :], bank(6)[:, 0:ED]).then_inc(y_ready[l], 1)
                return body

            pipelined(dve, NT0, (take_hid0, 1), (take_y(0), 2))
            dve.wait_ge(gathered, 16 * NT)
            for t in range(NT):
                dve.wait_ge(bias2_mm, t + 1)
                ch.did(dve.tensor_tensor(out=xn[:, t, :], in0=xn[:, t, :], in1=bank(t % 4)[:, 0:ED], op=ALU.add))
                ch.wait()
                dve.scalar_tensor_tensor(out=h[:, t, :], in0=xn[:, t, :], scalar=weight[:, t:t + 1],
                                         in1=h[:, t, :], op0=ALU.mult, op1=ALU.add).then_inc(o_taken, 1)
            dve.wait_ge(o_taken, 2 * NT)
            layernorm(2)

            dve.wait_ge(xn_ready, 3 * NT)
            ch.did(dve.tensor_tensor(out=h[:], in0=h[:], in1=over(bias_o[:], NT), op=ALU.add))
            ch.wait()
            chf1 = Chain(dve, sem("dve_chain_max1"), 1)
            chs1 = Chain(dve, sem("dve_chain_sum1"), 1)
            dve.wait_ge(at1_zeroed, 1)

            def fmax1(i, s, k):
                chf1.at(i)
                dve.wait_ge(s1_mm, i + 2)
                sc = bank(s)[:, 0:8 * S].rearrange("p (g n) -> p g n", n=S)
                chf1.did(dve.tensor_reduce(mx1[:, s, :], sc, axis=AX.X, op=ALU.max))
                chf1.wait()
                dve.wait_ge(t1_mm, i)
                dve.tensor_tensor(out=p1_ring[:, s, :, 0:S], in0=sc, in1=wide(mx1[:, s, :], S),
                                  op=ALU.subtract).then_inc(s1_taken, 1)

            def fctx1(i, s, k):
                dve.wait_ge(c1_mm, i + 2)
                for j in range(2):
                    ins = dve.tensor_copy(
                        ctx1T.rearrange("p r (n b) -> p r b n", b=B)[:, :, bass.ds(i * 2 + j, 1), 0:S]
                        .rearrange("p r o n -> p r (o n)"),
                        bank(7)[:, 2 * S * j:2 * S * j + 2 * S].rearrange("p (r n) -> p r n", r=2))
                    ins.then_inc(c1_taken, 1)

            def fsum1(i, s, k):
                chs1.at(i)
                dve.wait_ge(p1_exp, i + 1)
                chs1.did(dve.tensor_reduce(sm1[:, s, :], p1_ring[:, s, :, 0:S], axis=AX.X, op=ALU.add))
                chs1.wait()
                dve.reciprocal(sm1[:, s, :], sm1[:, s, :]).then_inc(p1_sum, 1)

            pipelined(dve, PAIRS, (fmax1, 0), (fctx1, 2), (fsum1, 0))
            add_heads(o1_mm, 3 * NT)
            layernorm(3)
            dve.wait_ge(xT_mm, 4 * NT)
            route(1)

            t_done = 0
            v = 0
            for bl, (c0, n) in enumerate(BLOCKS):
                for f in range(SF // P):
                    dve.wait_ge(silu_ready, v + 1)
                    dve.wait_ge(shu_mm, v + 1)
                    if bl and f == 0:
                        dve.wait_ge(sho_mm, t_done)
                    dve.tensor_tensor(out=sT[:, f, 0:n], in0=bank(2 + v % 2)[:, 0:n], in1=sg[:, v % 2, 0:n],
                                      op=ALU.mult).then_inc(sT_ready, 1)
                    v += 1
                for t in range(c0 // P, (c0 + n + P - 1) // P):
                    m = min(P, TOK - t * P)
                    dve.wait_ge(sho_mm, t + 1)
                    dve.tensor_tensor(out=h[0:m, t, :], in0=h[0:m, t, :], in1=bank(4 + t % 4)[0:m, 0:ED], op=ALU.add)\
                       .then_inc(sho_taken, 1)
                    t_done = t + 1

            def take_hid1(i, s, k):
                dve.wait_ge(hidT_mm[1], i)
                dve.wait_ge(silu1, i + 1)
                dve.tensor_tensor(out=hid[:, s, FF1:2 * FF1], in0=bank(2 + s)[:, FF1:2 * FF1], in1=hid[:, s, 0:FF1],
                                  op=ALU.mult).then_inc(hid_ready[1], 1)

            pipelined(dve, NT1, (take_hid1, 1), (take_y(1), 3))
            dve.wait_ge(gathered, 2 * 16 * NT)
            dve.wait_ge(sho_taken, NT)
            for t in range(NT):
                m = P if t < NT - 1 else B
                last = dve.tensor_tensor(out=h[0:m, t, :], in0=h[0:m, t, :], in1=xn[0:m, t, :], op=ALU.add)
            last.then_inc(experts_done, 1)

        @block.tensor
        def _(pe):
            def product(dst, terms):
                for n, (l, r) in enumerate(terms):
                    last = pe.matmul(dst, l, r, start=n == 0, stop=n == len(terms) - 1)
                return last

            for ahead in (v_mm, s_mm, c_mm, t_mm, lv_mm, s1_mm, c1_mm, t1_mm, *rows_mm, *hidT_mm, *y_mm):
                pe.sem_inc(ahead, 1)

            pe.wait_ge(consts_ready, 1)
            pe.wait_ge(prep_zeroed, 1)
            arrived(pe, "proj")
            product(bank(6)[:, 0:ED], [(ln1_b[:, c:c + 1].broadcast_to((P, P)), w_proj[:, c, :]) for c in range(PC)]
                    + [(ones_row[0:1, :], b_proj[0:1, :])]).then_inc(prep_mm, 1)
            pe.wait_ge(folded, 1)
            for t in range(NCUT + 1):
                if t < NCUT:
                    pe.wait_ge(patch_ready, t + 1)
                    if t >= 2:
                        pe.wait_ge(patchT_ready, t - 1)
                    for c in range(PC):
                        last = pe.transpose(bank(2 * (t % 2), 2)[:, P * c:P * c + P], patch[:, t % 2, P * c:P * c + P],
                                            ident[:])
                    last.then_inc(patch_mm, 1)
                if t:
                    u = t - 1
                    pe.wait_ge(patchT_ready, u + 1)
                    if u >= 2:
                        pe.wait_ge(z_taken, u - 1)
                    product(bank(4 + u % 2)[:, 0:ED], [(patchT[:, u % 2, c, :], wg_proj[:, c, :]) for c in range(PC)])\
                        .then_inc(z_mm, 1)

            arrived(pe, "attn0")
            arrived(pe, "attn1")
            arrived(pe, "small")
            pe.wait_ge(averages_ready, 1)

            def turned(dst, src, ident_n=P):
                return pe.transpose(dst, src, ident[0:ident_n, 0:ident_n])

            for n, what in enumerate(PREP):
                pe.wait_ge(prep_out, 1 + n)
                b = bank(7 - n % 2)
                if what in ("q", "k"):
                    w = wq_raw if what == "q" else wk_raw
                    for m in range(KC):
                        for oc in range(KC):
                            last = pe.matmul(b[:, ED * m + P * oc:ED * m + P * oc + P], w[:, oc, P * m:P * m + P],
                                             centre[:], start=True, stop=True)
                elif what in ("v", "woT"):
                    w = wv_raw if what == "v" else wo_raw
                    for m in range(KC):
                        for oc in range(KC):
                            last = turned(b[:, ED * m + P * oc:ED * m + P * oc + P], w[:, oc, P * m:P * m + P])
                elif what == "router":
                    for m in range(KC):
                        last = turned(b[:, E1 * m:E1 * m + E1], router1[:, P * m:P * m + P], E1)
                elif what == "b1":
                    last = turned(b[:, 0:E0 * FF0 // P], b1_rows[:], E0 * FF0 // P)
                elif what in ("uk0", "uk1"):
                    for m in range(4):
                        hd = m + 4 * (what == "uk1")
                        last = turned(b[:, P * m:P * m + P], uk_raw[:, DK * hd:DK * hd + DK])
                elif what in ("uq", "uv"):
                    w = uq_raw if what == "uq" else uv_raw
                    for hd in range(H1):
                        last = turned(b[:, (DC + 1) * hd:(DC + 1) * (hd + 1)], w[0:DC + 1, DK * hd:DK * hd + DK],
                                      DC + 1)
                elif what == "keyT":
                    for hd in range(H1):
                        o = (DC + 1) * hd
                        pe.matmul(b[:, o:o + DC + 1], ukT[:, hd, :], uqT[:, hd, :], start=True, stop=False)
                        last = pe.matmul(b[:, o:o + DC + 1], qr_raw[0:DC + 1, hd, :], ident[0:DC + 1, 0:DC + 1],
                                         start=False, stop=True)
                elif what == "valO":
                    for hd in range(H1):
                        r, half = 32 * (hd // 2), hd % 2
                        last = pe.matmul(b[r:r + 32, ED * half:ED * half + ED], uvT[:, hd, 0:DC], wo1_raw[:, hd, :],
                                         start=True, stop=True)
                elif what == "bias_o":
                    last = product(b[:, 0:ED], [(uvT[:, hd, DC:DC + 1].broadcast_to((P, P)), wo1_raw[:, hd, :])
                                                for hd in range(H1)] + [(ones_row[0:1, :], b_o[0:1, :])])
                elif what == "mix":
                    pe.wait_ge(tiled_ready, 1)
                    last = pe.matmul(b[:, 0:P], tiled_o[0:H0, :], tiled_v[0:H0, :], start=True, stop=True)
                elif what == "woe":
                    for m in range(KC):
                        last = pe.matmul(b[:, ED * m:ED * m + ED], blockM, woT[:, m, :], start=True, stop=True)
                last.then_inc(prep_mm, 1)

            def layernorm(n):
                for t in range(NT):
                    pe.wait_ge(xn_ready, NT * n + t + 1)
                    if t >= 4:
                        pe.wait_ge(xT_ready, NT * n + t - 3)
                    for k in range(KC):
                        last = turned(bank(t % 4)[:, P * k:P * k + P], xn[:, t, P * k:P * k + P])
                    last.then_inc(xT_mm, 1)
                pe.wait_ge(xT_ready, NT * (n + 1))

            layernorm(0)
            pe.wait_ge(prep_out, 1 + len(PREP))
            for v in range(len(QK) + 1):
                if v < len(QK):
                    which, c, bl = QK[v]
                    c0, n = BLOCKS[bl]
                    if v >= 2:
                        pe.wait_ge(sq_ready, 2 * (v - 1))
                    w = kT if which else qT
                    product(bank(v % 2)[:, 0:n], [(w[:, k, P * c:P * c + P], xT[:, k, c0:c0 + n]) for k in range(KC)])\
                        .then_inc(qk_mm, 1)
                if v:
                    u = v - 1
                    n = BLOCKS[QK[u][2]][1]
                    pe.wait_ge(sq_ready, 2 * (u + 1))
                    if u >= 2:
                        pe.wait_ge(sd_ready, u - 1)
                    pe.matmul(bank(2 + u % 2)[:, 0:n], average[:], sq[:, u % 2, 0:n], start=True, stop=True)\
                      .then_inc(var_mm, 1)
            pe.wait_ge(sd_ready, len(QK))

            def scores0(i, s, k):
                pe.wait_ge(xv_ready, i * 2 + 2)
                pe.wait_ge(v_ready, i * 4)
                product(bank(6)[:, 0:ED], [(xv[:, s, c, :], vT[:, c, :]) for c in range(KC)]).then_inc(v_mm, 1)
                pe.wait_ge(q_ready, i * 2 + 2)
                pe.wait_ge(k_ready, i * 2 + 2)
                pe.wait_ge(s_taken, i)
                for j in range(2):
                    for c in range(KC):
                        last = pe.matmul(bank(2 * s + j)[:, 4 * S * c:4 * S * c + 4 * S], q_ring[:, s, c, j, :],
                                         k_ring[s][:, c, j, :, :], start=True, stop=True)
                last.then_inc(s_mm, 1)

            def turn0(i, s, k):
                pe.wait_ge(p_norm, i + 1)
                pe.wait_ge(pT_ready, i)
                for g in range(8):
                    last = turned(bank(4, 2)[:, P * g:P * g + P], p_ring[:, s, 2 * g:2 * g + 2, :]
                                  .rearrange("p g n -> p (g n)"))
                last.then_inc(t_mm, 1)

            def context0(i, s, k):
                pe.wait_ge(pT_ready, i + 1)
                pe.wait_ge(v_ready, i * 4 + 4)
                pe.wait_ge(c_taken, i)
                for g in range(8):
                    j, c, pair = g // 4, g // 2 % 2, g % 2
                    for half in range(2):
                        r = 32 * (half * 2 + pair)
                        heads = c * 4 + half * 2 + pair
                        last = pe.matmul(bank(7)[r:r + 32, (2 * c + j) * S:(2 * c + j) * S + S],
                                         v_ring[:, s, j, 32 * heads:32 * heads + 32], pT[s][:, 2 * g + half, :],
                                         start=True, stop=True)
                last.then_inc(c_mm, 1)

            pipelined(pe, PAIRS, (turn0, 2), (scores0, 0), (context0, 2))
            pe.wait_ge(c_taken, PAIRS)

            def heads_out(tokens, w, done, before_):
                for t in range(NT):
                    m = P if t < NT - 1 else B
                    if t >= 4:
                        pe.wait_ge(o_taken, before_ + t - 3)
                    product(bank(t % 4)[0:m, 0:ED], [(tokens(c, t), w[:, c, :]) for c in range(2)])\
                        .then_inc(done, 1)

            pe.wait_ge(tile_order, 8)
            heads_out(lambda c, t: ctxT[:, c, P * t:P * t + (P if t < NT - 1 else B)], woe, o_mm, 0)
            layernorm(1)

            def route(l):
                E = e_of[l]
                w = gate_w0 if l == 0 else routerT1
                for t in range(NT):
                    last = product(bank(4)[:, E * t:E * t + E], [(xT[:, k, P * t:P * t + P], w[:, k, :])
                                                                 for k in range(KC)])
                last.then_inc(logits_mm, 1)
                pe.wait_ge(onehot_ready, l + 1)
                oh = onehot[:, :, 0:E]
                rank = bank(5)[:, 0:NT * E].rearrange("p (t e) -> p t e", e=E)
                pe.matmul(rank, before[:], oh, start=True, stop=False)
                for d in range(1, NT):
                    pe.matmul(rank[:, d:NT, :], ones16[:], oh[:, 0:NT - d, :], start=False, stop=d == NT - 1)
                for t in range(NT):
                    last = pe.matmul(bank(6)[:, 0:E], ones16[:], oh[:, t, :], start=t == 0, stop=t == NT - 1)
                last.then_inc(rank_mm, 1)

            route(0)
            pe.wait_ge(slots_ready, 1)
            for n in range(3):
                m = min(4, NT - 4 * n)
                for t in range(4 * n, 4 * n + m):
                    last = turned(bank(5 + n)[0:E0, P * (t - 4 * n):P * (t - 4 * n) + P], onehot_f[:, t, :])
                last.then_inc(ohT_mm, 1)
            pe.wait_ge(ohT_ready, 3)
            arrived(pe, "w1")
            arrived(pe, "w2")

            def turn_rows(l):
                def body(i, s, k):
                    pe.wait_ge(rows_loaded[l][s], k * 16 + 16)
                    pe.wait_ge(rowsT_ready[l], i)
                    for c in range(KC):
                        last = turned(bank(0)[:, P * c:P * c + P], rows_in[:, s, P * c:P * c + P])
                    last.then_inc(rows_mm[l], 1)
                return body

            def hidden0(i, s, k):
                e = pe.value_load(tile_e[0:1, 0, bass.ds(i, 1)], min_val=0, max_val=E0 - 1)
                pe.wait_ge(rowsT_ready[0], i + 1)
                for half in range(2):
                    pe.wait_ge(hid_ready[0], i * 2 + half)
                    product(bank(2 + half), [(rowsT[:, s, c, :], w1[:, bass.ds(e * (KC * FF0) + FF0 * c + 512 * half, 512)])
                                             for c in range(KC)]).then_inc(hid_mm[0], 1)

            def turn_hidden0(i, s, k):
                pe.wait_ge(hid_ready[0], i * 2 + 2)
                pe.wait_ge(hidT_ready[0], i * 8)
                for c in range(FF0 // P):
                    last = turned(bank(4, 2)[:, P * c:P * c + P], hid[:, s, P * c:P * c + P])
                last.then_inc(hidT_mm[0], 1)

            def out0(i, s, k):
                e = pe.value_load(tile_e[0:1, 0, bass.ds(i, 1)], min_val=0, max_val=E0 - 1)
                pe.wait_ge(hidT_ready[0], i * 8 + 8)
                pe.wait_ge(y_ready[0], i)
                product(bank(6)[:, 0:ED], [(hidT[:, s, c, :], w2[:, bass.ds(e * (FF0 // P * ED) + ED * c, ED)])
                                           for c in range(FF0 // P)]).then_inc(y_mm[0], 1)

            pipelined(pe, NT0, (turn_rows(0), 0), (turn_hidden0, 2), (hidden0, 1), (out0, 2))
            for t in range(NT):
                pe.wait_ge(o_taken, NT + max(0, t - 3))
                pe.matmul(bank(t % 4)[:, 0:ED], onehotT[0:E0, t, :], b2[:], start=True, stop=True).then_inc(bias2_mm, 1)

            layernorm(2)
            v = 0
            for w in (down_u, down_k):
                for c0, n in BLOCKS:
                    if v >= 2:
                        pe.wait_ge(lat_ready, v - 1)
                    product(bank(v % 2)[:, 0:n], [(w[:, k, :], xT[:, k, c0:c0 + n]) for k in range(KC)])\
                        .then_inc(lat_mm, 1)
                    v += 1
            pe.wait_ge(lat_ready, 6)
            for v in range(12):
                c0, n = BLOCKS[v % 3]
                if v >= 2:
                    pe.wait_ge(keys_ready, v - 1)
                pe.matmul(bank(2 + v % 2)[:, 0:n], keyT[:, v // 3, :], lat_k[:, c0:c0 + n], start=True, stop=True)\
                  .then_inc(keys_mm, 1)
            pe.wait_ge(keys_ready, 12)

            def scores1(i, s, k):
                pe.wait_ge(lk_ready, i + 1)
                pe.wait_ge(lv_ready, i * 4)
                turned(bank(6)[:, 0:P], lk_ring[:, s, :]).then_inc(lv_mm, 1)
                pe.wait_ge(u_ready, i * 2 + 2)
                pe.wait_ge(s1_taken, i)
                for j in range(2):
                    last = pe.matmul(bank(s)[:, 4 * S * j:4 * S * j + 4 * S], u_ring[:, s, j, :],
                                     keys[:, :, bass.ds(i * (2 * S) + S * j, S)], start=True, stop=True)
                last.then_inc(s1_mm, 1)

            def turn1(i, s, k):
                pe.wait_ge(p1_norm, i + 2)
                pe.wait_ge(pT1_ready, i)
                for g in range(4):
                    last = turned(bank(4)[:, P * g:P * g + P], p1_ring[:, s, 2 * g:2 * g + 2, :]
                                  .rearrange("p g n -> p (g n)"))
                last.then_inc(t1_mm, 1)

            def context1(i, s, k):
                pe.wait_ge(pT1_ready, i + 1)
                pe.wait_ge(lv_ready, i * 4 + 4)
                pe.wait_ge(c1_taken, i * 2)
                for g in range(4):
                    j, half = g // 2, g % 2
                    last = pe.matmul(bank(7)[64 * half:64 * half + 64, 2 * S * j:2 * S * j + 2 * S],
                                     lat_v[:, s, j, :], pT1[s][:, g, :, :].rearrange("p r n -> p (r n)"),
                                     start=True, stop=True)
                last.then_inc(c1_mm, 1)

            pipelined(pe, PAIRS, (turn1, 2), (scores1, 0), (context1, 2))
            pe.wait_ge(c1_taken, 2 * PAIRS)
            heads_out(lambda c, t: ctx1T[:, c, P * t:P * t + (P if t < NT - 1 else B)], valO, o1_mm, 2 * NT)
            layernorm(3)
            route(1)

            arrived(pe, "shared")
            pe.wait_ge(slots_ready, 2)
            for v in range(12):
                if v >= 2:
                    pe.wait_ge(w_ready, v - 1)
                for q in range(4):
                    if v < 8:
                        f, m = 4 * (v % 2) + q, v % 4 // 2
                        src = (g_raw if v < 4 else up_raw)[:, f, P * m:P * m + P]
                    else:
                        f, m = 2 * (v - 8) + q // 2, q % 2
                        src = d_raw[:, m, P * f:P * f + P]
                    last = turned(bank(v % 2)[:, P * q:P * q + P], src)
                last.then_inc(w_mm, 1)
            pe.wait_ge(w_ready, 12)
            v = 0
            for bl, (c0, n) in enumerate(BLOCKS):
                for f in range(SF // P):
                    if v >= 2:
                        pe.wait_ge(silu_ready, v - 1)
                    product(bank(v % 2)[:, 0:n], [(gT[:, k, P * f:P * f + P], xT[:, k, c0:c0 + n]) for k in range(KC)])\
                        .then_inc(shg_mm, 1)
                    if v >= 2:
                        pe.wait_ge(sT_ready, v - 1)
                    product(bank(2 + v % 2)[:, 0:n], [(upT[:, k, P * f:P * f + P], xT[:, k, c0:c0 + n])
                                                      for k in range(KC)]).then_inc(shu_mm, 1)
                    v += 1
                pe.wait_ge(sT_ready, v)
                for t in range(c0 // P, (c0 + n + P - 1) // P):
                    m = min(P, TOK - t * P)
                    if t >= 4:
                        pe.wait_ge(sho_taken, t - 3)
                    product(bank(4 + t % 4)[0:m, 0:ED], [(sT[:, f, P * t - c0:P * t - c0 + m], dT[:, f, :])
                                                         for f in range(SF // P)]).then_inc(sho_mm, 1)
            pe.wait_ge(sho_taken, NT)
            arrived(pe, "gate_up")
            arrived(pe, "down")

            def hidden1(i, s, k):
                e = pe.value_load(tile_e[0:1, 1, bass.ds(i, 1)], min_val=0, max_val=E1 - 1)
                pe.wait_ge(rowsT_ready[1], i + 1)
                pe.wait_ge(hid_ready[1], i)
                product(bank(2 + s), [(rowsT[:, s, c, :], gate_up[:, bass.ds(e * (KC * 2 * FF1) + 2 * FF1 * c, 2 * FF1)])
                                      for c in range(KC)]).then_inc(hid_mm[1], 1)

            def turn_hidden1(i, s, k):
                pe.wait_ge(hid_ready[1], i + 2)
                pe.wait_ge(hidT_ready[1], i)
                for c in range(FF1 // P):
                    last = turned(bank(4)[:, P * c:P * c + P], hid[:, s, FF1 + P * c:FF1 + P * c + P])
                last.then_inc(hidT_mm[1], 1)

            def out1(i, s, k):
                e = pe.value_load(tile_e[0:1, 1, bass.ds(i, 1)], min_val=0, max_val=E1 - 1)
                pe.wait_ge(hidT_ready[1], i + 1)
                pe.wait_ge(y_ready[1], i)
                product(bank(6)[:, 0:ED], [(hidT[:, s, c, :], down[:, bass.ds(e * (FF1 // P * ED) + ED * c, ED)])
                                           for c in range(FF1 // P)]).then_inc(y_mm[1], 1)

            pipelined(pe, NT1, (turn_rows(1), 0), (turn_hidden1, 2), (hidden1, 1), (out1, 3))


def kernel(**inputs):
    import numpy as np
    import concourse.bacc as bacc
    from concourse.bass_utils import run_bass_kernel_spmd as run

    nc = bacc.Bacc("TRN2", target_bir_lowering=False, num_devices=1)
    arrays, args = {}, {}
    for name, value in inputs.items():
        v = np.ascontiguousarray(value)
        arrays[f"in_{name}"] = v
        args[name] = nc.dram_tensor(f"in_{name}", v.shape, mybir.dt.from_np(v.dtype), kind="ExternalInput").ap()
    out = nc.dram_tensor("out", (B, S, ED), F32, kind="ExternalOutput").ap()
    vit_tower(nc, args, out)
    r = run(nc, [arrays], core_ids=[0])
    return r.results[0]["out"]
```

```python
import concourse.bass as bass
from concourse import mybir
from contextlib import ExitStack

F32 = mybir.dt.float32
BF16 = mybir.dt.bfloat16
I32 = mybir.dt.int32
U32 = mybir.dt.uint32
ALU = mybir.AluOpType
ACT = mybir.ActivationFunctionType
AX = mybir.AxisListType

P = 128
B, C, HW, PS = 32, 3, 96, 16
G = HW // PS
ED = 256
KC = ED // P
PD = C * PS * PS
PC = PD // P
NP = G * G
S = NP + 1
TOK = B * S
NT = 10
QP = 64
PAIRS = B // 2
EPS = 1e-5
QKR = 4

H0, HD0 = 16, 16
E0, FF0, NT0 = 8, 1024, 17
H1, DK, DC = 8, 128, 32
E1, FF1, NT1, SF = 16, 256, 25, 1024

assert NT0 == (TOK + E0 * (P - 1)) // P and NT1 == (TOK + E1 * (P - 1)) // P
BLOCKS = [(0, 512), (512, 512), (1024, TOK - 1024)]


class Chain:

    def __init__(self, engine, sem, per=None):
        self.engine, self.sem, self.per, self.base, self.n = engine, sem, per, 0, 0

    def at(self, i):
        assert self.n in (0, self.per), (self.n, self.per)
        self.base, self.n = i * self.per, 0

    def did(self, ins):
        ins.then_inc(self.sem, 1)
        self.n += 1

    def wait(self):
        self.engine.wait_ge(self.sem, self.base + self.n)


def pipelined(engine, n, *stages):
    longest = max(delay for _, delay in stages)

    def step(at, r=None):
        for f, delay in stages:
            i = at - delay
            if r is not None:
                f(r * 2 + i, i % 2, r + i // 2)
            elif 0 <= i < n:
                f(i, i % 2, i // 2)

    first = (longest + 3) // 2
    for at in range(2 * first):
        step(at)
    with engine.Fori(first, n // 2) as r:
        step(0, r)
        step(1, r)
    for at in range(2 * (n // 2), n + longest):
        step(at)


def vit_tower(nc, a, out):
    ctx = ExitStack()
    with ctx:
        def sb(name, shape, dt=F32):
            return ctx.enter_context(nc.sbuf_tensor(name, shape, dt))[:]

        def sem(name):
            return ctx.enter_context(nc.semaphore(name))

        sorted_x = [nc.dram_tensor("sorted_x0", (NT0 * P, ED), F32, kind="Internal").ap(),
                    nc.dram_tensor("sorted_x1", (NT1 * P, ED), F32, kind="Internal").ap()]
        sorted_y = [nc.dram_tensor("sorted_y0", (NT0 * P, ED), F32, kind="Internal").ap(),
                    nc.dram_tensor("sorted_y1", (NT1 * P, ED), F32, kind="Internal").ap()]

        shuffled = nc.dram_tensor("shuffled", (HD0, S * H0, B), F32, kind="Internal").ap()

        h = sb("h", [P, NT, ED])
        xn = sb("xn", [P, NT, ED])
        xT = sb("xT", [P, KC, NT * P])
        ident = sb("ident", [P, P])
        block16 = sb("block16", [P, 8, 16])
        centre = sb("centre", [P, P])
        average = sb("average", [P, P])
        ones_row = sb("ones_row", [1, P])
        before = sb("before", [P, P], BF16)
        ones16 = sb("ones16", [P, P], BF16)
        iota_e = sb("iota_e", [P, 17 * 2])
        thresholds = sb("thresholds", [P, NT])
        lower_e = sb("lower_e", [P, E1, E1])
        eps_col = sb("eps_col", [P, 1])
        stats = sb("stats", [P, NT, 3, 6])
        meanvar = sb("meanvar", [P, NT, 2])
        sd = sb("sd", [P, NT])
        rstd = sb("rstd", [P, NT])

        logits = sb("logits", [P, NT, E1])
        top = sb("top", [P, NT])
        first = sb("first", [P, NT])
        mask = sb("mask", [P, NT, E1])
        onehot = sb("onehot", [P, NT, E1], BF16)
        weight = sb("weight", [P, NT])
        counts_over = sb("counts_over", [P, E1, NT])
        tiles_e = sb("tiles_e", [P, E1])
        base_e = sb("base_e", [P, E1])
        end_e = sb("end_e", [P, E1])
        base_tmp = sb("base_tmp", [P, E1, E1])
        slot_f = sb("slot_f", [P, NT])
        slot = sb("slot", [P, 2, NT], I32)
        tile_cmp = sb("tile_cmp", [1, NT1, E1])
        tile_e_f = sb("tile_e_f", [1, NT1])
        tile_e = sb("tile_e", [1, 2, NT1], I32)
        onehot_f = sb("onehot_f", [P, NT, E0])

        gate_w0 = sb("gate_w0", [P, KC, E0])
        router1 = sb("router1", [E1, ED])
        routerT1 = sb("routerT1", [P, KC, E1])
        b1T = sb("b1T", [P, E0, FF0 // P])
        b2 = sb("b2", [E0, ED])
        b1_rows = sb("b1_rows", [E0 * FF0 // P, P])
        q_w = sb("q_w", [P, 1])
        q_b = sb("q_b", [P, 1])
        k_w = sb("k_w", [P, 1])
        k_b = sb("k_b", [P, 1])
        k_of = sb("k_of", [P, 4])
        down_u = sb("down_u", [P, KC, P])
        down_k = sb("down_k", [P, KC, P])
        bias_u = sb("bias_u", [P, 1])
        bias_k = sb("bias_k", [P, 1])
        keyT = sb("keyT", [P, H1 // 2, P])
        valO = sb("valO", [P, 2, ED])
        bias_o = sb("bias_o", [P, ED])

        KB = 256
        R1, R2, R3, RE = 0, 64 * KB, 96 * KB, 156 * KB
        arena = sb("arena", [P, RE])
        arena_ap = arena[:, :]

        class Area:

            def __init__(self, start, end):
                self.next, self.end = start, end

            def take(self, *shape):
                n = 1
                for x in shape:
                    n *= x
                v = arena_ap[:, self.next:self.next + n]
                self.next += n
                assert self.next <= self.end, (self.next, self.end)
                if len(shape) == 1:
                    return v
                names = "abcd"[:len(shape)]
                return v.rearrange(f"p ({' '.join(names)}) -> p {' '.join(names)}",
                                   **{c: s for c, s in zip(names, shape)})

        w1 = arena_ap[:, R1:R1 + E0 * KC * FF0]
        w2 = arena_ap[:, R2:R2 + E0 * FF0 // P * ED]
        gate_up = arena_ap[:, R1:R1 + E1 * KC * 2 * FF1]
        down = arena_ap[:, R2:R2 + E1 * FF1 // P * ED]

        wx = Area(R2 - 8 * KB, R2)
        qT, kT, vT, woe = (wx.take(KC, ED) for _ in range(4))

        prep = Area(R2, R3)
        wq_raw, wk_raw, wv_raw, wo_raw = (prep.take(KC, ED) for _ in range(4))
        uk_raw, uq_raw, uv_raw = (prep.take(H1 * DK) for _ in range(3))
        qr_raw = prep.take(H1, P)
        ukT = prep.take(H1, P)
        uqT = prep.take(H1, DC + 1)
        uvT = prep.take(H1, DC + 1)
        rawsq = Area(R2 + 8 * KB, R3)
        raw = rawsq.take(QKR, 512)
        sq = rawsq.take(QKR, 512)

        emb = Area(R3, RE)
        x_a = emb.take(C, PS, HW)
        wo1_raw = emb.take(H1, ED)
        sparse_v = emb.take(16, P)
        sparse_o = emb.take(P, 16)
        woT = emb.take(KC, ED)
        b_o = emb.take(ED)
        tiled_v, tiled_o, blockM = (emb.take(P) for _ in range(3))
        sv_w, so_w = emb.take(16), emb.take(16)
        emb1 = Area(R1, R2 - 8 * KB)
        x_b = emb1.take(C, PS, HW // 2)
        patch = emb1.take(2, PD)
        patchT = emb1.take(2, PC, P)
        w_proj = emb1.take(PC, ED)
        wg_proj = emb1.take(PC, ED)
        ln1_g, ln1_b = emb1.take(PC), emb1.take(PC)
        b_proj, bias_z, ln2_g, ln2_b = (emb1.take(ED) for _ in range(4))
        zero = emb1.take(8 * ED)

        at0 = Area(R3, RE)
        qn = at0.take(KC, B, S)
        kn = at0.take(KC, B, S)
        ctxT = at0.take(KC, S * B)
        q_ring = at0.take(2, KC, 2, 2 * QP)
        k_ring = [at0.take(KC, 2, 4, S) for _ in range(2)]
        xv = at0.take(2, KC, 2 * QP)
        v_ring = at0.take(2, 2, ED)
        yT = qn.rearrange("p c b n -> p c (b n)")
        p_ring = at0.take(2, 16, QP)
        pT = [at0.take(16, S) for _ in range(2)]
        mx = at0.take(2, 16)
        sm = at0.take(2, 16)

        def rings(area, width, chunks):
            return (area.take(2, ED), area.take(2, KC, P), area.take(2, width), area.take(2, chunks, P),
                    area.take(2, ED))

        moe = Area(R3 + 32 * KB, RE)
        onehotT = moe.take(NT, P)
        experts0 = rings(moe, FF0, FF0 // P)

        at1 = Area(R3, RE)
        lat_u = at1.take(B, QP)
        lat_k = at1.take(B * S)
        keys = at1.take(H1 // 2, B * S)
        ctx1T = at1.take(2, NT * P)
        lat_v = at1.take(2, 2, 2 * DC)
        u_ring = at1.take(2, 2, 2 * QP)
        lk_ring = at1.take(2, 2 * QP)
        p1_ring = at1.take(2, 8, QP)
        pT1 = [at1.take(4, 2, S) for _ in range(2)]
        mx1 = at1.take(2, 8)
        sm1 = at1.take(2, 8)

        sh = Area(R3, RE)
        gT = sh.take(KC, SF)
        upT = sh.take(KC, SF)
        dT = sh.take(SF // P, ED)
        sT = sh.take(SF // P, 512)
        sg = sh.take(2, 512)
        experts1 = rings(sh, 2 * FF1, FF1 // P)
        sh_raw = Area(R2, R3)
        g_raw = sh_raw.take(SF // P, ED)
        up_raw = sh_raw.take(SF // P, ED)
        d_raw = sh_raw.take(KC, SF)
        rows_in, rowsT, hid, hidT, rows_out = zip(experts0, experts1)

        psum = ctx.enter_context(nc.psum_tensor("psum", [P, 8 * 512], F32))

        def bank(b, n=1):
            return psum[:, 512 * b:512 * (b + n)]

        x = a["x"]
        loads = {}
        loads["x_a"] = [(x_a[32 * r:32 * r + 32, :, :, :].rearrange("p c i w -> p c (i w)"),
                         x[:, :, PS * r:PS * (r + 1), :].rearrange("b c i w -> b c (i w)")) for r in range(4)]
        loads["x_b"] = [(x_b[64 * wh + 32 * r:64 * wh + 32 * r + 32, c, :, :],
                         x[:, c, PS * (4 + r):PS * (5 + r), 48 * wh:48 * wh + 48])
                        for wh in range(2) for r in range(2) for c in range(C)]
        wp = a["L0_tok_W_proj"].rearrange("(f c) e -> c f e", c=C)
        loads["proj"] = [(w_proj[:, 2 * c:2 * c + 2, :], wp[c].rearrange("(k p) e -> p k e", p=P)) for c in range(C)] + [
            (v.rearrange("p (c k) -> p c k", c=C), a[name].rearrange("(k p c) -> p c k", p=P, c=C))
            for v, name in ((ln1_g, "L0_tok_ln1_g"), (ln1_b, "L0_tok_ln1_b"))] + [
            (b_proj[0:1, :], a["L0_tok_b_proj"].rearrange("(o e) -> o e", o=1)),
            (b_o[0:1, :], a["L1_attn_b_O"].rearrange("(o e) -> o e", o=1)),
            (ln2_g, a["L0_tok_ln2_g"].rearrange("(o e) -> o e", o=1).broadcast_to((P, ED))),
            (ln2_b, a["L0_tok_ln2_b"].rearrange("(o e) -> o e", o=1).broadcast_to((P, ED)))]
        pos = a["L0_tok_pos_emb"]

        def token_runs():
            for j in range(4):
                yield 0, G, j, 1 + G * j
            for j in range(4):
                yield G, G // 2, j, 1 + G * (4 + j % 2) + G // 2 * (j // 2)

        loads["pos"] = [(h[32 * j:32 * j + 32, t:t + nt, :], pos[:, n:n + nt, :].broadcast_to((32, nt, ED)))
                        for t, nt, j, n in token_runs()]
        cls_pos = xn[0:32, NT - 1, :]
        loads["cls"] = [(h[0:32, NT - 1, :], pos[0, 0:1, :].broadcast_to((32, ED))),
                        (cls_pos, a["L0_tok_cls_token"][0, 0:1, :].broadcast_to((32, ED)))]

        def rows(name):
            return a[name].rearrange("(k p) e -> p k e", p=P)
        loads["attn0"] = [(wq_raw, rows("L0_attn_W_Q")), (wk_raw, rows("L0_attn_W_K")),
                          (wv_raw, rows("L0_attn_W_V")), (wo_raw, rows("L0_attn_W_O")),
                          (sparse_v[0:H0], a["L0_attn_sparse_W_V"]), (sparse_o[0:H0], a["L0_attn_sparse_W_O"])]
        loads["small"] = [(d[:, :],
                           a[n].rearrange("(q d o) -> q d o", q=1, o=1).broadcast_to((P // HD0, HD0, 1)))
                          for d, n in ((q_w, "L0_attn_q_ln_w"), (q_b, "L0_attn_q_ln_b"),
                                       (k_w, "L0_attn_k_ln_w"), (k_b, "L0_attn_k_ln_b"))]
        loads["small"] += [(gate_w0, rows("L0_ffn_gate_w")), (router1, a["L1_ffn_router_w"]), (b2, a["L0_ffn_b2"])]
        loads["small"] += [(b1_rows[:], a["L0_ffn_b1"].rearrange("e (c p) -> (e c) p", p=P))]
        row = lambda name: a[name].rearrange("(o e) -> o e", o=1)
        col = lambda name: a[name].rearrange("(d o) -> d o", o=1)
        loads["attn1"] = [
            (down_u[:, :, 0:DC], rows("L1_attn_W_DQ")), (down_u[:, :, 64:64 + DC], rows("L1_attn_W_DQ")),
            (down_k[:, :, 0:DC], rows("L1_attn_W_DKV")), (down_k[:, :, DC:2 * DC], rows("L1_attn_W_KR")),
            (bias_u[0:DC, :], col("L1_attn_b_DQ")), (bias_u[64:64 + DC, :], col("L1_attn_b_DQ")),
            (bias_k[0:DC, :], col("L1_attn_b_DKV")), (bias_k[DC:2 * DC, :], col("L1_attn_b_KR")),
            (uk_raw[0:DC, :], a["L1_attn_W_UK"]), (uk_raw[64:65, :], row("L1_attn_b_UK")),
            (uq_raw[0:DC, :], a["L1_attn_W_UQ"]), (uq_raw[DC:DC + 1, :], row("L1_attn_b_UQ")),
            (uv_raw[0:DC, :], a["L1_attn_W_UV"]), (uv_raw[DC:DC + 1, :], row("L1_attn_b_UV")),
            (qr_raw[0:DC, :, DC:2 * DC], a["L1_attn_W_QR"].rearrange("c (h r) -> c h r", h=H1)),
            (qr_raw[DC:DC + 1, :, DC:2 * DC], row("L1_attn_b_QR").rearrange("o (h r) -> o h r", h=H1)),
            (wo1_raw, rows("L1_attn_W_O"))]
        w1v = w1.rearrange("p (e k f) -> p e k f", e=E0, k=KC)
        w2v = w2.rearrange("p (e c n) -> p e c n", e=E0, n=ED)
        W1 = a["L0_ffn_w1"].rearrange("e (k p) f -> p e k f", p=P)
        W2 = a["L0_ffn_w2"].rearrange("e (c p) n -> p e c n", p=P)
        loads["w1"] = [(w1v[:, e], W1[:, e]) for e in range(E0)]
        loads["w2"] = [(w2v[:, e], W2[:, e]) for e in range(E0)]
        guv = gate_up.rearrange("p (e k f) -> p e k f", e=E1, k=KC)
        dv = down.rearrange("p (e c n) -> p e c n", e=E1, n=ED)
        GU = a["L1_ffn_gate_up_proj"].rearrange("e (k p) f -> p e k f", p=P)
        DN = a["L1_ffn_down_proj"].rearrange("e (c p) n -> p e c n", p=P)
        loads["gate_up"] = [(guv[:, e], GU[:, e]) for e in range(E1)]
        loads["down"] = [(dv[:, 2 * e:2 * e + 2], DN[:, 2 * e:2 * e + 2]) for e in range(E1 // 2)]
        loads["shared"] = [(g_raw, rows("L1_ffn_shared_gate_w")), (up_raw, rows("L1_ffn_shared_up_w")),
                           (d_raw, rows("L1_ffn_shared_down_w"))]
        load_sem = {name: sem(f"ld_{name}") for name in loads}

        def arrived(engine, name, n=None):
            engine.wait_ge(load_sem[name], 16 * (len(loads[name]) if n is None else n))

        (prep_zeroed, consts_ready, averages_ready, prep_mm, prep_out, tiled_ready, folded, ln1_stats, ln1_sd,
         patch_ready, patch_mm, patchT_ready, z_mm, z_taken, ln2_stats, ln2_sd, pos_ready, embedded,
         ln_stats, ln_sd, xn_ready, xT_mm, xT_ready,
         qk_mm, sq_ready, var_mm, sd_ready, qk_norm, khead_ready, at0_zeroed,
         xv_ready, v_mm, v_ready, q_ready, k_ready, s_mm, s_taken, p_exp, p_sum, p_norm, t_mm, pT_ready, c_mm,
         c_taken, o_mm, o_taken,
         logits_mm, top_ready, gate_ready, onehot_ready, rank_mm, slots_ready, zero_stored, scattered, ohT_mm, ohT_ready,
         bias2_mm,
         lat_mm, lat_ready, keys_mm, keys_ready, at1_zeroed, u_ready, lk_ready, lv_mm, lv_ready,
         s1_mm, s1_taken, p1_exp, p1_sum, p1_norm, t1_mm, pT1_ready, c1_mm, c1_taken, o1_mm, bias_added,
         w_mm, w_ready, shg_mm, shu_mm, silu_ready, sT_ready, sho_mm, sho_taken, stored, xscaled) = [sem(n) for n in """
         prep_zeroed consts_ready averages_ready prep_mm prep_out tiled_ready folded ln1_stats ln1_sd
         patch_ready patch_mm patchT_ready z_mm z_taken ln2_stats ln2_sd pos_ready embedded
         ln_stats ln_sd xn_ready xT_mm xT_ready
         qk_mm sq_ready var_mm sd_ready qk_norm khead_ready at0_zeroed
         xv_ready v_mm v_ready q_ready k_ready s_mm s_taken p_exp p_sum p_norm t_mm pT_ready c_mm
         c_taken o_mm o_taken
         logits_mm top_ready gate_ready onehot_ready rank_mm slots_ready zero_stored scattered ohT_mm ohT_ready
         bias2_mm
         lat_mm lat_ready keys_mm keys_ready at1_zeroed u_ready lk_ready lv_mm lv_ready
         s1_mm s1_taken p1_exp p1_sum p1_norm t1_mm pT1_ready c1_mm c1_taken o1_mm bias_added
         w_mm w_ready shg_mm shu_mm silu_ready sT_ready sho_mm sho_taken stored xscaled""".split()]
        rows_loaded = [[sem(f"rows_loaded{l}{s}") for s in range(2)] for l in range(2)]
        rows_mm = [sem(f"rows_mm{l}") for l in range(2)]
        rowsT_ready = [sem(f"rowsT_ready{l}") for l in range(2)]
        hid_mm = [sem(f"hid_mm{l}") for l in range(2)]
        hid_ready = [sem(f"hid_ready{l}") for l in range(2)]
        hidT_mm = [sem(f"hidT_mm{l}") for l in range(2)]
        hidT_ready = [sem(f"hidT_ready{l}") for l in range(2)]
        y_mm = [sem(f"y_mm{l}") for l in range(2)]
        y_ready = [sem(f"y_ready{l}") for l in range(2)]
        y_stored = [[sem(f"y_stored{l}{s}") for s in range(2)] for l in range(2)]
        experts_done = sem("experts_done")
        spread, reshuffled, tile_order = sem("spread"), sem("reshuffled"), sem("tile_order")

        def to_tiles(c):
            y = yT[:, c, :].rearrange("p (n b) -> p n b", b=B)
            o = ctxT[:, c, :].rearrange("p (n b) -> p n b", b=B)
            yield (o[:, 0:4 * G, :].rearrange("p (t j) b -> p t j b", j=4),
                   y[:, 1:1 + 4 * G, :].rearrange("p (j t) b -> p t j b", j=4))
            late_o = o[:, 4 * G:6 * G, :].rearrange("p (u w r) b -> p w u r b", w=2, r=2)
            late_y = y[:, 1 + 4 * G:1 + 6 * G, :].rearrange("p (r w u) b -> p w u r b", r=2, w=2)
            for w in range(2):
                yield late_o[:, w], late_y[:, w]
            yield o[:, S - 1, :], y[:, 0, :]
        gathered = [sem(f"gathered{t}") for t in range(NT)]
        silu1, mixed = sem("silu1"), sem("mixed")

        QK = [(which, c, n) for which in range(2) for c in range(KC) for n in range(len(BLOCKS))]
        SCALE0, SCALE1 = HD0 ** -0.5, (DK + DC) ** -0.5
        PREP = ["q", "k", "v", "woT", "uk0", "uk1", "uq", "uv", "keyT", "mix", "router", "woe", "b1", "valO",
                "bias_o"]
        PREP_AT = 5
        MIX = PREP.index("mix")

        def prep_done(n):
            return 1 + n + 1 - (n >= MIX)
        NCUT = 9

        def halves(n):
            return [(0, 5), (5, NT)] if n else [(0, NT)]
        e_of = [E0, E1]
        nt_of = [NT0, NT1]

        block = ctx.enter_context(nc.Block())

        @block.sync
        def _(sp):
            def load(name, part=slice(None)):
                with nc.allow_non_contiguous_dma(reason="columns of a few vectors"):
                    for dst, src in loads[name][part]:
                        sp.dma_start(dst, src).then_inc(load_sem[name], 16)

            load("x_a")
            load("proj")
            load("x_b")
            load("attn0")
            sp.wait_ge(prep_zeroed, 1)
            load("attn1")
            load("pos")
            load("cls")
            load("small")
            for l in range(2):
                zx = sorted_x[l].rearrange("(n p) e -> p n e", p=P)
                for n in range(0, nt_of[l], 8):
                    m = min(8, nt_of[l] - n)
                    sp.dma_start(zx[:, n:n + m, :], zero[:, 0:m * ED].rearrange("p (n e) -> p n e", e=ED))\
                      .then_inc(zero_stored, 16)
            sp.wait_ge(zero_stored, 16 * 7)
            sp.wait_ge(embedded, 1)
            load("w1", slice(0, E0 - 1))
            sp.wait_ge(qk_norm, len(QK))
            load("w2", slice(0, E0 // 2))
            sp.wait_ge(c_taken, PAIRS)
            for hd in range(H0):
                r = HD0 * (hd % 8)
                sp.dma_start(shuffled.rearrange("d (q h) b -> h d q b", h=H0)[hd],
                             ctxT[r:r + HD0, hd // 8, :].rearrange("p (q b) -> p q b", b=B)).then_inc(spread, 16)
            sp.wait_ge(spread, 16 * H0)
            for hd in range(H0):
                r = HD0 * (hd % 8)
                sp.dma_start(yT[r:r + HD0, hd // 8, :], shuffled[:, S * hd:S * hd + S, :]
                             .rearrange("d q b -> d (q b)")).then_inc(reshuffled, 16)
            sp.wait_ge(o_mm, NT)
            load("w1", slice(E0 - 1, E0))
            load("w2", slice(E0 // 2, E0))

            def experts(l):
                xs = sorted_x[l].rearrange("(t p) e -> p t e", p=P)

                def front(i, s, k):
                    sp.wait_ge(rows_mm[l], i)
                    sp.dma_start(rows_in[l][:, s:s + 1, :], xs[:, bass.ds(i, 1), :]).then_inc(rows_loaded[l][s], 16)

                sp.wait_ge(scattered, 16 * NT * (l + 1))
                pipelined(sp, nt_of[l], (front, 0))

            experts(0)
            sp.wait_ge(y_mm[0], NT0 + 1)
            for t in range(NT):
                sp.wait_ge(gathered[t], 16)
            load("shared")
            load("gate_up")
            sp.wait_ge(w_mm, 12)
            load("down")
            experts(1)
            n = 0
            for t, nt, j, tok in token_runs():
                if j == 0:
                    sp.wait_ge(experts_done, NT)
                    sp.wait_ge(sho_taken, t + nt)
                sp.dma_start(out[:, tok:tok + nt, :], h[32 * j:32 * j + 32, t:t + nt, :]).then_inc(stored, 16)
                n += 1
            sp.wait_ge(sho_taken, NT)
            sp.dma_start(out[:, 0, :], h[0:32, NT - 1, :]).then_inc(stored, 16)
            sp.wait_ge(stored, 16 * (n + 1))

        @block.gpsimd
        def _(pool):
            ch = Chain(pool, sem("pool_chain"))

            def zeroed(*views):
                for v in views:
                    ch.did(pool.memset(v, 0.0))

            zeroed(keyT[:], down_u[:], down_k[:], bias_u[:], bias_k[:], uk_raw, uq_raw, uv_raw, qr_raw, zero,
                   h[:, NT - 1, :])
            ch.wait()
            for v, at in ((bias_u, DC), (bias_u, 64 + DC), (bias_k, 2 * DC)):
                ch.did(pool.affine_select(out=v[:], in_=v[:], pattern=[[0, 1]], compare_op=ALU.not_equal,
                                          fill=1.0, base=-at, channel_multiplier=1))
                ch.wait()
            pool.memset(ones_row[:], 1.0).then_inc(prep_zeroed, 1)

            def select(v, pattern, op, fill, base, mult):
                ch.did(pool.affine_select(out=v, in_=v, pattern=pattern, compare_op=op, fill=fill, base=base,
                                          channel_multiplier=mult))
                ch.wait()
            ch.did(pool.memset(ident[:], 0.0))
            ch.did(pool.memset(block16[:], 1.0))
            ch.did(pool.memset(ones16[:], 1.0))
            ch.did(pool.memset(before[:], 1.0))
            ch.did(pool.memset(lower_e[:], 1.0))
            ch.did(pool.memset(eps_col[:], EPS))
            ch.wait()
            select(ident[:], [[-1, P]], ALU.not_equal, 1.0, 0, 1)
            select(block16[:], [[-16, 8], [0, 16]], ALU.is_ge, 0.0, 0, 1)
            select(block16[:], [[16, 8], [0, 16]], ALU.is_ge, 0.0, 15, -1)
            select(before[:], [[1, P]], ALU.is_gt, 0.0, 0, -1)
            select(lower_e[:], [[1, E1], [-1, E1]], ALU.is_gt, 0.0, 0, 0)
            ch.did(pool.iota(iota_e[:], pattern=[[1, 34]], base=0, channel_multiplier=0,
                             allow_small_or_imprecise_dtypes=True))
            ch.did(pool.iota(thresholds[:], pattern=[[P, NT]], base=0, channel_multiplier=0,
                             allow_small_or_imprecise_dtypes=True))
            ch.wait()
            pool.sem_inc(consts_ready, 1)

            arrived(pool, "pos")
            arrived(pool, "proj")
            hp = h[:, 0:NCUT, :]
            pool.tensor_tensor(out=hp, in0=hp, in1=ln2_b.rearrange("p (o e) -> p o e", o=1)
                               .broadcast_to((P, NCUT, ED)), op=ALU.add).then_inc(pos_ready, 1)
            arrived(pool, "cls")
            pool.tensor_tensor(out=h[0:32, NT - 1, :], in0=h[0:32, NT - 1, :], in1=cls_pos, op=ALU.add)\
                .then_inc(pos_ready, 1)

            pool.wait_ge(embedded, 1)
            pool.wait_ge(prep_out, prep_done(len(PREP) - 1))
            for v in (q_ring, xv, v_ring, p_ring):
                last = pool.memset(v, 0.0)
                ch.did(last)
            ch.wait()
            pool.sem_inc(at0_zeroed, 1)

            pool.wait_ge(qk_norm, len(QK))
            pool.wait_ge(khead_ready, 1 + len(QK) // 2)
            ln_tok = xT.rearrange("p k (n b) -> p k b n", b=B)

            def front(i, s, k):
                pool.wait_ge(v_mm, i)
                for k in range(KC):
                    ins = pool.tensor_copy(xv[:, s, k, :].rearrange("p (j n) -> p j n", j=2)[:, :, 0:S],
                                           ln_tok[:, k, bass.ds(i * 2, 2), 0:S])
                    ins.then_inc(xv_ready, 1)
                pool.wait_ge(s_mm, i)
                for c in range(KC):
                    pool.tensor_tensor(
                        out=k_ring[s][:, c],
                        in0=kn[:, c, bass.ds(i * 2, 2), :].rearrange("p j (o n) -> p j o n", o=1)
                        .broadcast_to((P, 2, 4, S)),
                        in1=k_of[:].rearrange("p (o h q) -> p o h q", o=1, q=1).broadcast_to((P, 2, 4, S)),
                        op=ALU.mult).then_inc(k_ready, 1)

            def back(i, s, k):
                pool.wait_ge(p_sum, i + 1)
                pv = p_ring[:, s, :, 0:S]
                pool.tensor_tensor(out=pv, in0=pv, in1=sm[:, s, :].rearrange("p (g o) -> p g o", o=1)
                                   .broadcast_to((P, 16, S)), op=ALU.mult).then_inc(p_norm, 1)

            pipelined(pool, PAIRS, (front, 0), (back, 1))

            def scatter(l):
                pool.wait_ge(slots_ready, l + 1)
                pool.wait_ge(zero_stored, 16 * 7)
                for t in range(NT):
                    n = P if t < NT - 1 else B
                    pool.indirect_dma_start(
                        out=sorted_x[l], out_offset=bass.IndirectOffsetOnAxis(
                            ap=slot[0:n, l, t:t + 1].bitcast(U32), axis=0),
                        in_=xn[0:n, t, :], in_offset=None).then_inc(scattered, 16)

            def store_rows(l):
                ys = sorted_y[l].rearrange("(t p) e -> p t e", p=P)

                def store(i, s, k):
                    pool.wait_ge(y_ready[l], i + 1)
                    pool.dma_start(ys[:, bass.ds(i, 1), :], rows_out[l][:, s:s + 1, :]).then_inc(y_stored[l][s], 16)

                pipelined(pool, nt_of[l], (store, 0))

            def gather(l):
                for s in range(2):
                    pool.wait_ge(y_stored[l][s], 16 * ((nt_of[l] + 1 - s) // 2))
                pool.wait_ge(scattered, 16 * NT * (l + 1))
                for t in range(NT):
                    n = P if t < NT - 1 else B
                    pool.indirect_dma_start(
                        out=xn[0:n, t, :], out_offset=None, in_=sorted_y[l],
                        in_offset=bass.IndirectOffsetOnAxis(ap=slot[0:n, l, t:t + 1].bitcast(U32), axis=0))\
                        .then_inc(gathered[t], 16)

            scatter(0)
            store_rows(0)
            gather(0)

            pool.wait_ge(y_mm[0], NT0 + 1)
            pool.wait_ge(bias2_mm, NT)
            for v in (lat_u, lat_v, u_ring, lk_ring, p1_ring, ctx1T):
                ch.did(pool.memset(v, 0.0))
            ch.wait()
            pool.sem_inc(at1_zeroed, 1)
            pool.wait_ge(lat_ready, 6)

            pool.sem_inc(p1_norm, 1)

            def front1(i, s, k):
                pool.wait_ge(lv_mm, i)
                pool.wait_ge(p1_norm, i)
                pool.tensor_copy(lk_ring[:, s, :].rearrange("p (j n) -> p j n", j=2)[:, :, 0:S],
                                 lat_k.rearrange("p (b n) -> p b n", n=S)[:, bass.ds(i * 2, 2), :])\
                    .then_inc(lk_ready, 1)

            def back1(i, s, k):
                pool.wait_ge(p1_sum, i + 1)
                pool.wait_ge(lk_ready, i + 1)
                pv = p1_ring[:, s, :, 0:S]
                pool.tensor_tensor(out=pv, in0=pv, in1=sm1[:, s, :].rearrange("p (g o) -> p g o", o=1)
                                   .broadcast_to((P, 8, S)), op=ALU.mult).then_inc(p1_norm, 1)

            pipelined(pool, PAIRS, (front1, 0), (back1, 1))
            scatter(1)
            store_rows(1)
            gather(1)

        @block.scalar
        def _(act):
            def evacuated(sems, dst, src, **kw):
                ins = act.activation(dst, src, ACT.Copy)
                ins.then_inc(sems, 1)

            act.wait_ge(prep_mm, 1)
            evacuated(prep_out, bias_z, bank(6)[:, 0:ED])

            def ln1_deviation(n, t0, t1):
                act.wait_ge(ln1_stats, n + 1)
                act.activation(sd[:, t0:t1], meanvar[:, t0:t1, 1], ACT.Sqrt, bias=eps_col[:, 0:1])\
                   .then_inc(ln1_sd, 1)

            def prep_out_of_psum(n):
                what = PREP[n]
                if what == "mix":
                    return
                act.wait_ge(prep_mm, n + 2)
                src = bank(7 - n % 2)
                two = lambda v: v.rearrange("p k e -> p (k e)")
                if what in ("q", "k", "v", "woT", "woe"):
                    dst = {"q": qT, "k": kT, "v": vT, "woT": woT, "woe": woe}[what]
                    evacuated(prep_out, two(dst), src)
                elif what == "router":
                    evacuated(prep_out, two(routerT1[:]), src[:, 0:KC * E1])
                elif what == "b1":
                    evacuated(prep_out, two(b1T[:]), src[:, 0:E0 * FF0 // P])
                elif what in ("uk0", "uk1"):
                    m = 4 * (what == "uk1")
                    evacuated(prep_out, two(ukT[:, m:m + 4, :]), src)
                elif what in ("uq", "uv"):
                    evacuated(prep_out, two(uqT if what == "uq" else uvT), src[:, 0:H1 * (DC + 1)])
                elif what == "keyT":
                    evacuated(prep_out, keyT[:].rearrange("p a (r n) -> p (a r) n", r=2)[:, :, 0:DC + 1],
                              src[:, 0:H1 * (DC + 1)].rearrange("p (g n) -> p g n", g=H1))
                elif what == "valO":
                    evacuated(prep_out, two(valO[:]), src)
                elif what == "bias_o":
                    evacuated(prep_out, bias_o[:], src[:, 0:ED])

            ln1_deviation(0, 0, G)
            for t in range(NCUT):
                act.wait_ge(patch_mm, t + 1)
                if t >= 2:
                    act.wait_ge(z_mm, t - 1)
                act.activation(patchT[:, t % 2].rearrange("p c n -> p (c n)"),
                               bank(2 * (t % 2), 2)[:, 0:PD], ACT.Copy).then_inc(patchT_ready, 1)
                if t == G - 1:
                    ln1_deviation(1, G, NCUT)
                if t >= PREP_AT:
                    for n in range(2 * (t - PREP_AT), 2 * (t - PREP_AT) + 2):
                        prep_out_of_psum(n)
            act.wait_ge(ln2_stats, 1)
            act.activation(sd[:, 0:NCUT], meanvar[:, 0:NCUT, 1], ACT.Sqrt, bias=eps_col[:, 0:1]).then_inc(ln2_sd, 1)

            def layernorm(n):
                for half, (t0, t1) in enumerate(halves(n)):
                    act.wait_ge(ln_stats, 2 * n + half + (n == 0))
                    act.activation(sd[:, t0:t1], meanvar[:, t0:t1, 1], ACT.Sqrt, bias=eps_col[:, 0:1])\
                       .then_inc(ln_sd, 1)
                    for t in range(t0, t1):
                        act.wait_ge(xT_mm, NT * n + t + 1)
                        act.activation(xT[:, :, P * t:P * t + P],
                                       bank(t % 3)[:, 0:KC * P].rearrange("p (k n) -> p k n", k=KC),
                                       ACT.Copy).then_inc(xT_ready, 1)

            for n in range(2 * (NCUT - PREP_AT), len(PREP)):
                prep_out_of_psum(n)
            layernorm(0)

            def sd_of(v):
                n = BLOCKS[QK[v][2]][1]
                act.wait_ge(var_mm, v + 1)
                act.activation(sq[:, v % QKR, 0:n], bank(QKR + v % QKR)[:, 0:n], ACT.Sqrt, bias=eps_col[:, 0:1])\
                   .then_inc(sd_ready, 1)

            def key_affine(v):
                _, c, blk = QK[v]
                c0, n = BLOCKS[blk]
                act.wait_ge(qk_norm, v + 1)
                part = kn[:, c].rearrange("p b n -> p n b")[:, c0 // B:(c0 + n) // B, :]
                act.activation(part, part, ACT.Identity, scale=k_w[:, 0:1], bias=k_b[:, 0:1]).then_inc(khead_ready, 1)

            for v, (_, _, blk) in enumerate(QK):
                n = BLOCKS[blk][1]
                act.wait_ge(qk_mm, v + 1)
                if v >= QKR:
                    act.wait_ge(qk_norm, v - QKR + 1)
                act.activation(raw[:, v % QKR, 0:n], bank(v % QKR)[:, 0:n], ACT.Copy).then_inc(sq_ready, 1)
                act.activation(sq[:, v % QKR, 0:n], bank(v % QKR)[:, 0:n], ACT.Square).then_inc(sq_ready, 1)
                if v >= 2:
                    sd_of(v - 2)
                if v - 3 >= len(QK) // 2:
                    key_affine(v - 3)
            sd_of(len(QK) - 2)
            sd_of(len(QK) - 1)
            for v in range(len(QK) - 3, len(QK)):
                key_affine(v)

            act.wait_ge(at0_zeroed, 1)

            def queries(i, s, k):
                act.wait_ge(s_mm, i)
                for half in range(2):
                    r = slice(64 * half, 64 * half + 64)
                    act.activation(q_ring[r, s, :, :, QP * half:QP * half + S],
                                   qn[r, :, bass.ds(i * 2, 2), :], ACT.Identity,
                                   scale=q_w[r, 0:1], bias=q_b[r, 0:1]).then_inc(q_ready, 1)

            def values(i, s, k):
                act.wait_ge(v_mm, i + 2)
                act.wait_ge(c_mm, i)
                for half in range(2):
                    for j in range(2):
                        cols = lambda v: v.rearrange("p (g two d) -> p g two d", two=2, d=HD0)[:, :, half, :]
                        act.activation(cols(v_ring[64 * half:64 * half + 64, s, j, :]),
                                       cols(bank(6)[64 * j:64 * j + 64, 0:ED]), ACT.Copy).then_inc(v_ready, 1)

            def exps(i, s, k):
                act.wait_ge(s_taken, i + 2)
                pv = p_ring[:, s, :, 0:S]
                act.activation(pv, pv, ACT.Exp, scale=SCALE0).then_inc(p_exp, 1)

            def back(i, s, k):
                act.wait_ge(t_mm, i + 2)
                act.wait_ge(c_mm, i)
                act.activation(pT[s], bank(4, 2).rearrange("p (g n) -> p g n", n=QP)[:, :, 0:S], ACT.Copy)\
                   .then_inc(pT_ready, 1)

            pipelined(act, PAIRS, (back, 3), (queries, 0), (values, 1), (exps, 1))
            act.wait_ge(reshuffled, 16 * H0)
            for dst, src in to_tiles(0):
                act.activation(dst, src, ACT.Copy).then_inc(tile_order, 1)
            layernorm(1)
            act.wait_ge(top_ready, 1)
            act.activation(logits[:, :, 0:E0], logits[:, :, 0:E0], ACT.Exp).then_inc(gate_ready, 1)
            for n in range(3):
                act.wait_ge(ohT_mm, n + 1)
                m = min(4, NT - 4 * n)
                act.activation(onehotT[0:E0, 4 * n:4 * n + m, :].rearrange("p t n -> p (t n)"),
                               bank(5 + n)[0:E0, 0:P * m], ACT.Copy).then_inc(ohT_ready, 1)

            act.wait_ge(slots_ready, 1)

            def xfront(i, s, k):
                act.wait_ge(rows_mm[0], i + 2)
                act.activation(rowsT[0][:, s], bank(0)[:, 0:KC * P].rearrange("p (k n) -> p k n", k=KC), ACT.Copy)\
                   .then_inc(rowsT_ready[0], 1)

            def xback(i, s, k):
                e = act.value_load(tile_e[0:1, 0, bass.ds(i, 1)], min_val=0, max_val=E0 - 1)
                act.wait_ge(hidT_mm[0], i + 2)
                act.wait_ge(y_mm[0], i)
                b1f = b1T[:, :, :].rearrange("p e c -> p (e c)")
                for c in range(FF0 // P):
                    act.activation(hidT[0][:, s, c, :], bank(4, 2)[:, P * c:P * c + P], ACT.Gelu,
                                   bias=b1f[:, bass.ds(e * (FF0 // P) + c, 1)]).then_inc(hidT_ready[0], 1)

            pipelined(act, NT0, (xfront, 0), (xback, 2))
            layernorm(2)

            act.wait_ge(at1_zeroed, 1)
            v = 0
            for which in range(2):
                for c0, n in BLOCKS:
                    act.wait_ge(lat_mm, v + 1)
                    if which == 0:
                        dst = lat_u.rearrange("p b n -> p n b")[:, c0 // B:(c0 + n) // B, :]
                    else:
                        dst = lat_k.rearrange("p (b n) -> p n b", n=S)[:, c0 // B:(c0 + n) // B, :]
                    act.activation(dst, bank(v % 2)[:, 0:n].rearrange("p (n b) -> p n b", b=B), ACT.Identity,
                                   bias=(bias_k if which else bias_u)[:, 0:1]).then_inc(lat_ready, 1)
                    v += 1
            for v in range(12):
                c0, n = BLOCKS[v % 3]
                act.wait_ge(keys_mm, v + 1)
                act.activation(keys[:, v // 3, c0:c0 + n], bank(2 + v % 2)[:, 0:n], ACT.Copy).then_inc(keys_ready, 1)

            def queries1(i, s, k):
                act.wait_ge(s1_mm, i)
                for half in range(2):
                    r = slice(64 * half, 64 * half + 64)
                    act.activation(u_ring[r, s, :, QP * half:QP * half + QP],
                                   lat_u[r, bass.ds(i * 2, 2), :], ACT.Copy).then_inc(u_ready, 1)

            def values1(i, s, k):
                act.wait_ge(lv_mm, i + 2)
                act.wait_ge(c1_mm, i)
                for half in range(2):
                    for j in range(2):
                        act.activation(lat_v[64 * half:64 * half + 64, s, j, DC * half:DC * half + DC],
                                       bank(6)[64 * j:64 * j + 64, 0:DC], ACT.Copy).then_inc(lv_ready, 1)

            def exps1(i, s, k):
                act.wait_ge(s1_taken, i + 2)
                pv = p1_ring[:, s, :, 0:S]
                act.activation(pv, pv, ACT.Exp, scale=SCALE1).then_inc(p1_exp, 1)

            def back1(i, s, k):
                act.wait_ge(t1_mm, i + 2)
                act.wait_ge(c1_mm, i)
                act.activation(pT1[s], bank(4).rearrange("p (g r n) -> p g r n", g=4, n=QP)[:, :, :, 0:S], ACT.Copy)\
                   .then_inc(pT1_ready, 1)

            pipelined(act, PAIRS, (back1, 3), (queries1, 0), (values1, 1), (exps1, 1))
            layernorm(3)
            act.wait_ge(top_ready, 2)
            act.activation(weight[:], top[:], ACT.Sigmoid).then_inc(gate_ready, 1)

            for v in range(12):
                act.wait_ge(w_mm, v + 1)
                if v < 8:
                    dst = (gT if v < 4 else upT)[:, v % 4 // 2, 512 * (v % 2):512 * (v % 2) + 512]
                else:
                    dst = dT[:, 2 * (v - 8):2 * (v - 8) + 2, :].rearrange("p c e -> p (c e)")
                act.activation(dst, bank(v % 2), ACT.Copy).then_inc(w_ready, 1)
            def silus(bl):
                n = BLOCKS[bl][1]
                for v in range(bl * (SF // P), (bl + 1) * (SF // P)):
                    act.wait_ge(shg_mm, v + 1)
                    if v >= 2:
                        act.wait_ge(sT_ready, v - 1)
                    act.activation(sg[:, v % 2, 0:n], bank(v % 2)[:, 0:n], ACT.Silu).then_inc(silu_ready, 1)

            silus(0)

            def xfront1(i, s, k):
                act.wait_ge(rows_mm[1], i + 2)
                act.activation(rowsT[1][:, s], bank(0)[:, 0:KC * P].rearrange("p (k n) -> p k n", k=KC), ACT.Copy)\
                   .then_inc(rowsT_ready[1], 1)

            def xsilu1(i, s, k):
                act.wait_ge(hid_mm[1], i + 1)
                act.wait_ge(hid_ready[1], i)
                act.activation(hid[1][:, s, 0:FF1], bank(2 + s)[:, 0:FF1], ACT.Silu).then_inc(silu1, 1)

            def xback1(i, s, k):
                act.wait_ge(hidT_mm[1], i + 2)
                act.wait_ge(y_mm[1], i)
                act.activation(hidT[1][:, s, 0:2, :].rearrange("p c n -> p (c n)"), bank(4)[:, 0:2 * P], ACT.Copy)\
                   .then_inc(hidT_ready[1], 1)

            pipelined(act, NT1, (xfront1, 0), (xback1, 2), (xsilu1, 1))
            silus(1)
            silus(2)

        @block.vector
        def _(dve):
            ch = Chain(dve, sem("dve_chain"))

            def wide(v, n):
                return v.rearrange("p (g o) -> p g o", o=1).broadcast_to((v.shape[0], v.shape[1], n))

            def over(v, n):
                return v.rearrange("p (o g) -> p o g", o=1).broadcast_to((v.shape[0], n, v.shape[1]))

            for credit in (hid_ready[1], s_taken, s1_taken):
                dve.sem_inc(credit, 1)
            dve.wait_ge(consts_ready, 1)
            blk = block16[:, :, :].rearrange("p j i -> p (j i)")
            ch.did(dve.tensor_scalar(average[:], blk, 1.0 / HD0, None, ALU.mult))
            ch.wait()
            dve.tensor_tensor(out=centre[:], in0=ident[:], in1=average[:], op=ALU.subtract).then_inc(averages_ready, 1)

            def patch_of(t):
                return x_a[:, :, :, PS * t:PS * t + PS] if t < G else x_b[:, :, :, PS * (t - G):PS * (t - G) + PS]

            def ln1(t0, t1):
                for t in range(t0, t1):
                    for c in range(C):
                        ch.did(dve.bn_stats(stats[:, t, c, :], patch_of(t)[:, c]))
                ch.wait()
                for t in range(t0, t1):
                    last = dve.bn_aggr(meanvar[:, t, :], stats[:, t, :, :].rearrange("p c s -> p (c s)"))
                last.then_inc(ln1_stats, 1)

            arrived(dve, "x_a")
            ln1(0, G)
            arrived(dve, "proj")
            for c in range(PC):
                last = dve.tensor_scalar(wg_proj[:, c, :], w_proj[:, c, :], ln1_g[:, c:c + 1], None, ALU.mult)
            last.then_inc(folded, 1)
            dve.wait_ge(ln1_sd, 1)
            ch.did(dve.reciprocal(rstd[:, 0:G], sd[:, 0:G]))
            ch.wait()

            def norm1(t):
                if t >= 2:
                    dve.wait_ge(patch_mm, t - 1)
                dve.tensor_scalar(patch[:, t % 2].rearrange("p (c i w) -> p c i w", c=C, i=PS), patch_of(t),
                                  meanvar[:, t, 0:1], rstd[:, t:t + 1], ALU.subtract, ALU.mult).then_inc(patch_ready, 1)

            def take_z(t):
                dve.wait_ge(z_mm, t + 1)
                if t == 0:
                    dve.wait_ge(prep_out, 1)
                dve.tensor_tensor(out=xn[:, t, :], in0=bank(4 + t % 2)[:, 0:ED], in1=bias_z, op=ALU.add)\
                   .then_inc(z_taken, 1)

            norm1(0)
            for t in range(1, NCUT):
                if t == G:
                    arrived(dve, "x_b")
                    ln1(G, NCUT)
                    dve.wait_ge(ln1_sd, 2)
                    ch.did(dve.reciprocal(rstd[:, G:NCUT], sd[:, G:NCUT]))
                    ch.wait()
                norm1(t)
                take_z(t - 1)
            take_z(NCUT - 1)
            dve.wait_ge(z_taken, NCUT)
            for t in range(NCUT):
                ch.did(dve.bn_stats(stats[:, t, 0, :], xn[:, t, :]))
            ch.wait()
            for t in range(NCUT):
                last = dve.bn_aggr(meanvar[:, t, :], stats[:, t, 0, :])
            last.then_inc(ln2_stats, 1)

            arrived(dve, "attn0")
            ch.did(dve.tensor_reduce(sv_w[0:H0, :], sparse_v[0:H0], axis=AX.X, op=ALU.add))
            ch.did(dve.tensor_reduce(so_w[0:H0, :], sparse_o[0:H0].rearrange("p k d -> p d k"), axis=AX.X, op=ALU.add))
            ch.wait()
            for dst, src in ((tiled_v, sv_w), (tiled_o, so_w)):
                last = dve.tensor_copy(dst[0:H0, :].rearrange("p (r d) -> p r d", d=HD0), over(src[0:H0, :], 8))
            last.then_inc(tiled_ready, 1)

            dve.wait_ge(ln2_sd, 1)
            ch.did(dve.reciprocal(rstd[:, 0:NCUT], sd[:, 0:NCUT]))
            ch.wait()
            for t in range(NCUT):
                ch.did(dve.tensor_scalar(xn[:, t, :], xn[:, t, :], meanvar[:, t, 0:1], rstd[:, t:t + 1],
                                         ALU.subtract, ALU.mult))
            ch.wait()
            dve.wait_ge(prep_mm, 1 + PREP.index("mix") + 1)
            dve.scalar_tensor_tensor(out=blockM, in0=bank(7 - PREP.index("mix") % 2)[:, 0:P], scalar=1.0 / (P * P),
                                     in1=blk, op0=ALU.mult, op1=ALU.mult).then_inc(mixed, 1)
            dve.wait_ge(pos_ready, 2)
            for t in range(NCUT):
                ch.did(dve.tensor_tensor(out=xn[:, t, :], in0=xn[:, t, :], in1=ln2_g, op=ALU.mult))
            ch.wait()
            for t in range(NCUT):
                last = dve.tensor_tensor(out=h[:, t, :], in0=h[:, t, :], in1=xn[:, t, :], op=ALU.add)
                ch.did(last)
            ch.wait()
            dve.sem_inc(embedded, 1)

            arrived(dve, "small")
            dve.tensor_tensor(out=k_of[:], in0=block16[:, 0:4, 0], in1=block16[:, 4:8, 0], op=ALU.add)\
               .then_inc(khead_ready, 1)

            def layernorm(n, bring=None):
                for half, (t0, t1) in enumerate(halves(n)):
                    if bring:
                        bring(t0, t1)
                    for t in range(t0, t1):
                        ch.did(dve.bn_stats(stats[:, t, 0, :], h[:, t, :]))
                    ch.wait()
                    for t in range(t0, t1):
                        last = dve.bn_aggr(meanvar[:, t, :], stats[:, t, 0, :])
                    last.then_inc(ln_stats, 1)
                    dve.wait_ge(ln_sd, 2 * n + half + (n == 0))
                    ch.did(dve.reciprocal(rstd[:, t0:t1], sd[:, t0:t1]))
                    ch.wait()
                    for t in range(t0, t1):
                        dve.tensor_scalar(xn[:, t, :], h[:, t, :], meanvar[:, t, 0:1], rstd[:, t:t + 1],
                                          ALU.subtract, ALU.mult).then_inc(xn_ready, 1)

            layernorm(0)
            for v, (which, c, bl) in enumerate(QK):
                c0, n = BLOCKS[bl]
                dve.wait_ge(sd_ready, v + 1)
                ch.did(dve.reciprocal(sq[:, v % QKR, 0:n], sq[:, v % QKR, 0:n]))
                ch.wait()
                dst = (kn if which else qn)[:, c].rearrange("p b n -> p n b")[:, c0 // B:(c0 + n) // B, :]
                if v == 0:
                    dve.wait_ge(embedded, 1)
                r3 = raw[:, v % QKR, 0:n].rearrange("p (n b) -> p n b", b=B)
                s3 = sq[:, v % QKR, 0:n].rearrange("p (n b) -> p n b", b=B)
                if which:
                    dve.tensor_tensor(out=dst, in0=r3, in1=s3, op=ALU.mult).then_inc(qk_norm, 1)
                    continue
                seq = qn[:, c].rearrange("p b n -> p n b")
                parts = []
                n0 = c0 // B
                for t in range(n0 // 4, (n0 + n // B) // 4):
                    q0 = 4 * t - n0
                    if t < G:
                        parts.append((seq[:, 1 + t:1 + t + 3 * G + 1:G, :], q0, 4))
                    else:
                        for j1 in range(2):
                            at = 1 + 4 * G + G // 2 * j1 + t - G
                            parts.append((seq[:, at:at + G + 1:G, :], q0 + 2 * j1, 2))
                if n0 + n // B == S:
                    parts.append((seq[:, 0:1, :], S - 1 - n0, 1))
                for q, (d, q0, m) in enumerate(parts):
                    ins = dve.tensor_tensor(out=d, in0=r3[:, q0:q0 + m, :], in1=s3[:, q0:q0 + m, :], op=ALU.mult)
                ins.then_inc(qk_norm, 1)

            chf = Chain(dve, sem("dve_chain_max0"), 1)
            chs = Chain(dve, sem("dve_chain_sum0"), 1)
            dve.wait_ge(at0_zeroed, 1)

            def fmax(i, s, k):
                chf.at(i)
                dve.wait_ge(s_mm, i + 2)
                sc = bank(2 * s, 2).rearrange("p (j n) -> p j n", j=2)[:, :, 0:8 * S]\
                    .rearrange("p j (g n) -> p j g n", n=S)
                chf.did(dve.tensor_reduce(mx[:, s, :], sc, axis=AX.X, op=ALU.max))
                chf.wait()
                dve.wait_ge(t_mm, i)
                dve.tensor_tensor(out=p_ring[:, s, :, 0:S].rearrange("p (j g) n -> p j g n", j=2), in0=sc,
                                  in1=mx[:, s, :].rearrange("p (j g o) -> p j g o", j=2, o=1)
                                  .broadcast_to((P, 2, 8, S)), op=ALU.subtract).then_inc(s_taken, 1)

            def fctx(i, s, k):
                dve.wait_ge(c_mm, i + 2)
                dve.tensor_copy(ctxT.rearrange("p c (n b) -> p c b n", b=B)[:, :, bass.ds(i * 2, 2), :],
                                bank(7)[:, 0:4 * S].rearrange("p (c j n) -> p c j n", c=2, j=2)).then_inc(c_taken, 1)

            def fsum(i, s, k):
                chs.at(i)
                dve.wait_ge(p_exp, i + 1)
                chs.did(dve.tensor_reduce(sm[:, s, :], p_ring[:, s, :, 0:S], axis=AX.X, op=ALU.add))
                chs.wait()
                dve.reciprocal(sm[:, s, :], sm[:, s, :]).then_inc(p_sum, 1)

            pipelined(dve, PAIRS, (fmax, 0), (fctx, 2), (fsum, 0))

            def add_heads(made, taken):
                def bring(t0, t1):
                    for t in range(t0, t1):
                        dve.wait_ge(made, t + 1)
                        m = P if t < NT - 1 else B
                        dve.tensor_tensor(out=h[0:m, t, :], in0=h[0:m, t, :], in1=bank(4 + t % 4)[0:m, 0:ED],
                                          op=ALU.add).then_inc(o_taken, 1)
                    dve.wait_ge(o_taken, taken + t1)
                return bring

            dve.wait_ge(reshuffled, 16 * H0)
            for dst, src in to_tiles(1):
                dve.tensor_copy(dst, src).then_inc(tile_order, 1)
            layernorm(1, add_heads(o_mm, 0))

            def route(l):
                E, nt = e_of[l], nt_of[l]
                lg, mk, oh = logits[:, :, 0:E], mask[:, :, 0:E], onehot[:, :, 0:E]
                dve.wait_ge(logits_mm, l + 1)
                ch.did(dve.tensor_copy(lg, bank(3)[:, 0:NT * E].rearrange("p (t e) -> p t e", e=E)))
                ch.wait()
                ch.did(dve.tensor_reduce(top[:], lg, axis=AX.X, op=ALU.max))
                ch.wait()
                if l:
                    dve.sem_inc(top_ready, 1)
                ch.did(dve.tensor_tensor(out=mk, in0=lg, in1=wide(top[:], E), op=ALU.is_equal))
                ch.wait()
                if l == 0:
                    dve.tensor_tensor(out=lg, in0=lg, in1=wide(top[:], E), op=ALU.subtract).then_inc(top_ready, 1)
                ch.did(dve.scalar_tensor_tensor(out=mk, in0=mk, scalar=-64.0, in1=over(iota_e[:, 0:E], NT),
                                                op0=ALU.mult, op1=ALU.add))
                ch.wait()
                ch.did(dve.tensor_reduce(first[:], mk, axis=AX.X, op=ALU.min))
                ch.wait()
                ch.did(dve.tensor_tensor(out=oh, in0=mk, in1=wide(first[:], E), op=ALU.is_equal))
                ch.wait()
                ch.did(dve.memset(onehot[32:64, NT - 1, 0:E], 0.0))
                ch.did(dve.memset(onehot[64:128, NT - 1, 0:E], 0.0))
                ch.wait()
                if l == 0:
                    ch.did(dve.tensor_copy(onehot_f[:], oh))
                    ch.wait()
                dve.sem_inc(onehot_ready, 1)
                dve.wait_ge(gate_ready, l + 1)
                if l == 0:
                    ch.did(dve.tensor_reduce(weight[:], lg, axis=AX.X, op=ALU.add))
                    ch.wait()
                    ch.did(dve.reciprocal(weight[:], weight[:]))
                else:
                    for t in range(NT):
                        ch.did(dve.tensor_scalar(xn[:, t, :], xn[:, t, :], weight[:, t:t + 1], None, ALU.mult))
                ch.wait()
                dve.wait_ge(rank_mm, l + 1)
                rank = bank(5)[:, 0:NT * E].rearrange("p (t e) -> p t e", e=E)
                over_e, tl, bs, en = counts_over[:, 0:E, :], tiles_e[:, 0:E], base_e[:, 0:E], end_e[:, 0:E]
                ch.did(dve.tensor_tensor(out=over_e, in0=wide(bank(6)[:, 0:E], NT), in1=over(thresholds[:], E),
                                         op=ALU.is_gt))
                ch.wait()
                ch.did(dve.tensor_reduce(tl, over_e, axis=AX.X, op=ALU.add))
                ch.wait()
                ch.did(dve.tensor_tensor(out=base_tmp[:, 0:E, 0:E], in0=lower_e[:, 0:E, 0:E], in1=over(tl, E),
                                         op=ALU.mult))
                ch.wait()
                ch.did(dve.tensor_reduce(bs, base_tmp[:, 0:E, 0:E], axis=AX.X, op=ALU.add))
                ch.wait()
                ch.did(dve.tensor_tensor(out=en, in0=bs, in1=tl, op=ALU.add))
                ch.did(dve.scalar_tensor_tensor(out=mk, in0=over(bs, NT), scalar=float(P), in1=rank,
                                                op0=ALU.mult, op1=ALU.add))
                ch.wait()
                ch.did(dve.tensor_tensor(out=mk, in0=mk, in1=oh, op=ALU.mult))
                ch.did(dve.tensor_tensor(out=tile_cmp[0:1, 0:nt, 0:E - 1], in0=wide(iota_e[0:1, 0:nt], E - 1),
                                         in1=over(end_e[0:1, 0:E - 1], nt), op=ALU.is_ge))
                ch.wait()
                ch.did(dve.tensor_reduce(slot_f[:], mk, axis=AX.X, op=ALU.add))
                ch.did(dve.tensor_reduce(tile_e_f[0:1, 0:nt], tile_cmp[0:1, 0:nt, 0:E - 1], axis=AX.X, op=ALU.add))
                ch.wait()
                ch.did(dve.tensor_copy(slot[:, l, :], slot_f[:]))
                ch.did(dve.tensor_copy(tile_e[0:1, l, 0:nt], tile_e_f[0:1, 0:nt]))
                ch.wait()
                dve.sem_inc(slots_ready, 1)

            route(0)

            def take_hid0(i, s, k):
                dve.wait_ge(hidT_mm[0], i)
                for half in range(2):
                    dve.wait_ge(hid_mm[0], i * 2 + half + 1)
                    dve.tensor_copy(hid[0][:, s, 512 * half:512 * half + 512], bank(2 + half)).then_inc(hid_ready[0], 1)

            def take_y(l):
                def body(i, s, k):
                    dve.wait_ge(y_mm[l], i + 2)
                    dve.wait_ge(y_stored[l][s], k * 16)
                    dve.tensor_copy(rows_out[l][:, s, :], bank(6)[:, 0:ED]).then_inc(y_ready[l], 1)
                return body

            pipelined(dve, NT0, (take_hid0, 1), (take_y(0), 2))
            def add_gated(src, t):
                return dve.scalar_tensor_tensor(out=h[:, t, :], in0=src, scalar=weight[:, t:t + 1],
                                                in1=h[:, t, :], op0=ALU.mult, op1=ALU.add)

            for t in range(NT):
                dve.wait_ge(bias2_mm, t + 1)
                add_gated(bank(4 + t % 4)[:, 0:ED], t).then_inc(o_taken, 1)
            dve.wait_ge(o_taken, 2 * NT)

            def add_experts(t0, t1):
                for t in range(t0, t1):
                    dve.wait_ge(gathered[t], 16)
                    ch.did(add_gated(xn[:, t, :], t))
                ch.wait()

            layernorm(2, add_experts)

            dve.wait_ge(xn_ready, 3 * NT)
            ch.did(dve.tensor_tensor(out=h[:], in0=h[:], in1=over(bias_o[:], NT), op=ALU.add))
            ch.wait()
            chf1 = Chain(dve, sem("dve_chain_max1"), 1)
            chs1 = Chain(dve, sem("dve_chain_sum1"), 1)
            dve.wait_ge(at1_zeroed, 1)

            def fmax1(i, s, k):
                chf1.at(i)
                dve.wait_ge(s1_mm, i + 2)
                sc = bank(s)[:, 0:8 * S].rearrange("p (g n) -> p g n", n=S)
                chf1.did(dve.tensor_reduce(mx1[:, s, :], sc, axis=AX.X, op=ALU.max))
                chf1.wait()
                dve.wait_ge(t1_mm, i)
                dve.tensor_tensor(out=p1_ring[:, s, :, 0:S], in0=sc, in1=wide(mx1[:, s, :], S),
                                  op=ALU.subtract).then_inc(s1_taken, 1)

            def fctx1(i, s, k):
                dve.wait_ge(c1_mm, i + 2)
                for j in range(2):
                    ins = dve.tensor_copy(
                        ctx1T.rearrange("p r (n b) -> p r b n", b=B)[:, :, bass.ds(i * 2 + j, 1), 0:S]
                        .rearrange("p r o n -> p r (o n)"),
                        bank(7)[:, 2 * S * j:2 * S * j + 2 * S].rearrange("p (r n) -> p r n", r=2))
                    ins.then_inc(c1_taken, 1)

            def fsum1(i, s, k):
                chs1.at(i)
                dve.wait_ge(p1_exp, i + 1)
                chs1.did(dve.tensor_reduce(sm1[:, s, :], p1_ring[:, s, :, 0:S], axis=AX.X, op=ALU.add))
                chs1.wait()
                dve.reciprocal(sm1[:, s, :], sm1[:, s, :]).then_inc(p1_sum, 1)

            pipelined(dve, PAIRS, (fmax1, 0), (fctx1, 2), (fsum1, 0))
            layernorm(3, add_heads(o1_mm, 2 * NT))
            dve.wait_ge(xT_mm, 4 * NT)
            route(1)

            def shared_hidden(bl):
                n = BLOCKS[bl][1]
                if bl:
                    dve.wait_ge(sho_mm, 4 * bl)
                for f in range(SF // P):
                    v = bl * (SF // P) + f
                    dve.wait_ge(silu_ready, v + 1)
                    dve.wait_ge(shu_mm, v + 1)
                    dve.tensor_tensor(out=sT[:, f, 0:n], in0=bank(2 + v % 2)[:, 0:n], in1=sg[:, v % 2, 0:n],
                                      op=ALU.mult).then_inc(sT_ready, 1)

            def shared_out(bl):
                c0, n = BLOCKS[bl]
                for t in range(c0 // P, (c0 + n + P - 1) // P):
                    m = min(P, TOK - t * P)
                    dve.wait_ge(sho_mm, t + 1)
                    dve.tensor_tensor(out=h[0:m, t, :], in0=h[0:m, t, :], in1=bank(4 + t % 4)[0:m, 0:ED], op=ALU.add)\
                       .then_inc(sho_taken, 1)

            shared_hidden(0)
            shared_out(0)

            def take_hid1(i, s, k):
                dve.wait_ge(hidT_mm[1], i)
                dve.wait_ge(silu1, i + 1)
                dve.tensor_tensor(out=hid[1][:, s, FF1:2 * FF1], in0=bank(2 + s)[:, FF1:2 * FF1], in1=hid[1][:, s, 0:FF1],
                                  op=ALU.mult).then_inc(hid_ready[1], 1)

            pipelined(dve, NT1, (take_hid1, 1), (take_y(1), 3))
            shared_hidden(1)
            dve.wait_ge(sho_taken, 4)
            for t in range(NT):
                m = P if t < NT - 1 else B
                dve.wait_ge(gathered[t], 2 * 16)
                dve.tensor_tensor(out=h[0:m, t, :], in0=h[0:m, t, :], in1=xn[0:m, t, :], op=ALU.add)\
                   .then_inc(experts_done, 1)
            dve.wait_ge(experts_done, NT)
            shared_out(1)
            shared_hidden(2)
            shared_out(2)

        @block.tensor
        def _(pe):
            def product(dst, terms):
                for n, (l, r) in enumerate(terms):
                    last = pe.matmul(dst, l, r, start=n == 0, stop=n == len(terms) - 1)
                return last

            for ahead in (v_mm, s_mm, c_mm, t_mm, lv_mm, s1_mm, c1_mm, t1_mm, *rows_mm, *hidT_mm, *y_mm):
                pe.sem_inc(ahead, 1)

            pe.wait_ge(consts_ready, 1)
            pe.wait_ge(prep_zeroed, 1)
            arrived(pe, "proj")
            product(bank(6)[:, 0:ED], [(ln1_b[:, c:c + 1].broadcast_to((P, P)), w_proj[:, c, :]) for c in range(PC)]
                    + [(ones_row[0:1, :], b_proj[0:1, :])]).then_inc(prep_mm, 1)
            def turned(dst, src, ident_n=P):
                return pe.transpose(dst, src, ident[0:ident_n, 0:ident_n])

            def prep_step(n):
                what = PREP[n]
                if n == 0:
                    arrived(pe, "attn0")
                    pe.wait_ge(averages_ready, 1)
                elif what == "uk0":
                    arrived(pe, "attn1")
                elif what == "router":
                    arrived(pe, "small")
                if n >= 2:
                    if n - 2 == MIX:
                        pe.wait_ge(mixed, 1)
                    pe.wait_ge(prep_out, prep_done(n - 2))
                b = bank(7 - n % 2)
                if what in ("q", "k"):
                    w = wq_raw if what == "q" else wk_raw
                    for m in range(KC):
                        for oc in range(KC):
                            last = pe.matmul(b[:, ED * m + P * oc:ED * m + P * oc + P], w[:, oc, P * m:P * m + P],
                                             centre[:], start=True, stop=True)
                elif what in ("v", "woT"):
                    w = wv_raw if what == "v" else wo_raw
                    for m in range(KC):
                        for oc in range(KC):
                            last = turned(b[:, ED * m + P * oc:ED * m + P * oc + P], w[:, oc, P * m:P * m + P])
                elif what == "router":
                    for m in range(KC):
                        last = turned(b[:, E1 * m:E1 * m + E1], router1[:, P * m:P * m + P], E1)
                elif what == "b1":
                    last = turned(b[:, 0:E0 * FF0 // P], b1_rows[:], E0 * FF0 // P)
                elif what in ("uk0", "uk1"):
                    for m in range(4):
                        hd = m + 4 * (what == "uk1")
                        last = turned(b[:, P * m:P * m + P], uk_raw[:, DK * hd:DK * hd + DK])
                elif what in ("uq", "uv"):
                    w = uq_raw if what == "uq" else uv_raw
                    for hd in range(H1):
                        last = turned(b[:, (DC + 1) * hd:(DC + 1) * (hd + 1)], w[0:DC + 1, DK * hd:DK * hd + DK],
                                      DC + 1)
                elif what == "keyT":
                    for hd in range(H1):
                        o = (DC + 1) * hd
                        pe.matmul(b[:, o:o + DC + 1], ukT[:, hd, :], uqT[:, hd, :], start=True, stop=False)
                        last = pe.matmul(b[:, o:o + DC + 1], qr_raw[0:DC + 1, hd, :], ident[0:DC + 1, 0:DC + 1],
                                         start=False, stop=True)
                elif what == "valO":
                    for hd in range(H1):
                        r, half = 32 * (hd // 2), hd % 2
                        last = pe.matmul(b[r:r + 32, ED * half:ED * half + ED], uvT[:, hd, 0:DC], wo1_raw[:, hd, :],
                                         start=True, stop=True)
                elif what == "bias_o":
                    last = product(b[:, 0:ED], [(uvT[:, hd, DC:DC + 1].broadcast_to((P, P)), wo1_raw[:, hd, :])
                                                for hd in range(H1)] + [(ones_row[0:1, :], b_o[0:1, :])])
                elif what == "mix":
                    pe.wait_ge(tiled_ready, 1)
                    last = pe.matmul(b[:, 0:P], tiled_o[0:H0, :], tiled_v[0:H0, :], start=True, stop=True)
                elif what == "woe":
                    pe.wait_ge(mixed, 1)
                    for m in range(KC):
                        last = pe.matmul(b[:, ED * m:ED * m + ED], blockM, woT[:, m, :], start=True, stop=True)
                last.then_inc(prep_mm, 1)

            pe.wait_ge(folded, 1)
            for t in range(NCUT + 1):
                if t < NCUT:
                    pe.wait_ge(patch_ready, t + 1)
                    if t >= 2:
                        pe.wait_ge(patchT_ready, t - 1)
                    for c in range(PC):
                        last = pe.transpose(bank(2 * (t % 2), 2)[:, P * c:P * c + P], patch[:, t % 2, P * c:P * c + P],
                                            ident[:])
                    last.then_inc(patch_mm, 1)
                if t:
                    u = t - 1
                    pe.wait_ge(patchT_ready, u + 1)
                    if u >= 2:
                        pe.wait_ge(z_taken, u - 1)
                    product(bank(4 + u % 2)[:, 0:ED], [(patchT[:, u % 2, c, :], wg_proj[:, c, :]) for c in range(PC)])\
                        .then_inc(z_mm, 1)
                if t >= PREP_AT:
                    for n in range(2 * (t - PREP_AT), 2 * (t - PREP_AT) + 2):
                        prep_step(n)
            for n in range(2 * (NCUT + 1 - PREP_AT), len(PREP)):
                prep_step(n)

            def layernorm(n, router=None):
                def route_tile(t):
                    if router is not None:
                        pe.wait_ge(xT_ready, NT * n + t + 1)
                        E = router.shape[2]
                        last = product(bank(3)[:, E * t:E * t + E], [(xT[:, k, P * t:P * t + P], router[:, k, :])
                                                                     for k in range(KC)])
                        if t == NT - 1:
                            last.then_inc(logits_mm, 1)

                for t in range(NT):
                    pe.wait_ge(xn_ready, NT * n + t + 1)
                    if t >= 3:
                        pe.wait_ge(xT_ready, NT * n + t - 2)
                    for k in range(KC):
                        last = turned(bank(t % 3)[:, P * k:P * k + P], xn[:, t, P * k:P * k + P])
                    last.then_inc(xT_mm, 1)
                    if t >= 2:
                        route_tile(t - 2)
                route_tile(NT - 2)
                route_tile(NT - 1)
                pe.wait_ge(xT_ready, NT * (n + 1))

            layernorm(0)
            pe.wait_ge(prep_out, prep_done(len(PREP) - 1))
            for v in range(len(QK) + 1):
                if v < len(QK):
                    which, c, bl = QK[v]
                    c0, n = BLOCKS[bl]
                    if v >= QKR:
                        pe.wait_ge(sq_ready, 2 * (v - QKR + 1))
                    w = kT if which else qT
                    product(bank(v % QKR)[:, 0:n], [(w[:, k, P * c:P * c + P], xT[:, k, c0:c0 + n]) for k in range(KC)])\
                        .then_inc(qk_mm, 1)
                if v:
                    u = v - 1
                    n = BLOCKS[QK[u][2]][1]
                    pe.wait_ge(sq_ready, 2 * (u + 1))
                    if u >= QKR:
                        pe.wait_ge(sd_ready, u - QKR + 1)
                    pe.matmul(bank(QKR + u % QKR)[:, 0:n], average[:], sq[:, u % QKR, 0:n], start=True, stop=True)\
                      .then_inc(var_mm, 1)
            pe.wait_ge(sd_ready, len(QK))

            def scores0(i, s, k):
                pe.wait_ge(xv_ready, i * 2 + 2)
                pe.wait_ge(v_ready, i * 4)
                product(bank(6)[:, 0:ED], [(xv[:, s, c, :], vT[:, c, :]) for c in range(KC)]).then_inc(v_mm, 1)
                pe.wait_ge(q_ready, i * 2 + 2)
                pe.wait_ge(k_ready, i * 2 + 2)
                pe.wait_ge(s_taken, i)
                for j in range(2):
                    for c in range(KC):
                        last = pe.matmul(bank(2 * s + j)[:, 4 * S * c:4 * S * c + 4 * S], q_ring[:, s, c, j, :],
                                         k_ring[s][:, c, j, :, :], start=True, stop=True)
                last.then_inc(s_mm, 1)

            def turn0(i, s, k):
                pe.wait_ge(p_norm, i + 1)
                pe.wait_ge(pT_ready, i)
                for g in range(8):
                    last = turned(bank(4, 2)[:, P * g:P * g + P], p_ring[:, s, 2 * g:2 * g + 2, :]
                                  .rearrange("p g n -> p (g n)"))
                last.then_inc(t_mm, 1)

            def context0(i, s, k):
                pe.wait_ge(pT_ready, i + 1)
                pe.wait_ge(v_ready, i * 4 + 4)
                pe.wait_ge(c_taken, i)
                for g in range(8):
                    j, c, pair = g // 4, g // 2 % 2, g % 2
                    for half in range(2):
                        r = 32 * (half * 2 + pair)
                        heads = c * 4 + half * 2 + pair
                        last = pe.matmul(bank(7)[r:r + 32, (2 * c + j) * S:(2 * c + j) * S + S],
                                         v_ring[:, s, j, 32 * heads:32 * heads + 32], pT[s][:, 2 * g + half, :],
                                         start=True, stop=True)
                last.then_inc(c_mm, 1)

            pipelined(pe, PAIRS, (turn0, 2), (scores0, 0), (context0, 2))
            pe.wait_ge(c_taken, PAIRS)

            def heads_out(tokens, w, done, before_):
                for t in range(NT):
                    m = P if t < NT - 1 else B
                    if t >= 4:
                        pe.wait_ge(o_taken, before_ + t - 3)
                    product(bank(4 + t % 4)[0:m, 0:ED], [(tokens(c, t), w[:, c, :]) for c in range(2)])\
                        .then_inc(done, 1)

            pe.wait_ge(tile_order, 8)
            heads_out(lambda c, t: ctxT[:, c, P * t:P * t + (P if t < NT - 1 else B)], woe, o_mm, 0)
            layernorm(1, gate_w0)

            def turn_shared_weights():
                arrived(pe, "shared")
                for v in range(12):
                    if v >= 2:
                        pe.wait_ge(w_ready, v - 1)
                    for q in range(4):
                        if v < 8:
                            f, m = 4 * (v % 2) + q, v % 4 // 2
                            src = (g_raw if v < 4 else up_raw)[:, f, P * m:P * m + P]
                        else:
                            f, m = 2 * (v - 8) + q // 2, q % 2
                            src = d_raw[:, m, P * f:P * f + P]
                        last = turned(bank(v % 2)[:, P * q:P * q + P], src)
                    last.then_inc(w_mm, 1)
                pe.wait_ge(w_ready, 12)

            def route(l):
                E = e_of[l]
                if l:
                    turn_shared_weights()
                pe.wait_ge(onehot_ready, l + 1)
                oh = onehot[:, :, 0:E]
                rank = bank(5)[:, 0:NT * E].rearrange("p (t e) -> p t e", e=E)
                pe.matmul(rank, before[:], oh, start=True, stop=False)
                for d in range(1, NT):
                    pe.matmul(rank[:, d:NT, :], ones16[:], oh[:, 0:NT - d, :], start=False, stop=d == NT - 1)
                for t in range(NT):
                    last = pe.matmul(bank(6)[:, 0:E], ones16[:], oh[:, t, :], start=t == 0, stop=t == NT - 1)
                last.then_inc(rank_mm, 1)

            route(0)
            pe.wait_ge(slots_ready, 1)
            for n in range(3):
                m = min(4, NT - 4 * n)
                for t in range(4 * n, 4 * n + m):
                    last = turned(bank(5 + n)[0:E0, P * (t - 4 * n):P * (t - 4 * n) + P], onehot_f[:, t, :])
                last.then_inc(ohT_mm, 1)
            pe.wait_ge(ohT_ready, 3)
            arrived(pe, "w1")
            arrived(pe, "w2")

            expert = {}

            def expert_of(l, use):
                def body(i, s, k):
                    expert[use] = pe.value_load(tile_e[0:1, l, bass.ds(i, 1)], min_val=0, max_val=e_of[l] - 1)
                return body

            def turn_rows(l):
                def body(i, s, k):
                    pe.wait_ge(rows_loaded[l][s], k * 16 + 16)
                    pe.wait_ge(rowsT_ready[l], i)
                    for c in range(KC):
                        last = turned(bank(0)[:, P * c:P * c + P], rows_in[l][:, s, P * c:P * c + P])
                    last.then_inc(rows_mm[l], 1)
                return body

            def hidden0(i, s, k):
                e = expert["hidden"]
                pe.wait_ge(rowsT_ready[0], i + 1)
                for half in range(2):
                    pe.wait_ge(hid_ready[0], i * 2 + half)
                    product(bank(2 + half), [(rowsT[0][:, s, c, :], w1[:, bass.ds(e * (KC * FF0) + FF0 * c + 512 * half, 512)])
                                             for c in range(KC)]).then_inc(hid_mm[0], 1)

            def turn_hidden0(i, s, k):
                pe.wait_ge(hid_ready[0], i * 2 + 2)
                pe.wait_ge(hidT_ready[0], i * 8)
                for c in range(FF0 // P):
                    last = turned(bank(4, 2)[:, P * c:P * c + P], hid[0][:, s, P * c:P * c + P])
                last.then_inc(hidT_mm[0], 1)

            def out0(i, s, k):
                e = expert["out"]
                pe.wait_ge(hidT_ready[0], i * 8 + 8)
                pe.wait_ge(y_ready[0], i)
                product(bank(6)[:, 0:ED], [(hidT[0][:, s, c, :], w2[:, bass.ds(e * (FF0 // P * ED) + ED * c, ED)])
                                           for c in range(FF0 // P)]).then_inc(y_mm[0], 1)

            pipelined(pe, NT0, (expert_of(0, "hidden"), 1), (expert_of(0, "out"), 2), (turn_rows(0), 0), (turn_hidden0, 2), (hidden0, 1), (out0, 2))
            pe.wait_ge(y_ready[0], NT0)
            for t in range(NT):
                pe.wait_ge(o_taken, NT + max(0, t - 3))
                pe.matmul(bank(4 + t % 4)[:, 0:ED], onehotT[0:E0, t, :], b2[:], start=True, stop=True).then_inc(bias2_mm, 1)

            layernorm(2)
            v = 0
            for w in (down_u, down_k):
                for c0, n in BLOCKS:
                    if v >= 2:
                        pe.wait_ge(lat_ready, v - 1)
                    product(bank(v % 2)[:, 0:n], [(w[:, k, :], xT[:, k, c0:c0 + n]) for k in range(KC)])\
                        .then_inc(lat_mm, 1)
                    v += 1
            pe.wait_ge(lat_ready, 6)
            for v in range(12):
                c0, n = BLOCKS[v % 3]
                if v >= 2:
                    pe.wait_ge(keys_ready, v - 1)
                pe.matmul(bank(2 + v % 2)[:, 0:n], keyT[:, v // 3, :], lat_k[:, c0:c0 + n], start=True, stop=True)\
                  .then_inc(keys_mm, 1)
            pe.wait_ge(keys_ready, 12)

            def scores1(i, s, k):
                pe.wait_ge(lk_ready, i + 1)
                pe.wait_ge(lv_ready, i * 4)
                turned(bank(6)[:, 0:P], lk_ring[:, s, :]).then_inc(lv_mm, 1)
                pe.wait_ge(u_ready, i * 2 + 2)
                pe.wait_ge(s1_taken, i)
                for j in range(2):
                    last = pe.matmul(bank(s)[:, 4 * S * j:4 * S * j + 4 * S], u_ring[:, s, j, :],
                                     keys[:, :, bass.ds(i * (2 * S) + S * j, S)], start=True, stop=True)
                last.then_inc(s1_mm, 1)

            def turn1(i, s, k):
                pe.wait_ge(p1_norm, i + 2)
                pe.wait_ge(pT1_ready, i)
                for g in range(4):
                    last = turned(bank(4)[:, P * g:P * g + P], p1_ring[:, s, 2 * g:2 * g + 2, :]
                                  .rearrange("p g n -> p (g n)"))
                last.then_inc(t1_mm, 1)

            def context1(i, s, k):
                pe.wait_ge(pT1_ready, i + 1)
                pe.wait_ge(lv_ready, i * 4 + 4)
                pe.wait_ge(c1_taken, i * 2)
                for g in range(4):
                    j, half = g // 2, g % 2
                    last = pe.matmul(bank(7)[64 * half:64 * half + 64, 2 * S * j:2 * S * j + 2 * S],
                                     lat_v[:, s, j, :], pT1[s][:, g, :, :].rearrange("p r n -> p (r n)"),
                                     start=True, stop=True)
                last.then_inc(c1_mm, 1)

            pipelined(pe, PAIRS, (turn1, 2), (scores1, 0), (context1, 2))
            pe.wait_ge(c1_taken, 2 * PAIRS)
            heads_out(lambda c, t: ctx1T[:, c, P * t:P * t + (P if t < NT - 1 else B)], valO, o1_mm, 2 * NT)
            layernorm(3, routerT1)
            route(1)

            def shared_block(bl):
                c0, n = BLOCKS[bl]
                for f in range(SF // P):
                    v = bl * (SF // P) + f
                    if v >= 2:
                        pe.wait_ge(silu_ready, v - 1)
                    product(bank(v % 2)[:, 0:n], [(gT[:, k, P * f:P * f + P], xT[:, k, c0:c0 + n]) for k in range(KC)])\
                        .then_inc(shg_mm, 1)
                    if v >= 2:
                        pe.wait_ge(sT_ready, v - 1)
                    product(bank(2 + v % 2)[:, 0:n], [(upT[:, k, P * f:P * f + P], xT[:, k, c0:c0 + n])
                                                      for k in range(KC)]).then_inc(shu_mm, 1)
                pe.wait_ge(sT_ready, (bl + 1) * (SF // P))
                pe.wait_ge(slots_ready, 2)
                for t in range(c0 // P, (c0 + n + P - 1) // P):
                    m = min(P, TOK - t * P)
                    if t >= 4:
                        pe.wait_ge(sho_taken, t - 3)
                    product(bank(4 + t % 4)[0:m, 0:ED], [(sT[:, f, P * t - c0:P * t - c0 + m], dT[:, f, :])
                                                         for f in range(SF // P)]).then_inc(sho_mm, 1)

            shared_block(0)
            pe.wait_ge(sho_taken, 4)
            arrived(pe, "gate_up")
            arrived(pe, "down")

            def hidden1(i, s, k):
                e = expert["hidden"]
                pe.wait_ge(rowsT_ready[1], i + 1)
                pe.wait_ge(hid_ready[1], i)
                product(bank(2 + s), [(rowsT[1][:, s, c, :], gate_up[:, bass.ds(e * (KC * 2 * FF1) + 2 * FF1 * c, 2 * FF1)])
                                      for c in range(KC)]).then_inc(hid_mm[1], 1)

            def turn_hidden1(i, s, k):
                pe.wait_ge(hid_ready[1], i + 2)
                pe.wait_ge(hidT_ready[1], i)
                for c in range(FF1 // P):
                    last = turned(bank(4)[:, P * c:P * c + P], hid[1][:, s, FF1 + P * c:FF1 + P * c + P])
                last.then_inc(hidT_mm[1], 1)

            def out1(i, s, k):
                e = expert["out"]
                pe.wait_ge(hidT_ready[1], i + 1)
                pe.wait_ge(y_ready[1], i)
                product(bank(6)[:, 0:ED], [(hidT[1][:, s, c, :], down[:, bass.ds(e * (FF1 // P * ED) + ED * c, ED)])
                                           for c in range(FF1 // P)]).then_inc(y_mm[1], 1)

            pipelined(pe, NT1, (expert_of(1, "hidden"), 1), (expert_of(1, "out"), 3), (turn_rows(1), 0), (turn_hidden1, 2), (hidden1, 1), (out1, 3))
            pe.wait_ge(y_ready[1], NT1)
            shared_block(1)
            shared_block(2)


def kernel(**inputs):
    import numpy as np
    import concourse.bacc as bacc
    from concourse.bass_utils import run_bass_kernel_spmd as run

    nc = bacc.Bacc("TRN2", target_bir_lowering=False, num_devices=1)
    arrays, args = {}, {}
    for name, value in inputs.items():
        v = np.ascontiguousarray(value)
        arrays[f"in_{name}"] = v
        args[name] = nc.dram_tensor(f"in_{name}", v.shape, mybir.dt.from_np(v.dtype), kind="ExternalInput").ap()
    out = nc.dram_tensor("out", (B, S, ED), F32, kind="ExternalOutput").ap()
    vit_tower(nc, args, out)
    r = run(nc, [arrays], core_ids=[0])
    return r.results[0]["out"]
```

```python
import concourse.bass as bass
from concourse import mybir
from contextlib import ExitStack

F32 = mybir.dt.float32
BF16 = mybir.dt.bfloat16
I32 = mybir.dt.int32
U32 = mybir.dt.uint32
ALU = mybir.AluOpType
ACT = mybir.ActivationFunctionType
AX = mybir.AxisListType

P = 128
B, C, HW, PS = 32, 3, 96, 16
G = HW // PS
ED = 256
KC = ED // P
PD = C * PS * PS
PC = PD // P
NP = G * G
S = NP + 1
TOK = B * S
NT = 10
QP = 64
PATCH_TILES = NT - 1
PAIRS = B // 2
EPS = 1e-5

H0, HD0 = 16, 16
E0, FF0, NT0 = 8, 1024, 17
H1, DK, DC = 8, 128, 32
E1, FF1, NT1, SF = 16, 256, 25, 1024

assert NT0 == (TOK + E0 * (P - 1)) // P and NT1 == (TOK + E1 * (P - 1)) // P
BLOCKS = [(0, 512), (512, 512), (1024, TOK - 1024)]


class Chain:

    def __init__(self, engine, sem, per=None):
        self.engine, self.sem, self.per, self.base, self.n = engine, sem, per, 0, 0

    def at(self, i):
        assert self.n in (0, self.per), (self.n, self.per)
        self.base, self.n = i * self.per, 0

    def did(self, ins):
        ins.then_inc(self.sem, 1)
        self.n += 1

    def wait(self):
        self.engine.wait_ge(self.sem, self.base + self.n)


def pipelined(engine, n, *stages):
    longest = max(delay for _, delay in stages)

    def step(at, r=None):
        for f, delay in stages:
            i = at - delay
            if r is not None:
                f(r * 2 + i, i % 2, r + i // 2)
            elif 0 <= i < n:
                f(i, i % 2, i // 2)

    first = (longest + 3) // 2
    for at in range(2 * first):
        step(at)
    with engine.Fori(first, n // 2) as r:
        step(0, r)
        step(1, r)
    for at in range(2 * (n // 2), n + longest):
        step(at)


def vit_tower(nc, a, out):
    ctx = ExitStack()
    with ctx:
        def sb(name, shape, dt=F32):
            return ctx.enter_context(nc.sbuf_tensor(name, shape, dt))[:]

        def sem(name):
            return ctx.enter_context(nc.semaphore(name))

        sorted_x = [nc.dram_tensor("sorted_x0", (NT0 * P, ED), F32, kind="Internal").ap(),
                    nc.dram_tensor("sorted_x1", (NT1 * P, ED), F32, kind="Internal").ap()]
        sorted_y = [nc.dram_tensor("sorted_y0", (NT0 * P, ED), F32, kind="Internal").ap(),
                    nc.dram_tensor("sorted_y1", (NT1 * P, ED), F32, kind="Internal").ap()]

        shuffled = nc.dram_tensor("shuffled", (HD0, S * H0, B), F32, kind="Internal").ap()

        h = sb("h", [P, NT, ED])
        xn = sb("xn", [P, NT, ED])
        xT = sb("xT", [P, KC, NT * P])
        ident = sb("ident", [P, P])
        block16 = sb("block16", [P, 8, 16])
        centre = sb("centre", [P, P])
        average = sb("average", [P, P])
        ones_row = sb("ones_row", [1, P])
        before = sb("before", [P, P], BF16)
        ones16 = sb("ones16", [P, P], BF16)
        iota_e = sb("iota_e", [P, 17 * 2])
        thresholds = sb("thresholds", [P, NT])
        lower_e = sb("lower_e", [P, E1, E1])
        eps_col = sb("eps_col", [P, 1])
        warm = sb("warm", [P, 1])
        stats = sb("stats", [P, NT, 3, 6])
        meanvar = sb("meanvar", [P, NT, 2])
        sd = sb("sd", [P, NT])
        rstd = sb("rstd", [P, NT])

        logits = sb("logits", [P, NT, E1])
        top = sb("top", [P, NT])
        first = sb("first", [P, NT])
        mask = sb("mask", [P, NT, E1])
        onehot = sb("onehot", [P, NT, E1], BF16)
        weight = sb("weight", [P, NT])
        counts_over = sb("counts_over", [P, E1, NT])
        tiles_e = sb("tiles_e", [P, E1])
        base_e = sb("base_e", [P, E1])
        end_e = sb("end_e", [P, E1])
        base_tmp = sb("base_tmp", [P, E1, E1])
        slot_f = sb("slot_f", [P, NT])
        slot = sb("slot", [P, 2, NT], I32)
        tile_cmp = sb("tile_cmp", [1, NT1, E1])
        tile_e_f = sb("tile_e_f", [1, NT1])
        tile_e = sb("tile_e", [1, 2, NT1], I32)
        onehot_f = sb("onehot_f", [P, NT, E0])

        gate_w0 = sb("gate_w0", [P, KC, E0])
        router1 = sb("router1", [E1, ED])
        routerT1 = sb("routerT1", [P, KC, E1])
        b1T = sb("b1T", [P, E0, FF0 // P])
        b2 = sb("b2", [E0, ED])
        b1_rows = sb("b1_rows", [E0 * FF0 // P, P])
        q_w = sb("q_w", [P, 1])
        q_b = sb("q_b", [P, 1])
        k_w = sb("k_w", [P, 1])
        k_b = sb("k_b", [P, 1])
        k_of = sb("k_of", [P, 4])
        down_u = sb("down_u", [P, KC, P])
        down_k = sb("down_k", [P, KC, P])
        bias_u = sb("bias_u", [P, 1])
        bias_k = sb("bias_k", [P, 1])
        keyT = sb("keyT", [P, H1 // 2, P])
        valO = sb("valO", [P, 2, ED])
        bias_o = sb("bias_o", [P, ED])

        KB = 256
        R1, R2, R3, RE = 0, 64 * KB, 96 * KB, 156 * KB
        arena = sb("arena", [P, RE])
        arena_ap = arena[:, :]

        class Area:

            def __init__(self, start, end):
                self.next, self.end = start, end

            def take(self, *shape):
                n = 1
                for x in shape:
                    n *= x
                v = arena_ap[:, self.next:self.next + n]
                self.next += n
                assert self.next <= self.end, (self.next, self.end)
                if len(shape) == 1:
                    return v
                names = "abcd"[:len(shape)]
                return v.rearrange(f"p ({' '.join(names)}) -> p {' '.join(names)}",
                                   **{c: s for c, s in zip(names, shape)})

        w1 = arena_ap[:, R1:R1 + E0 * KC * FF0]
        w2 = arena_ap[:, R2:R2 + E0 * FF0 // P * ED]
        gate_up = arena_ap[:, R1:R1 + E1 * KC * 2 * FF1]
        down = arena_ap[:, R2:R2 + E1 * FF1 // P * ED]

        wx = Area(R2 - 8 * KB, R2)
        qT, kT, vT, woe = (wx.take(KC, ED) for _ in range(4))

        prep = Area(R2, R3)
        wq_raw, wk_raw, wv_raw, wo_raw = (prep.take(KC, ED) for _ in range(4))
        uk_raw, uq_raw, uv_raw = (prep.take(H1 * DK) for _ in range(3))
        qr_raw = prep.take(H1, P)
        ukT = prep.take(H1, P)
        uqT = prep.take(H1, DC + 1)
        uvT = prep.take(H1, DC + 1)
        squares = Area(R2 + 8 * KB, R3)
        sq = squares.take(2 * KC * len(BLOCKS), 512)

        emb = Area(R3, RE)
        x_a = emb.take(C, PS, HW)
        wo1_raw = emb.take(H1, ED)
        sparse_v = emb.take(16, P)
        sparse_o = emb.take(P, 16)
        woT = emb.take(KC, ED)
        b_o = emb.take(ED)
        tiled_v, tiled_o, blockM = (emb.take(P) for _ in range(3))
        sv_w, so_w = emb.take(16), emb.take(16)
        emb1 = Area(R1, R2 - 8 * KB)
        x_b = emb1.take(C, PS, HW // 2)
        patch = emb1.take(2, PD)
        patchT = emb1.take(2, PC, P)
        w_proj = emb1.take(PC, ED)
        wg_proj = emb1.take(PC, ED)
        ln1_g, ln1_b = emb1.take(PC), emb1.take(PC)
        b_proj, bias_z, ln2_g, ln2_b = (emb1.take(ED) for _ in range(4))
        zero = emb1.take(8 * ED)

        at0 = Area(R3, RE)
        kn = at0.take(KC, B, S)
        q_ring = at0.take(2, KC, 2, 2 * QP)
        k_ring = [at0.take(KC, 2, 4, S) for _ in range(2)]
        xv = at0.take(2, KC, 2 * QP)
        v_ring = at0.take(2, 2, ED)
        p_ring = at0.take(2, 16, QP)
        at0.take(R3 + E0 * FF0 // P * ED // 2 - at0.next)
        qn = at0.take(KC, B, S)
        ctxT = at0.take(KC, S * B)
        yT = qn.rearrange("p c b n -> p c (b n)")
        pT = [at0.take(16, S) for _ in range(2)]
        mx = at0.take(2, 16)
        sm = at0.take(2, 16)

        def rings(area, width, chunks):
            return (area.take(2, ED), area.take(2, KC, P), area.take(2, width), area.take(2, chunks, P),
                    area.take(2, ED))

        moe = Area(R3 + 32 * KB, RE)
        onehotT = moe.take(NT, P)
        experts0 = rings(moe, FF0, FF0 // P)

        at1 = Area(R3, RE)
        lat_u = at1.take(B, QP)
        lat_k = at1.take(B * S)
        keys = at1.take(H1 // 2, B * S)
        ctx1T = at1.take(2, NT * P)
        lat_v = at1.take(2, 2, 2 * DC)
        u_ring = at1.take(2, 2, 2 * QP)
        lk_ring = at1.take(2, 2 * QP)
        p1_ring = at1.take(2, 8, QP)
        pT1 = [at1.take(4, 2, S) for _ in range(2)]
        mx1 = at1.take(2, 8)
        sm1 = at1.take(2, 8)

        sh = Area(R3, RE)
        gT = sh.take(KC, SF)
        upT = sh.take(KC, SF)
        dT = sh.take(SF // P, ED)
        sT = sh.take(SF // P, 512)
        sg = sh.take(2, 512)
        experts1 = rings(sh, 2 * FF1, FF1 // P)
        sh_raw = Area(R2, R3)
        g_raw = sh_raw.take(SF // P, ED)
        up_raw = sh_raw.take(SF // P, ED)
        d_raw = sh_raw.take(KC, SF)
        rows_in, rowsT, hid, hidT, rows_out = zip(experts0, experts1)

        psum = ctx.enter_context(nc.psum_tensor("psum", [P, 8 * 512], F32))

        def bank(b, n=1):
            return psum[:, 512 * b:512 * (b + n)]

        x = a["x"]
        loads = {}
        for c in range(C):
            loads[f"x_a{c}"] = [(x_a[:, c].rearrange("p i w -> p (i w)"),
                                 x[:, c, 0:4 * PS, :].rearrange("b (r i) w -> r b (i w)", r=4))]
        loads["x_b"] = [(x_b[64 * wh + 32 * r:64 * wh + 32 * r + 32, c, :, :],
                         x[:, c, PS * (4 + r):PS * (5 + r), 48 * wh:48 * wh + 48])
                        for wh in range(2) for r in range(2) for c in range(C)]
        wp = a["L0_tok_W_proj"].rearrange("(f c) e -> c f e", c=C)
        loads["proj"] = [(w_proj[:, 2 * c:2 * c + 2, :], wp[c].rearrange("(k p) e -> p k e", p=P)) for c in range(C)] + [
            (v.rearrange("p (c k) -> p c k", c=C), a[name].rearrange("(k p c) -> p c k", p=P, c=C))
            for v, name in ((ln1_g, "L0_tok_ln1_g"), (ln1_b, "L0_tok_ln1_b"))] + [
            (b_proj[0:1, :], a["L0_tok_b_proj"].rearrange("(o e) -> o e", o=1)),
            (b_o[0:1, :], a["L1_attn_b_O"].rearrange("(o e) -> o e", o=1)),
            (ln2_g, a["L0_tok_ln2_g"].rearrange("(o e) -> o e", o=1).broadcast_to((P, ED))),
            (ln2_b, a["L0_tok_ln2_b"].rearrange("(o e) -> o e", o=1).broadcast_to((P, ED)))]
        pos = a["L0_tok_pos_emb"]

        def token_runs():
            for j in range(4):
                yield 0, G, j, 1 + G * j
            for j in range(4):
                yield G, G // 2, j, 1 + G * (4 + j % 2) + G // 2 * (j // 2)

        loads["pos"] = [(h[32 * j:32 * j + 32, t:t + nt, :], pos[:, n:n + nt, :].broadcast_to((32, nt, ED)))
                        for t, nt, j, n in token_runs()]
        cls_pos = xn[0:32, NT - 1, :]
        loads["cls"] = [(h[0:32, NT - 1, :], pos[0, 0:1, :].broadcast_to((32, ED))),
                        (cls_pos, a["L0_tok_cls_token"][0, 0:1, :].broadcast_to((32, ED)))]

        def rows(name):
            return a[name].rearrange("(k p) e -> p k e", p=P)
        loads["attn0"] = [(wq_raw, rows("L0_attn_W_Q")), (wk_raw, rows("L0_attn_W_K")),
                          (wv_raw, rows("L0_attn_W_V")), (wo_raw, rows("L0_attn_W_O")),
                          (sparse_v[0:H0], a["L0_attn_sparse_W_V"]), (sparse_o[0:H0], a["L0_attn_sparse_W_O"])]
        loads["small"] = [(d[:, :],
                           a[n].rearrange("(q d o) -> q d o", q=1, o=1).broadcast_to((P // HD0, HD0, 1)))
                          for d, n in ((q_w, "L0_attn_q_ln_w"), (q_b, "L0_attn_q_ln_b"),
                                       (k_w, "L0_attn_k_ln_w"), (k_b, "L0_attn_k_ln_b"))]
        loads["small"] += [(gate_w0, rows("L0_ffn_gate_w")), (router1, a["L1_ffn_router_w"]), (b2, a["L0_ffn_b2"])]
        loads["small"] += [(b1_rows[:], a["L0_ffn_b1"].rearrange("e (c p) -> (e c) p", p=P))]
        row = lambda name: a[name].rearrange("(o e) -> o e", o=1)
        col = lambda name: a[name].rearrange("(d o) -> d o", o=1)
        loads["attn1"] = [
            (down_u[:, :, 0:DC], rows("L1_attn_W_DQ")), (down_u[:, :, 64:64 + DC], rows("L1_attn_W_DQ")),
            (down_k[:, :, 0:DC], rows("L1_attn_W_DKV")), (down_k[:, :, DC:2 * DC], rows("L1_attn_W_KR")),
            (bias_u[0:DC, :], col("L1_attn_b_DQ")), (bias_u[64:64 + DC, :], col("L1_attn_b_DQ")),
            (bias_k[0:DC, :], col("L1_attn_b_DKV")), (bias_k[DC:2 * DC, :], col("L1_attn_b_KR")),
            (uk_raw[0:DC, :], a["L1_attn_W_UK"]), (uk_raw[64:65, :], row("L1_attn_b_UK")),
            (uq_raw[0:DC, :], a["L1_attn_W_UQ"]), (uq_raw[DC:DC + 1, :], row("L1_attn_b_UQ")),
            (uv_raw[0:DC, :], a["L1_attn_W_UV"]), (uv_raw[DC:DC + 1, :], row("L1_attn_b_UV")),
            (qr_raw[0:DC, :, DC:2 * DC], a["L1_attn_W_QR"].rearrange("c (h r) -> c h r", h=H1)),
            (qr_raw[DC:DC + 1, :, DC:2 * DC], row("L1_attn_b_QR").rearrange("o (h r) -> o h r", h=H1)),
            (wo1_raw, rows("L1_attn_W_O"))]
        w1v = w1.rearrange("p (e k f) -> p e k f", e=E0, k=KC)
        w2v = w2.rearrange("p (e c n) -> p e c n", e=E0, n=ED)
        W1 = a["L0_ffn_w1"].rearrange("e (k p) f -> p e k f", p=P)
        W2 = a["L0_ffn_w2"].rearrange("e (c p) n -> p e c n", p=P)
        loads["w1"] = [(w1v[:, e], W1[:, e]) for e in range(E0)]
        loads["w2"] = [(w2v[:, e], W2[:, e]) for e in range(E0)]
        guv = gate_up.rearrange("p (e k f) -> p e k f", e=E1, k=KC)
        dv = down.rearrange("p (e c n) -> p e c n", e=E1, n=ED)
        GU = a["L1_ffn_gate_up_proj"].rearrange("e (k p) f -> p e k f", p=P)
        DN = a["L1_ffn_down_proj"].rearrange("e (c p) n -> p e c n", p=P)
        loads["gate_up"] = [(guv[:, e], GU[:, e]) for e in range(E1)]
        loads["down"] = [(dv[:, 2 * e:2 * e + 2], DN[:, 2 * e:2 * e + 2]) for e in range(E1 // 2)]
        loads["shared"] = [(g_raw, rows("L1_ffn_shared_gate_w")), (up_raw, rows("L1_ffn_shared_up_w")),
                           (d_raw, rows("L1_ffn_shared_down_w"))]
        load_sem = {name: sem(f"ld_{name}") for name in loads}

        def arrived(engine, name, n=None):
            engine.wait_ge(load_sem[name], 16 * (len(loads[name]) if n is None else n))

        (prep_zeroed, consts_ready, averages_ready, prep_mm, prep_out, tiled_ready, folded, ln1_stats, ln1_sd,
         patch_ready, patch_mm, patchT_ready, z_mm, z_taken, ln2_stats, ln2_sd, pos_ready, embedded,
         ln_stats, ln_sd, xn_ready, xT_mm, xT_ready,
         qk_mm, raw_ready, sq_ready, var_mm, log_ready, inverse_ready, q_norm, k_norm, khead_ready, at0_zeroed,
         xv_ready, v_mm, v_ready, q_ready, k_ready, s_mm, s_taken, p_exp, p_sum, p_norm, t_mm, pT_ready, c_mm,
         c_taken, o_mm, o_taken,
         logits_mm, top_ready, gate_ready, onehot_ready, rank_mm, slots_ready, zero_stored, scattered, ohT_mm, ohT_ready,
         bias2_mm,
         lat_mm, lat_ready, keys_mm, keys_ready, at1_zeroed, u_ready, lk_ready, lv_mm, lv_ready,
         s1_mm, s1_taken, p1_exp, p1_sum, p1_norm, t1_mm, pT1_ready, c1_mm, c1_taken, o1_mm,
         w_mm, w_ready, shg_mm, shu_mm, silu_ready, sT_ready, sho_mm, sho_taken, stored) = [sem(n) for n in """
         prep_zeroed consts_ready averages_ready prep_mm prep_out tiled_ready folded ln1_stats ln1_sd
         patch_ready patch_mm patchT_ready z_mm z_taken ln2_stats ln2_sd pos_ready embedded
         ln_stats ln_sd xn_ready xT_mm xT_ready
         qk_mm raw_ready sq_ready var_mm log_ready inverse_ready q_norm k_norm khead_ready at0_zeroed
         xv_ready v_mm v_ready q_ready k_ready s_mm s_taken p_exp p_sum p_norm t_mm pT_ready c_mm
         c_taken o_mm o_taken
         logits_mm top_ready gate_ready onehot_ready rank_mm slots_ready zero_stored scattered ohT_mm ohT_ready
         bias2_mm
         lat_mm lat_ready keys_mm keys_ready at1_zeroed u_ready lk_ready lv_mm lv_ready
         s1_mm s1_taken p1_exp p1_sum p1_norm t1_mm pT1_ready c1_mm c1_taken o1_mm
         w_mm w_ready shg_mm shu_mm silu_ready sT_ready sho_mm sho_taken stored""".split()]
        rows_loaded = [[sem(f"rows_loaded{l}{s}") for s in range(2)] for l in range(2)]
        rows_mm = [sem(f"rows_mm{l}") for l in range(2)]
        rowsT_ready = [sem(f"rowsT_ready{l}") for l in range(2)]
        hid_mm = [sem(f"hid_mm{l}") for l in range(2)]
        hid_ready = [sem(f"hid_ready{l}") for l in range(2)]
        hidT_mm = [sem(f"hidT_mm{l}") for l in range(2)]
        hidT_ready = [sem(f"hidT_ready{l}") for l in range(2)]
        y_mm = [sem(f"y_mm{l}") for l in range(2)]
        y_ready = [sem(f"y_ready{l}") for l in range(2)]
        y_stored = [[sem(f"y_stored{l}{s}") for s in range(2)] for l in range(2)]
        experts_done = sem("experts_done")
        spread, reshuffled, tile_order = sem("spread"), [sem("reshuffled0"), sem("reshuffled1")], sem("tile_order")

        def to_tiles(c):
            y = yT[:, c, :].rearrange("p (n b) -> p n b", b=B)
            o = ctxT[:, c, :].rearrange("p (n b) -> p n b", b=B)
            yield (o[:, 0:4 * G, :].rearrange("p (t j) b -> p t j b", j=4),
                   y[:, 1:1 + 4 * G, :].rearrange("p (j t) b -> p t j b", j=4))
            late_o = o[:, 4 * G:6 * G, :].rearrange("p (u w r) b -> p w u r b", w=2, r=2)
            late_y = y[:, 1 + 4 * G:1 + 6 * G, :].rearrange("p (r w u) b -> p w u r b", r=2, w=2)
            for w in range(2):
                yield late_o[:, w], late_y[:, w]
            yield o[:, S - 1, :], y[:, 0, :]
        gathered = [sem(f"gathered{t}") for t in range(NT)]
        silu1, mixed = sem("silu1"), sem("mixed")

        QK = [(which, c, n) for n in range(len(BLOCKS)) for which in range(2) for c in range(KC)]
        QK_BATCHES = [(0, 4), (4, 8), (8, 12)]
        SCALE0, SCALE1 = HD0 ** -0.5, (DK + DC) ** -0.5
        PREP = ["q", "k", "v", "woT", "uk0", "uk1", "uq", "mix", "uv", "keyT", "router", "woe", "b1", "valO",
                "bias_o"]
        PREP_AT = 5
        MIX = PREP.index("mix")

        def prep_done(n):
            return 1 + n + 1 - (n >= MIX)

        def halves(n):
            return [(0, 5), (5, NT)] if n else [(0, G), (G, NT)]

        LATENTS = [(which, bl) for bl in range(len(BLOCKS)) for which in range(2)]
        e_of = [E0, E1]
        nt_of = [NT0, NT1]

        block = ctx.enter_context(nc.Block())

        @block.sync
        def _(sp):
            def load(name, part=slice(None)):
                with nc.allow_non_contiguous_dma(reason="columns of a few vectors"):
                    for dst, src in loads[name][part]:
                        sp.dma_start(dst, src).then_inc(load_sem[name], 16)

            for c in range(C):
                load(f"x_a{c}")
            load("proj")
            load("x_b")
            load("attn0")
            sp.wait_ge(prep_zeroed, 1)
            load("attn1")
            load("pos")
            load("cls")
            load("small")
            for l in range(2):
                zx = sorted_x[l].rearrange("(n p) e -> p n e", p=P)
                for n in range(0, nt_of[l], 8):
                    m = min(8, nt_of[l] - n)
                    sp.dma_start(zx[:, n:n + m, :], zero[:, 0:m * ED].rearrange("p (n e) -> p n e", e=ED))\
                      .then_inc(zero_stored, 16)
            sp.wait_ge(zero_stored, 16 * 7)
            sp.wait_ge(embedded, 1)
            load("w1", slice(0, E0 - 1))
            sp.wait_ge(q_norm, len(QK) // 2)
            sp.wait_ge(k_norm, len(QK) // 2)
            load("w2", slice(0, E0 // 2))
            sp.wait_ge(c_taken, PAIRS)
            by_source = shuffled.rearrange("d (q h) b -> h d q b", h=H0)
            by_target = shuffled.rearrange("d (h q) b -> h d (q b)", h=H0)
            for c in range(KC):
                sp.dma_start(by_source[8 * c:8 * c + 8], ctxT[:, c, :].rearrange("p (q b) -> p q b", b=B))\
                  .then_inc(spread, 16)
            sp.wait_ge(spread, 16 * KC)
            for c in range(KC):
                sp.dma_start(yT[:, c, :], by_target[8 * c:8 * c + 8]).then_inc(reshuffled[c], 16)
            load("w2", slice(E0 // 2, E0))
            sp.wait_ge(o_mm, NT)
            load("w1", slice(E0 - 1, E0))

            def experts(l):
                xs = sorted_x[l].rearrange("(t p) e -> p t e", p=P)

                def front(i, s, k):
                    sp.wait_ge(rows_mm[l], i)
                    sp.dma_start(rows_in[l][:, s:s + 1, :], xs[:, bass.ds(i, 1), :]).then_inc(rows_loaded[l][s], 16)

                sp.wait_ge(scattered, 16 * NT * (l + 1))
                pipelined(sp, nt_of[l], (front, 0))

            experts(0)
            sp.wait_ge(y_mm[0], NT0 + 1)
            for t in range(NT):
                sp.wait_ge(gathered[t], 16)
            load("shared")
            load("gate_up")
            sp.wait_ge(w_mm, 12)
            load("down")
            experts(1)
            n = 0
            for t, nt, j, tok in token_runs():
                if j == 0:
                    sp.wait_ge(experts_done, NT)
                    sp.wait_ge(sho_taken, t + nt)
                sp.dma_start(out[:, tok:tok + nt, :], h[32 * j:32 * j + 32, t:t + nt, :]).then_inc(stored, 16)
                n += 1
            sp.wait_ge(sho_taken, NT)
            sp.dma_start(out[:, 0, :], h[0:32, NT - 1, :]).then_inc(stored, 16)
            sp.wait_ge(stored, 16 * (n + 1))

        @block.gpsimd
        def _(pool):
            ch = Chain(pool, sem("pool_chain"))

            def zeroed(*views):
                for v in views:
                    ch.did(pool.memset(v, 0.0))

            def select(v, pattern, op, fill, base, mult):
                ch.did(pool.affine_select(out=v, in_=v, pattern=pattern, compare_op=op, fill=fill, base=base,
                                          channel_multiplier=mult))
                ch.wait()
            ch.did(pool.memset(ident[:], 0.0))
            ch.did(pool.memset(block16[:], 1.0))
            ch.did(pool.memset(ones16[:], 1.0))
            ch.did(pool.memset(before[:], 1.0))
            ch.did(pool.memset(lower_e[:], 1.0))
            ch.did(pool.memset(eps_col[:], EPS))
            ch.wait()
            select(ident[:], [[-1, P]], ALU.not_equal, 1.0, 0, 1)
            select(block16[:], [[-16, 8], [0, 16]], ALU.is_ge, 0.0, 0, 1)
            select(block16[:], [[16, 8], [0, 16]], ALU.is_ge, 0.0, 15, -1)
            select(before[:], [[1, P]], ALU.is_gt, 0.0, 0, -1)
            select(lower_e[:], [[1, E1], [-1, E1]], ALU.is_gt, 0.0, 0, 0)
            ch.did(pool.iota(iota_e[:], pattern=[[1, 34]], base=0, channel_multiplier=0,
                             allow_small_or_imprecise_dtypes=True))
            ch.did(pool.iota(thresholds[:], pattern=[[P, NT]], base=0, channel_multiplier=0,
                             allow_small_or_imprecise_dtypes=True))
            ch.wait()
            pool.sem_inc(consts_ready, 1)

            zeroed(keyT[:], down_u[:], down_k[:], bias_u[:], bias_k[:], uk_raw, uq_raw, uv_raw, qr_raw, zero,
                   h[:, NT - 1, :])
            ch.wait()
            for v, at in ((bias_u, DC), (bias_u, 64 + DC), (bias_k, 2 * DC)):
                ch.did(pool.affine_select(out=v[:], in_=v[:], pattern=[[0, 1]], compare_op=ALU.not_equal,
                                          fill=1.0, base=-at, channel_multiplier=1))
                ch.wait()
            pool.memset(ones_row[:], 1.0).then_inc(prep_zeroed, 1)

            arrived(pool, "pos")
            arrived(pool, "proj")
            hp = h[:, 0:PATCH_TILES, :]
            pool.tensor_tensor(out=hp, in0=hp, in1=ln2_b.rearrange("p (o e) -> p o e", o=1)
                               .broadcast_to((P, PATCH_TILES, ED)), op=ALU.add).then_inc(pos_ready, 1)
            arrived(pool, "cls")
            pool.tensor_tensor(out=h[0:32, NT - 1, :], in0=h[0:32, NT - 1, :], in1=cls_pos, op=ALU.add)\
                .then_inc(pos_ready, 1)

            pool.wait_ge(embedded, 1)
            pool.wait_ge(prep_out, prep_done(len(PREP) - 1))
            for v in (q_ring, xv, v_ring, p_ring):
                last = pool.memset(v, 0.0)
                ch.did(last)
            ch.wait()
            pool.sem_inc(at0_zeroed, 1)

            ln_tok = xT.rearrange("p k (n b) -> p k b n", b=B)
            pool.wait_ge(xT_ready, NT)

            def front(i, s, k):
                pool.wait_ge(v_mm, i)
                for c in range(KC):
                    ins = pool.tensor_copy(xv[:, s, c, :].rearrange("p (j n) -> p j n", j=2)[:, :, 0:S],
                                           ln_tok[:, c, bass.ds(i * 2, 2), 0:S])
                    ins.then_inc(xv_ready, 1)
                pool.wait_ge(s_mm, i)
                if isinstance(i, int) and i == 0:
                    pool.wait_ge(khead_ready, 1 + len(QK) // 2)
                for c in range(KC):
                    pool.tensor_tensor(
                        out=k_ring[s][:, c],
                        in0=kn[:, c, bass.ds(i * 2, 2), :].rearrange("p j (o n) -> p j o n", o=1)
                        .broadcast_to((P, 2, 4, S)),
                        in1=k_of[:].rearrange("p (o h q) -> p o h q", o=1, q=1).broadcast_to((P, 2, 4, S)),
                        op=ALU.mult).then_inc(k_ready, 1)

            def back(i, s, k):
                pool.wait_ge(p_sum, i + 1)
                pv = p_ring[:, s, :, 0:S]
                pool.tensor_tensor(out=pv, in0=pv, in1=sm[:, s, :].rearrange("p (g o) -> p g o", o=1)
                                   .broadcast_to((P, 16, S)), op=ALU.mult).then_inc(p_norm, 1)

            pipelined(pool, PAIRS, (front, 0), (back, 1))

            def scatter(l):
                pool.wait_ge(slots_ready, l + 1)
                pool.wait_ge(zero_stored, 16 * 7)
                for t in range(NT):
                    n = P if t < NT - 1 else B
                    pool.indirect_dma_start(
                        out=sorted_x[l], out_offset=bass.IndirectOffsetOnAxis(
                            ap=slot[0:n, l, t:t + 1].bitcast(U32), axis=0),
                        in_=xn[0:n, t, :], in_offset=None).then_inc(scattered, 16)

            def store_rows(l):
                ys = sorted_y[l].rearrange("(t p) e -> p t e", p=P)

                def store(i, s, k):
                    pool.wait_ge(y_ready[l], i + 1)
                    pool.dma_start(ys[:, bass.ds(i, 1), :], rows_out[l][:, s:s + 1, :]).then_inc(y_stored[l][s], 16)

                pipelined(pool, nt_of[l], (store, 0))

            def gather(l):
                for s in range(2):
                    pool.wait_ge(y_stored[l][s], 16 * ((nt_of[l] + 1 - s) // 2))
                pool.wait_ge(scattered, 16 * NT * (l + 1))
                for t in range(NT):
                    n = P if t < NT - 1 else B
                    pool.indirect_dma_start(
                        out=xn[0:n, t, :], out_offset=None, in_=sorted_y[l],
                        in_offset=bass.IndirectOffsetOnAxis(ap=slot[0:n, l, t:t + 1].bitcast(U32), axis=0))\
                        .then_inc(gathered[t], 16)

            scatter(0)
            store_rows(0)
            pool.wait_ge(y_mm[0], NT0 + 1)
            ch.did(pool.memset(lat_u, 0.0))
            gather(0)

            for v in (lat_v, u_ring, lk_ring, p1_ring, ctx1T):
                ch.did(pool.memset(v, 0.0))
            ch.wait()
            pool.sem_inc(at1_zeroed, 1)
            pool.wait_ge(lat_ready, 6)

            pool.sem_inc(p1_norm, 1)

            def front1(i, s, k):
                pool.wait_ge(lv_mm, i)
                pool.wait_ge(p1_norm, i)
                pool.tensor_copy(lk_ring[:, s, :].rearrange("p (j n) -> p j n", j=2)[:, :, 0:S],
                                 lat_k.rearrange("p (b n) -> p b n", n=S)[:, bass.ds(i * 2, 2), :])\
                    .then_inc(lk_ready, 1)

            def back1(i, s, k):
                pool.wait_ge(p1_sum, i + 1)
                pool.wait_ge(lk_ready, i + 1)
                pv = p1_ring[:, s, :, 0:S]
                pool.tensor_tensor(out=pv, in0=pv, in1=sm1[:, s, :].rearrange("p (g o) -> p g o", o=1)
                                   .broadcast_to((P, 8, S)), op=ALU.mult).then_inc(p1_norm, 1)

            pipelined(pool, PAIRS, (front1, 0), (back1, 1))
            scatter(1)
            store_rows(1)
            gather(1)

        @block.scalar
        def _(act):
            def evacuated(done, dst, src):
                act.activation(dst, src, ACT.Copy).then_inc(done, 1)

            act.wait_ge(consts_ready, 1)
            act.activation(warm[:], eps_col[:], ACT.Sqrt)

            def ln1_deviation(n, t0, t1):
                act.wait_ge(ln1_stats, n + 1)
                act.activation(sd[:, t0:t1], meanvar[:, t0:t1, 1], ACT.Sqrt, bias=eps_col[:, 0:1])\
                   .then_inc(ln1_sd, 1)

            def prep_out_of_psum(n):
                what = PREP[n]
                if what == "mix":
                    return
                act.wait_ge(prep_mm, n + 2)
                src = bank(7 - n % 2)
                two = lambda v: v.rearrange("p k e -> p (k e)")
                if what in ("q", "k", "v", "woT", "woe"):
                    dst = {"q": qT, "k": kT, "v": vT, "woT": woT, "woe": woe}[what]
                    evacuated(prep_out, two(dst), src)
                elif what == "router":
                    evacuated(prep_out, two(routerT1[:]), src[:, 0:KC * E1])
                elif what == "b1":
                    evacuated(prep_out, two(b1T[:]), src[:, 0:E0 * FF0 // P])
                elif what in ("uk0", "uk1"):
                    m = 4 * (what == "uk1")
                    evacuated(prep_out, two(ukT[:, m:m + 4, :]), src)
                elif what in ("uq", "uv"):
                    evacuated(prep_out, two(uqT if what == "uq" else uvT), src[:, 0:H1 * (DC + 1)])
                elif what == "keyT":
                    evacuated(prep_out, keyT[:].rearrange("p a (r n) -> p (a r) n", r=2)[:, :, 0:DC + 1],
                              src[:, 0:H1 * (DC + 1)].rearrange("p (g n) -> p g n", g=H1))
                elif what == "valO":
                    evacuated(prep_out, two(valO[:]), src)
                elif what == "bias_o":
                    evacuated(prep_out, bias_o[:], src[:, 0:ED])

            def ln2_deviation(n, t0, t1):
                act.wait_ge(ln2_stats, n + 1)
                act.activation(sd[:, t0:t1], meanvar[:, t0:t1, 1], ACT.Sqrt, bias=eps_col[:, 0:1])\
                   .then_inc(ln2_sd, 1)

            ln1_deviation(0, 0, G)
            for t in range(PATCH_TILES):
                act.wait_ge(patch_mm, t + 1)
                if t >= 2:
                    act.wait_ge(z_mm, t - 1)
                act.activation(patchT[:, t % 2].rearrange("p c n -> p (c n)"),
                               bank(2 * (t % 2), 2)[:, 0:PD], ACT.Copy).then_inc(patchT_ready, 1)
                if t == 1:
                    act.wait_ge(prep_mm, 1)
                    evacuated(prep_out, bias_z, bank(6)[:, 0:ED])
                if t == 2:
                    ln1_deviation(1, G, PATCH_TILES)
                if t == PATCH_TILES - 2:
                    ln2_deviation(0, 0, G)
                if t >= PREP_AT:
                    for n in range(2 * (t - PREP_AT), 2 * (t - PREP_AT) + 2):
                        prep_out_of_psum(n)
            ln2_deviation(1, G, PATCH_TILES)

            def deviation(n, half):
                t0, t1 = halves(n)[half]
                act.wait_ge(ln_stats, 2 * n + half + 1)
                act.activation(sd[:, t0:t1], meanvar[:, t0:t1, 1], ACT.Sqrt, bias=eps_col[:, 0:1])\
                   .then_inc(ln_sd, 1)

            def layernorm(n, between=None):
                for half, (t0, t1) in enumerate(halves(n)):
                    if n or half:
                        deviation(n, half)
                    if half and between:
                        between()
                    for t in range(t0, t1):
                        act.wait_ge(xT_mm, NT * n + t + 1)
                        act.activation(xT[:, :, P * t:P * t + P],
                                       bank(t % 3)[:, 0:KC * P].rearrange("p (k n) -> p k n", k=KC),
                                       ACT.Copy).then_inc(xT_ready, 1)

            deviation(0, 0)
            for n in range(2 * (PATCH_TILES - PREP_AT), len(PREP)):
                prep_out_of_psum(n)
            layernorm(0)

            def squares_of(v0, v1):
                for v in range(v0, v1):
                    n = BLOCKS[QK[v][2]][1]
                    act.wait_ge(raw_ready, v + 1)
                    act.activation(sq[:, v, 0:n], bank(4 + v % 4)[:, 0:n], ACT.Square).then_inc(sq_ready, 1)

            def inverses_of(v0, v1):
                for v in range(v0, v1):
                    n = BLOCKS[QK[v][2]][1]
                    act.wait_ge(var_mm, v + 1)
                    act.activation(sq[:, v, 0:n], bank(v % 4)[:, 0:n], ACT.Ln, bias=eps_col[:, 0:1])\
                       .then_inc(log_ready, 1)
                for v in range(v0, v1):
                    n = BLOCKS[QK[v][2]][1]
                    act.wait_ge(log_ready, v + 1)
                    act.activation(sq[:, v, 0:n], sq[:, v, 0:n], ACT.Exp, scale=-0.5).then_inc(inverse_ready, 1)

            squares_of(0, 8)
            inverses_of(0, 4)
            squares_of(8, 12)
            inverses_of(4, 12)
            act.wait_ge(q_norm, len(QK) // 2)
            act.wait_ge(at0_zeroed, 1)

            def queries(i, s, k):
                act.wait_ge(s_mm, i)
                for half in range(2):
                    r = slice(64 * half, 64 * half + 64)
                    act.activation(q_ring[r, s, :, :, QP * half:QP * half + S],
                                   qn[r, :, bass.ds(i * 2, 2), :], ACT.Identity,
                                   scale=q_w[r, 0:1], bias=q_b[r, 0:1]).then_inc(q_ready, 1)

            def values(i, s, k):
                act.wait_ge(v_mm, i + 2)
                act.wait_ge(c_mm, i)
                for half in range(2):
                    for j in range(2):
                        cols = lambda v: v.rearrange("p (g two d) -> p g two d", two=2, d=HD0)[:, :, half, :]
                        act.activation(cols(v_ring[64 * half:64 * half + 64, s, j, :]),
                                       cols(bank(6)[64 * j:64 * j + 64, 0:ED]), ACT.Copy).then_inc(v_ready, 1)

            def exps(i, s, k):
                act.wait_ge(s_taken, i + 2)
                pv = p_ring[:, s, :, 0:S]
                act.activation(pv, pv, ACT.Exp, scale=SCALE0).then_inc(p_exp, 1)

            def back(i, s, k):
                act.wait_ge(t_mm, i + 2)
                act.wait_ge(c_mm, i)
                act.activation(pT[s], bank(4, 2).rearrange("p (g n) -> p g n", n=QP)[:, :, 0:S], ACT.Copy)\
                   .then_inc(pT_ready, 1)

            pipelined(act, PAIRS, (back, 3), (queries, 0), (values, 1), (exps, 1))
            act.wait_ge(reshuffled[0], 16)
            for dst, src in to_tiles(0):
                act.activation(dst, src, ACT.Copy).then_inc(tile_order, 1)
            layernorm(1)
            act.wait_ge(top_ready, 1)
            act.activation(logits[:, :, 0:E0], logits[:, :, 0:E0], ACT.Exp).then_inc(gate_ready, 1)
            for n in range(3):
                act.wait_ge(ohT_mm, n + 1)
                m = min(4, NT - 4 * n)
                act.activation(onehotT[0:E0, 4 * n:4 * n + m, :].rearrange("p t n -> p (t n)"),
                               bank(5 + n)[0:E0, 0:P * m], ACT.Copy).then_inc(ohT_ready, 1)

            act.wait_ge(slots_ready, 1)

            expert = {}

            def expert_of_bias(i, s, k):
                expert["bias"] = act.value_load(tile_e[0:1, 0, bass.ds(i, 1)], min_val=0, max_val=E0 - 1)

            def xfront(i, s, k):
                act.wait_ge(rows_mm[0], i + 2)
                act.activation(rowsT[0][:, s], bank(0)[:, 0:KC * P].rearrange("p (k n) -> p k n", k=KC), ACT.Copy)\
                   .then_inc(rowsT_ready[0], 1)

            def xback(i, s, k):
                e = expert["bias"]
                act.wait_ge(hidT_mm[0], i + 2)
                act.wait_ge(y_mm[0], i)
                b1f = b1T[:, :, :].rearrange("p e c -> p (e c)")
                for c in range(FF0 // P):
                    act.activation(hidT[0][:, s, c, :], bank(4, 2)[:, P * c:P * c + P], ACT.Gelu,
                                   bias=b1f[:, bass.ds(e * (FF0 // P) + c, 1)]).then_inc(hidT_ready[0], 1)

            pipelined(act, NT0, (expert_of_bias, 2), (xfront, 0), (xback, 2))

            def latents(v0, v1):
                act.wait_ge(at1_zeroed, 1)
                for v in range(v0, v1):
                    which, bl = LATENTS[v]
                    c0, n = BLOCKS[bl]
                    act.wait_ge(lat_mm, v + 1)
                    if which == 0:
                        dst = lat_u.rearrange("p b n -> p n b")[:, c0 // B:(c0 + n) // B, :]
                    else:
                        dst = lat_k.rearrange("p (b n) -> p n b", n=S)[:, c0 // B:(c0 + n) // B, :]
                    act.activation(dst, bank(4 + v % 4)[:, 0:n].rearrange("p (n b) -> p n b", b=B), ACT.Identity,
                                   bias=(bias_k if which else bias_u)[:, 0:1]).then_inc(lat_ready, 1)

            layernorm(2, between=lambda: latents(0, 2))
            latents(2, 6)
            for v in range(12):
                c0, n = BLOCKS[v % 3]
                act.wait_ge(keys_mm, v + 1)
                act.activation(keys[:, v // 3, c0:c0 + n], bank(v % 4)[:, 0:n], ACT.Copy).then_inc(keys_ready, 1)

            def queries1(i, s, k):
                act.wait_ge(s1_mm, i)
                for half in range(2):
                    r = slice(64 * half, 64 * half + 64)
                    act.activation(u_ring[r, s, :, QP * half:QP * half + QP],
                                   lat_u[r, bass.ds(i * 2, 2), :], ACT.Copy).then_inc(u_ready, 1)

            def values1(i, s, k):
                act.wait_ge(lv_mm, i + 2)
                act.wait_ge(c1_mm, i)
                for half in range(2):
                    for j in range(2):
                        act.activation(lat_v[64 * half:64 * half + 64, s, j, DC * half:DC * half + DC],
                                       bank(6)[64 * j:64 * j + 64, 0:DC], ACT.Copy).then_inc(lv_ready, 1)

            def exps1(i, s, k):
                act.wait_ge(s1_taken, i + 2)
                pv = p1_ring[:, s, :, 0:S]
                act.activation(pv, pv, ACT.Exp, scale=SCALE1).then_inc(p1_exp, 1)

            def back1(i, s, k):
                act.wait_ge(t1_mm, i + 2)
                act.wait_ge(c1_mm, i)
                act.activation(pT1[s], bank(4).rearrange("p (g r n) -> p g r n", g=4, n=QP)[:, :, :, 0:S], ACT.Copy)\
                   .then_inc(pT1_ready, 1)

            pipelined(act, PAIRS, (back1, 3), (queries1, 0), (values1, 1), (exps1, 1))
            layernorm(3)
            act.wait_ge(top_ready, 2)
            act.activation(weight[:], top[:], ACT.Sigmoid).then_inc(gate_ready, 1)

            for v in range(12):
                act.wait_ge(w_mm, v + 1)
                if v < 8:
                    dst = (gT if v < 4 else upT)[:, v % 4 // 2, 512 * (v % 2):512 * (v % 2) + 512]
                else:
                    dst = dT[:, 2 * (v - 8):2 * (v - 8) + 2, :].rearrange("p c e -> p (c e)")
                act.activation(dst, bank(v % 2), ACT.Copy).then_inc(w_ready, 1)

            def silus(bl):
                n = BLOCKS[bl][1]
                for v in range(bl * (SF // P), (bl + 1) * (SF // P)):
                    act.wait_ge(shg_mm, v + 1)
                    if v >= 2:
                        act.wait_ge(sT_ready, v - 1)
                    act.activation(sg[:, v % 2, 0:n], bank(v % 2)[:, 0:n], ACT.Silu).then_inc(silu_ready, 1)

            silus(0)

            def xfront1(i, s, k):
                act.wait_ge(rows_mm[1], i + 2)
                act.activation(rowsT[1][:, s], bank(0)[:, 0:KC * P].rearrange("p (k n) -> p k n", k=KC), ACT.Copy)\
                   .then_inc(rowsT_ready[1], 1)

            def xsilu1(i, s, k):
                act.wait_ge(hid_mm[1], i + 1)
                act.wait_ge(hid_ready[1], i)
                act.activation(hid[1][:, s, 0:FF1], bank(2 + s)[:, 0:FF1], ACT.Silu).then_inc(silu1, 1)

            def xback1(i, s, k):
                act.wait_ge(hidT_mm[1], i + 2)
                act.wait_ge(y_mm[1], i)
                act.activation(hidT[1][:, s, 0:2, :].rearrange("p c n -> p (c n)"), bank(4)[:, 0:2 * P], ACT.Copy)\
                   .then_inc(hidT_ready[1], 1)

            pipelined(act, NT1, (xfront1, 0), (xback1, 2), (xsilu1, 1))
            silus(1)
            silus(2)

        @block.vector
        def _(dve):
            ch = Chain(dve, sem("dve_chain"))

            def wide(v, n):
                return v.rearrange("p (g o) -> p g o", o=1).broadcast_to((v.shape[0], v.shape[1], n))

            def over(v, n):
                return v.rearrange("p (o g) -> p o g", o=1).broadcast_to((v.shape[0], n, v.shape[1]))

            for credit in (hid_ready[1], s_taken, s1_taken):
                dve.sem_inc(credit, 1)

            def patch_of(t):
                return x_a[:, :, :, PS * t:PS * t + PS] if t < G else x_b[:, :, :, PS * (t - G):PS * (t - G) + PS]

            def ln1(t0, t1):
                for c in range(C):
                    if t0 == 0:
                        arrived(dve, f"x_a{c}")
                    for t in range(t0, t1):
                        ch.did(dve.bn_stats(stats[:, t, c, :], patch_of(t)[:, c]))
                ch.wait()
                for t in range(t0, t1):
                    last = dve.bn_aggr(meanvar[:, t, :], stats[:, t, :, :].rearrange("p c s -> p (c s)"))
                last.then_inc(ln1_stats, 1)

            ln1(0, G)
            dve.wait_ge(consts_ready, 1)
            blk = block16[:, :, :].rearrange("p j i -> p (j i)")
            ch.did(dve.tensor_scalar(average[:], blk, 1.0 / HD0, None, ALU.mult))
            ch.wait()
            dve.tensor_tensor(out=centre[:], in0=ident[:], in1=average[:], op=ALU.subtract).then_inc(averages_ready, 1)
            dve.wait_ge(ln1_sd, 1)
            ch.did(dve.reciprocal(rstd[:, 0:G], sd[:, 0:G]))
            ch.wait()

            def norm1(t):
                if t >= 2:
                    dve.wait_ge(patch_mm, t - 1)
                dve.tensor_scalar(patch[:, t % 2].rearrange("p (c i w) -> p c i w", c=C, i=PS), patch_of(t),
                                  meanvar[:, t, 0:1], rstd[:, t:t + 1], ALU.subtract, ALU.mult).then_inc(patch_ready, 1)

            def take_z(t):
                dve.wait_ge(z_mm, t + 1)
                if t == 0:
                    dve.wait_ge(prep_out, 1)
                dve.tensor_tensor(out=xn[:, t, :], in0=bank(4 + t % 2)[:, 0:ED], in1=bias_z, op=ALU.add)\
                   .then_inc(z_taken, 1)

            def z_stats(t):
                dve.wait_ge(z_taken, t + 1)
                if t == 0:
                    dve.wait_ge(patch_ready, 1)
                ch.did(dve.bn_stats(stats[:, t, 0, :], xn[:, t, :]))

            def ln2(t0, t1):
                ch.wait()
                for t in range(t0, t1):
                    last = dve.bn_aggr(meanvar[:, t, :], stats[:, t, 0, :])
                last.then_inc(ln2_stats, 1)

            def embed(t0, t1, n):
                dve.wait_ge(ln2_sd, n)
                ch.did(dve.reciprocal(rstd[:, t0:t1], sd[:, t0:t1]))
                dve.wait_ge(pos_ready, 2)
                for t in range(t0, t1):
                    ch.did(dve.scalar_tensor_tensor(out=xn[:, t, :], in0=xn[:, t, :], scalar=meanvar[:, t, 0:1],
                                                    in1=ln2_g, op0=ALU.subtract, op1=ALU.mult))
                ch.wait()
                for t in range(t0, t1):
                    ch.did(dve.scalar_tensor_tensor(out=h[:, t, :], in0=xn[:, t, :], scalar=rstd[:, t:t + 1],
                                                    in1=h[:, t, :], op0=ALU.mult, op1=ALU.add))
                ch.wait()

            def head_sums(which):
                if which == 0:
                    arrived(dve, "attn0")
                    ch.did(dve.tensor_reduce(sv_w[0:H0, :], sparse_v[0:H0], axis=AX.X, op=ALU.add))
                    return
                ch.did(dve.tensor_reduce(so_w[0:H0, :], sparse_o[0:H0].rearrange("p k d -> p d k"), axis=AX.X,
                                         op=ALU.add))
                ch.wait()
                for dst, src in ((tiled_v, sv_w), (tiled_o, so_w)):
                    last = dve.tensor_copy(dst[0:H0, :].rearrange("p (r d) -> p r d", d=HD0), over(src[0:H0, :], 8))
                last.then_inc(tiled_ready, 1)

            norm1(0)
            norm1(1)
            arrived(dve, "proj")
            for c in range(PC):
                last = dve.tensor_scalar(wg_proj[:, c, :], w_proj[:, c, :], ln1_g[:, c:c + 1], None, ALU.mult)
            last.then_inc(folded, 1)
            for t in range(1, PATCH_TILES):
                if t == 2:
                    arrived(dve, "x_b")
                    ln1(G, PATCH_TILES)
                if t == G - 1:
                    dve.wait_ge(ln1_sd, 2)
                    ch.did(dve.reciprocal(rstd[:, G:PATCH_TILES], sd[:, G:PATCH_TILES]))
                    ch.wait()
                if t + 1 < PATCH_TILES:
                    norm1(t + 1)
                take_z(t - 1)
                if t >= 2:
                    z_stats(t - 2)
                if t == G - 3 or t == G - 2:
                    head_sums(t - (G - 3))
                if t == PATCH_TILES - 2:
                    dve.wait_ge(patch_ready, G)
                    ln2(0, G)
                    embed(0, G, 1)
            dve.wait_ge(prep_mm, 1 + PREP.index("mix") + 1)
            dve.scalar_tensor_tensor(out=blockM, in0=bank(7 - PREP.index("mix") % 2)[:, 0:P], scalar=1.0 / (P * P),
                                     in1=blk, op0=ALU.mult, op1=ALU.mult).then_inc(mixed, 1)
            z_stats(PATCH_TILES - 2)
            take_z(PATCH_TILES - 1)
            z_stats(PATCH_TILES - 1)
            ln2(G, PATCH_TILES)

            def embed_rest(t0, t1):
                if t0:
                    embed(G, PATCH_TILES, 2)
                    dve.sem_inc(embedded, 1)

            arrived(dve, "small")
            dve.tensor_tensor(out=k_of[:], in0=block16[:, 0:4, 0], in1=block16[:, 4:8, 0], op=ALU.add)\
               .then_inc(khead_ready, 1)

            def layernorm(n, bring=None):
                for half, (t0, t1) in enumerate(halves(n)):
                    if bring:
                        bring(t0, t1)
                    for t in range(t0, t1):
                        ch.did(dve.bn_stats(stats[:, t, 0, :], h[:, t, :]))
                    ch.wait()
                    for t in range(t0, t1):
                        last = dve.bn_aggr(meanvar[:, t, :], stats[:, t, 0, :])
                    last.then_inc(ln_stats, 1)
                    dve.wait_ge(ln_sd, 2 * n + half + 1)
                    ch.did(dve.reciprocal(rstd[:, t0:t1], sd[:, t0:t1]))
                    ch.wait()
                    for t in range(t0, t1):
                        dve.tensor_scalar(xn[:, t, :], h[:, t, :], meanvar[:, t, 0:1], rstd[:, t:t + 1],
                                          ALU.subtract, ALU.mult).then_inc(xn_ready, 1)

            layernorm(0, embed_rest)

            def qk_parts(v):
                which, c, bl = QK[v]
                c0, n = BLOCKS[bl]
                n0 = c0 // B
                if which:
                    return [(kn[:, c].rearrange("p b n -> p n b")[:, n0:n0 + n // B, :], 0, n // B)]
                seq = qn[:, c].rearrange("p b n -> p n b")
                parts = []
                for t in range(n0 // 4, (n0 + n // B) // 4):
                    q0 = 4 * t - n0
                    if t < G:
                        parts.append((seq[:, 1 + t:1 + t + 3 * G + 1:G, :], q0, 4))
                    else:
                        for j1 in range(2):
                            at = 1 + 4 * G + G // 2 * j1 + t - G
                            parts.append((seq[:, at:at + G + 1:G, :], q0 + 2 * j1, 2))
                if n0 + n // B == S:
                    parts.append((seq[:, 0:1, :], S - 1 - n0, 1))
                return parts

            def qk_out(v0, v1):
                for v in range(v0, v1):
                    dve.wait_ge(qk_mm, v + 1)
                    src = bank(4 + v % 4).rearrange("p (n b) -> p n b", b=B)
                    for dst, q0, m in qk_parts(v):
                        last = dve.tensor_copy(dst, src[:, q0:q0 + m, :])
                    last.then_inc(raw_ready, 1)

            def qk_normed(v0, v1):
                for v in range(v0, v1):
                    dve.wait_ge(raw_ready, v + 1)
                    dve.wait_ge(inverse_ready, v + 1)
                    inverse = sq[:, v].rearrange("p (n b) -> p n b", b=B)
                    for dst, q0, m in qk_parts(v):
                        last = dve.tensor_tensor(out=dst, in0=dst, in1=inverse[:, q0:q0 + m, :], op=ALU.mult)
                    if QK[v][0] == 0:
                        last.then_inc(q_norm, 1)
                        continue
                    last.then_inc(k_norm, 1)
                    dve.wait_ge(k_norm, sum(which for which, _, _ in QK[0:v + 1]))
                    dve.tensor_scalar(dst, dst, k_w[:, 0:1], k_b[:, 0:1], ALU.mult, ALU.add).then_inc(khead_ready, 1)

            dve.wait_ge(embedded, 1)
            qk_out(0, len(QK))
            qk_normed(0, len(QK))

            chf = Chain(dve, sem("dve_chain_max0"), 1)
            chs = Chain(dve, sem("dve_chain_sum0"), 1)
            dve.wait_ge(at0_zeroed, 1)

            def fmax(i, s, k):
                chf.at(i)
                dve.wait_ge(s_mm, i + 2)
                sc = bank(2 * s, 2).rearrange("p (j n) -> p j n", j=2)[:, :, 0:8 * S]\
                    .rearrange("p j (g n) -> p j g n", n=S)
                chf.did(dve.tensor_reduce(mx[:, s, :], sc, axis=AX.X, op=ALU.max))
                chf.wait()
                dve.wait_ge(t_mm, i)
                dve.tensor_tensor(out=p_ring[:, s, :, 0:S].rearrange("p (j g) n -> p j g n", j=2), in0=sc,
                                  in1=mx[:, s, :].rearrange("p (j g o) -> p j g o", j=2, o=1)
                                  .broadcast_to((P, 2, 8, S)), op=ALU.subtract).then_inc(s_taken, 1)

            def fctx(i, s, k):
                dve.wait_ge(c_mm, i + 2)
                dve.tensor_copy(ctxT.rearrange("p c (n b) -> p c b n", b=B)[:, :, bass.ds(i * 2, 2), :],
                                bank(7)[:, 0:4 * S].rearrange("p (c j n) -> p c j n", c=2, j=2)).then_inc(c_taken, 1)

            def fsum(i, s, k):
                chs.at(i)
                dve.wait_ge(p_exp, i + 1)
                chs.did(dve.tensor_reduce(sm[:, s, :], p_ring[:, s, :, 0:S], axis=AX.X, op=ALU.add))
                chs.wait()
                dve.reciprocal(sm[:, s, :], sm[:, s, :]).then_inc(p_sum, 1)

            pipelined(dve, PAIRS, (fmax, 0), (fctx, 2), (fsum, 0))

            def add_heads(made, taken):
                def bring(t0, t1):
                    for t in range(t0, t1):
                        dve.wait_ge(made, t + 1)
                        m = P if t < NT - 1 else B
                        dve.tensor_tensor(out=h[0:m, t, :], in0=h[0:m, t, :], in1=bank(4 + t % 4)[0:m, 0:ED],
                                          op=ALU.add).then_inc(o_taken, 1)
                    dve.wait_ge(o_taken, taken + t1)
                return bring

            dve.wait_ge(reshuffled[1], 16)
            for dst, src in to_tiles(1):
                dve.tensor_copy(dst, src).then_inc(tile_order, 1)
            layernorm(1, add_heads(o_mm, 0))

            def route(l):
                E, nt = e_of[l], nt_of[l]
                lg, mk, oh = logits[:, :, 0:E], mask[:, :, 0:E], onehot[:, :, 0:E]
                dve.wait_ge(logits_mm, l + 1)
                ch.did(dve.tensor_copy(lg, bank(3)[:, 0:NT * E].rearrange("p (t e) -> p t e", e=E)))
                ch.wait()
                ch.did(dve.tensor_reduce(top[:], lg, axis=AX.X, op=ALU.max))
                ch.wait()
                if l:
                    dve.sem_inc(top_ready, 1)
                ch.did(dve.tensor_tensor(out=mk, in0=lg, in1=wide(top[:], E), op=ALU.is_equal))
                ch.wait()
                if l == 0:
                    dve.tensor_tensor(out=lg, in0=lg, in1=wide(top[:], E), op=ALU.subtract).then_inc(top_ready, 1)
                ch.did(dve.scalar_tensor_tensor(out=mk, in0=mk, scalar=-64.0, in1=over(iota_e[:, 0:E], NT),
                                                op0=ALU.mult, op1=ALU.add))
                ch.wait()
                ch.did(dve.tensor_reduce(first[:], mk, axis=AX.X, op=ALU.min))
                ch.wait()
                ch.did(dve.tensor_tensor(out=oh, in0=mk, in1=wide(first[:], E), op=ALU.is_equal))
                ch.wait()
                ch.did(dve.memset(onehot[32:64, NT - 1, 0:E], 0.0))
                ch.did(dve.memset(onehot[64:128, NT - 1, 0:E], 0.0))
                ch.wait()
                if l == 0:
                    ch.did(dve.tensor_copy(onehot_f[:], oh))
                    ch.wait()
                dve.sem_inc(onehot_ready, 1)
                dve.wait_ge(gate_ready, l + 1)
                if l == 0:
                    ch.did(dve.tensor_reduce(weight[:], lg, axis=AX.X, op=ALU.add))
                    ch.wait()
                    ch.did(dve.reciprocal(weight[:], weight[:]))
                else:
                    for t in range(NT):
                        ch.did(dve.tensor_scalar(xn[:, t, :], xn[:, t, :], weight[:, t:t + 1], None, ALU.mult))
                ch.wait()
                dve.wait_ge(rank_mm, l + 1)
                rank = bank(5)[:, 0:NT * E].rearrange("p (t e) -> p t e", e=E)
                over_e, tl, bs, en = counts_over[:, 0:E, :], tiles_e[:, 0:E], base_e[:, 0:E], end_e[:, 0:E]
                ch.did(dve.tensor_tensor(out=over_e, in0=wide(bank(6)[:, 0:E], NT), in1=over(thresholds[:], E),
                                         op=ALU.is_gt))
                ch.wait()
                ch.did(dve.tensor_reduce(tl, over_e, axis=AX.X, op=ALU.add))
                ch.wait()
                ch.did(dve.tensor_tensor(out=base_tmp[:, 0:E, 0:E], in0=lower_e[:, 0:E, 0:E], in1=over(tl, E),
                                         op=ALU.mult))
                ch.wait()
                ch.did(dve.tensor_reduce(bs, base_tmp[:, 0:E, 0:E], axis=AX.X, op=ALU.add))
                ch.wait()
                ch.did(dve.tensor_tensor(out=en, in0=bs, in1=tl, op=ALU.add))
                ch.did(dve.scalar_tensor_tensor(out=mk, in0=over(bs, NT), scalar=float(P), in1=rank,
                                                op0=ALU.mult, op1=ALU.add))
                ch.wait()
                ch.did(dve.tensor_tensor(out=mk, in0=mk, in1=oh, op=ALU.mult))
                ch.did(dve.tensor_tensor(out=tile_cmp[0:1, 0:nt, 0:E - 1], in0=wide(iota_e[0:1, 0:nt], E - 1),
                                         in1=over(end_e[0:1, 0:E - 1], nt), op=ALU.is_ge))
                ch.wait()
                ch.did(dve.tensor_reduce(slot_f[:], mk, axis=AX.X, op=ALU.add))
                ch.did(dve.tensor_reduce(tile_e_f[0:1, 0:nt], tile_cmp[0:1, 0:nt, 0:E - 1], axis=AX.X, op=ALU.add))
                ch.wait()
                ch.did(dve.tensor_copy(slot[:, l, :], slot_f[:]))
                ch.did(dve.tensor_copy(tile_e[0:1, l, 0:nt], tile_e_f[0:1, 0:nt]))
                ch.wait()
                dve.sem_inc(slots_ready, 1)

            route(0)

            def add_gated(src, t):
                return dve.scalar_tensor_tensor(out=h[:, t, :], in0=src, scalar=weight[:, t:t + 1],
                                                in1=h[:, t, :], op0=ALU.mult, op1=ALU.add)

            for t in range(NT):
                dve.wait_ge(bias2_mm, t + 1)
                add_gated(bank(4 + t % 4)[:, 0:ED], t).then_inc(o_taken, 1)
            dve.wait_ge(o_taken, 2 * NT)

            def take_hid0(i, s, k):
                dve.wait_ge(hidT_mm[0], i)
                for half in range(2):
                    dve.wait_ge(hid_mm[0], i * 2 + half + 1)
                    dve.tensor_copy(hid[0][:, s, 512 * half:512 * half + 512], bank(2 + half)).then_inc(hid_ready[0], 1)

            def take_y(l):
                def body(i, s, k):
                    dve.wait_ge(y_mm[l], i + 2)
                    dve.wait_ge(y_stored[l][s], k * 16)
                    dve.tensor_copy(rows_out[l][:, s, :], bank(6)[:, 0:ED]).then_inc(y_ready[l], 1)
                return body

            pipelined(dve, NT0, (take_hid0, 1), (take_y(0), 2))

            def add_experts(t0, t1):
                for t in range(t0, t1):
                    dve.wait_ge(gathered[t], 16)
                    ch.did(add_gated(xn[:, t, :], t))
                ch.wait()

            layernorm(2, add_experts)

            dve.wait_ge(xn_ready, 3 * NT)
            ch.did(dve.tensor_tensor(out=h[:], in0=h[:], in1=over(bias_o[:], NT), op=ALU.add))
            ch.wait()
            chf1 = Chain(dve, sem("dve_chain_max1"), 1)
            chs1 = Chain(dve, sem("dve_chain_sum1"), 1)
            dve.wait_ge(at1_zeroed, 1)

            def fmax1(i, s, k):
                chf1.at(i)
                dve.wait_ge(s1_mm, i + 2)
                sc = bank(s)[:, 0:8 * S].rearrange("p (g n) -> p g n", n=S)
                chf1.did(dve.tensor_reduce(mx1[:, s, :], sc, axis=AX.X, op=ALU.max))
                chf1.wait()
                dve.wait_ge(t1_mm, i)
                dve.tensor_tensor(out=p1_ring[:, s, :, 0:S], in0=sc, in1=wide(mx1[:, s, :], S),
                                  op=ALU.subtract).then_inc(s1_taken, 1)

            def fctx1(i, s, k):
                dve.wait_ge(c1_mm, i + 2)
                for j in range(2):
                    ins = dve.tensor_copy(
                        ctx1T.rearrange("p r (n b) -> p r b n", b=B)[:, :, bass.ds(i * 2 + j, 1), 0:S]
                        .rearrange("p r o n -> p r (o n)"),
                        bank(7)[:, 2 * S * j:2 * S * j + 2 * S].rearrange("p (r n) -> p r n", r=2))
                    ins.then_inc(c1_taken, 1)

            def fsum1(i, s, k):
                chs1.at(i)
                dve.wait_ge(p1_exp, i + 1)
                chs1.did(dve.tensor_reduce(sm1[:, s, :], p1_ring[:, s, :, 0:S], axis=AX.X, op=ALU.add))
                chs1.wait()
                dve.reciprocal(sm1[:, s, :], sm1[:, s, :]).then_inc(p1_sum, 1)

            pipelined(dve, PAIRS, (fmax1, 0), (fctx1, 2), (fsum1, 0))
            layernorm(3, add_heads(o1_mm, 2 * NT))
            dve.wait_ge(xT_mm, 4 * NT)
            route(1)

            def shared_hidden(bl):
                n = BLOCKS[bl][1]
                if bl:
                    dve.wait_ge(sho_mm, 4 * bl)
                for f in range(SF // P):
                    v = bl * (SF // P) + f
                    dve.wait_ge(silu_ready, v + 1)
                    dve.wait_ge(shu_mm, v + 1)
                    dve.tensor_tensor(out=sT[:, f, 0:n], in0=bank(2 + v % 2)[:, 0:n], in1=sg[:, v % 2, 0:n],
                                      op=ALU.mult).then_inc(sT_ready, 1)

            def shared_out(bl):
                c0, n = BLOCKS[bl]
                for t in range(c0 // P, (c0 + n + P - 1) // P):
                    m = min(P, TOK - t * P)
                    dve.wait_ge(sho_mm, t + 1)
                    dve.tensor_tensor(out=h[0:m, t, :], in0=h[0:m, t, :], in1=bank(4 + t % 4)[0:m, 0:ED], op=ALU.add)\
                       .then_inc(sho_taken, 1)

            shared_hidden(0)
            shared_out(0)

            def take_hid1(i, s, k):
                dve.wait_ge(hidT_mm[1], i)
                dve.wait_ge(silu1, i + 1)
                dve.tensor_tensor(out=hid[1][:, s, FF1:2 * FF1], in0=bank(2 + s)[:, FF1:2 * FF1], in1=hid[1][:, s, 0:FF1],
                                  op=ALU.mult).then_inc(hid_ready[1], 1)

            pipelined(dve, NT1, (take_hid1, 1), (take_y(1), 3))
            shared_hidden(1)
            dve.wait_ge(sho_taken, 4)
            for t in range(NT):
                m = P if t < NT - 1 else B
                dve.wait_ge(gathered[t], 2 * 16)
                dve.tensor_tensor(out=h[0:m, t, :], in0=h[0:m, t, :], in1=xn[0:m, t, :], op=ALU.add)\
                   .then_inc(experts_done, 1)
            dve.wait_ge(experts_done, NT)
            shared_out(1)
            shared_hidden(2)
            shared_out(2)

        @block.tensor
        def _(pe):
            def product(dst, terms):
                for n, (l, r) in enumerate(terms):
                    last = pe.matmul(dst, l, r, start=n == 0, stop=n == len(terms) - 1)
                return last

            for ahead in (v_mm, s_mm, c_mm, t_mm, lv_mm, s1_mm, c1_mm, t1_mm, *rows_mm, *hidT_mm, *y_mm):
                pe.sem_inc(ahead, 1)

            pe.wait_ge(consts_ready, 1)
            pe.wait_ge(prep_zeroed, 1)

            def turned(dst, src, ident_n=P):
                return pe.transpose(dst, src, ident[0:ident_n, 0:ident_n])

            def prep_step(n):
                what = PREP[n]
                if n == 0:
                    arrived(pe, "attn0")
                    pe.wait_ge(averages_ready, 1)
                elif what == "uk0":
                    arrived(pe, "attn1")
                elif what == "router":
                    arrived(pe, "small")
                if n >= 2:
                    if n - 2 == MIX:
                        pe.wait_ge(mixed, 1)
                    pe.wait_ge(prep_out, prep_done(n - 2))
                b = bank(7 - n % 2)
                if what in ("q", "k"):
                    w = wq_raw if what == "q" else wk_raw
                    for m in range(KC):
                        for oc in range(KC):
                            last = pe.matmul(b[:, ED * m + P * oc:ED * m + P * oc + P], w[:, oc, P * m:P * m + P],
                                             centre[:], start=True, stop=True)
                elif what in ("v", "woT"):
                    w = wv_raw if what == "v" else wo_raw
                    for m in range(KC):
                        for oc in range(KC):
                            last = turned(b[:, ED * m + P * oc:ED * m + P * oc + P], w[:, oc, P * m:P * m + P])
                elif what == "router":
                    for m in range(KC):
                        last = turned(b[:, E1 * m:E1 * m + E1], router1[:, P * m:P * m + P], E1)
                elif what == "b1":
                    last = turned(b[:, 0:E0 * FF0 // P], b1_rows[:], E0 * FF0 // P)
                elif what in ("uk0", "uk1"):
                    for m in range(4):
                        hd = m + 4 * (what == "uk1")
                        last = turned(b[:, P * m:P * m + P], uk_raw[:, DK * hd:DK * hd + DK])
                elif what in ("uq", "uv"):
                    w = uq_raw if what == "uq" else uv_raw
                    for hd in range(H1):
                        last = turned(b[:, (DC + 1) * hd:(DC + 1) * (hd + 1)], w[0:DC + 1, DK * hd:DK * hd + DK],
                                      DC + 1)
                elif what == "keyT":
                    for hd in range(H1):
                        o = (DC + 1) * hd
                        pe.matmul(b[:, o:o + DC + 1], ukT[:, hd, :], uqT[:, hd, :], start=True, stop=False)
                        last = pe.matmul(b[:, o:o + DC + 1], qr_raw[0:DC + 1, hd, :], ident[0:DC + 1, 0:DC + 1],
                                         start=False, stop=True)
                elif what == "valO":
                    for hd in range(H1):
                        r, half = 32 * (hd // 2), hd % 2
                        last = pe.matmul(b[r:r + 32, ED * half:ED * half + ED], uvT[:, hd, 0:DC], wo1_raw[:, hd, :],
                                         start=True, stop=True)
                elif what == "bias_o":
                    last = product(b[:, 0:ED], [(uvT[:, hd, DC:DC + 1].broadcast_to((P, P)), wo1_raw[:, hd, :])
                                                for hd in range(H1)] + [(ones_row[0:1, :], b_o[0:1, :])])
                elif what == "mix":
                    pe.wait_ge(tiled_ready, 1)
                    last = pe.matmul(b[:, 0:P], tiled_o[0:H0, :], tiled_v[0:H0, :], start=True, stop=True)
                elif what == "woe":
                    pe.wait_ge(mixed, 1)
                    for m in range(KC):
                        last = pe.matmul(b[:, ED * m:ED * m + ED], blockM, woT[:, m, :], start=True, stop=True)
                last.then_inc(prep_mm, 1)

            for t in range(PATCH_TILES + 1):
                if t < PATCH_TILES:
                    pe.wait_ge(patch_ready, t + 1)
                    if t >= 2:
                        pe.wait_ge(patchT_ready, t - 1)
                    for c in range(PC):
                        last = pe.transpose(bank(2 * (t % 2), 2)[:, P * c:P * c + P], patch[:, t % 2, P * c:P * c + P],
                                            ident[:])
                    last.then_inc(patch_mm, 1)
                if t == 1:
                    arrived(pe, "proj")
                    product(bank(6)[:, 0:ED], [(ln1_b[:, c:c + 1].broadcast_to((P, P)), w_proj[:, c, :])
                                               for c in range(PC)]
                            + [(ones_row[0:1, :], b_proj[0:1, :])]).then_inc(prep_mm, 1)
                    pe.wait_ge(folded, 1)
                if t:
                    u = t - 1
                    pe.wait_ge(patchT_ready, u + 1)
                    if u >= 2:
                        pe.wait_ge(z_taken, u - 1)
                    product(bank(4 + u % 2)[:, 0:ED], [(patchT[:, u % 2, c, :], wg_proj[:, c, :]) for c in range(PC)])\
                        .then_inc(z_mm, 1)
                if t >= PREP_AT:
                    for n in range(2 * (t - PREP_AT), 2 * (t - PREP_AT) + 2):
                        prep_step(n)
            for n in range(2 * (PATCH_TILES + 1 - PREP_AT), len(PREP)):
                prep_step(n)

            def layernorm(n, router=None, between=None):
                def route_tile(t):
                    if router is not None:
                        pe.wait_ge(xT_ready, NT * n + t + 1)
                        E = router.shape[2]
                        last = product(bank(3)[:, E * t:E * t + E], [(xT[:, k, P * t:P * t + P], router[:, k, :])
                                                                     for k in range(KC)])
                        if t == NT - 1:
                            last.then_inc(logits_mm, 1)

                for t in range(NT):
                    pe.wait_ge(xn_ready, NT * n + t + 1)
                    if t >= 3:
                        pe.wait_ge(xT_ready, NT * n + t - 2)
                    for k in range(KC):
                        last = turned(bank(t % 3)[:, P * k:P * k + P], xn[:, t, P * k:P * k + P])
                    last.then_inc(xT_mm, 1)
                    if between and t == halves(n)[0][1] - 1:
                        between()
                    if t >= 2:
                        route_tile(t - 2)
                route_tile(NT - 2)
                route_tile(NT - 1)
                pe.wait_ge(xT_ready, NT * (n + 1))

            def queries_keys(v0, v1):
                for v in range(v0, v1):
                    which, c, bl = QK[v]
                    c0, n = BLOCKS[bl]
                    pe.wait_ge(xT_ready, (c0 + n + P - 1) // P)
                    if v >= 4:
                        pe.wait_ge(sq_ready, v - 3)
                    w = kT if which else qT
                    product(bank(4 + v % 4)[:, 0:n], [(w[:, k, P * c:P * c + P], xT[:, k, c0:c0 + n])
                                                      for k in range(KC)]).then_inc(qk_mm, 1)

            pe.wait_ge(prep_out, prep_done(len(PREP) - 1))
            layernorm(0, between=lambda: queries_keys(*QK_BATCHES[0]))
            for b in range(len(QK_BATCHES)):
                if b + 1 < len(QK_BATCHES):
                    queries_keys(*QK_BATCHES[b + 1])
                for u in range(*QK_BATCHES[b]):
                    n = BLOCKS[QK[u][2]][1]
                    pe.wait_ge(sq_ready, u + 1)
                    if u >= 4:
                        pe.wait_ge(log_ready, u - 3)
                    pe.matmul(bank(u % 4)[:, 0:n], average[:], sq[:, u, 0:n], start=True, stop=True)\
                      .then_inc(var_mm, 1)
            pe.wait_ge(log_ready, len(QK))

            def values0(i, s, k):
                pe.wait_ge(xv_ready, i * 2 + 2)
                pe.wait_ge(v_ready, i * 4)
                product(bank(6)[:, 0:ED], [(xv[:, s, c, :], vT[:, c, :]) for c in range(KC)]).then_inc(v_mm, 1)

            def scores0(i, s, k):
                pe.wait_ge(q_ready, i * 2 + 2)
                pe.wait_ge(k_ready, i * 2 + 2)
                pe.wait_ge(s_taken, i)
                for j in range(2):
                    for c in range(KC):
                        last = pe.matmul(bank(2 * s + j)[:, 4 * S * c:4 * S * c + 4 * S], q_ring[:, s, c, j, :],
                                         k_ring[s][:, c, j, :, :], start=True, stop=True)
                last.then_inc(s_mm, 1)

            def turn0(i, s, k):
                pe.wait_ge(p_norm, i + 1)
                pe.wait_ge(pT_ready, i)
                for g in range(8):
                    last = turned(bank(4, 2)[:, P * g:P * g + P], p_ring[:, s, 2 * g:2 * g + 2, :]
                                  .rearrange("p g n -> p (g n)"))
                last.then_inc(t_mm, 1)

            def context0(i, s, k):
                pe.wait_ge(pT_ready, i + 1)
                pe.wait_ge(v_ready, i * 4 + 4)
                pe.wait_ge(c_taken, i)
                for g in range(8):
                    j, c, pair = g // 4, g // 2 % 2, g % 2
                    for half in range(2):
                        r = 32 * (half * 2 + pair)
                        heads = c * 4 + half * 2 + pair
                        last = pe.matmul(bank(7)[r:r + 32, (2 * c + j) * S:(2 * c + j) * S + S],
                                         v_ring[:, s, j, 32 * heads:32 * heads + 32], pT[s][:, 2 * g + half, :],
                                         start=True, stop=True)
                last.then_inc(c_mm, 1)

            pipelined(pe, PAIRS, (turn0, 2), (values0, 0), (scores0, 0), (context0, 2))
            pe.wait_ge(c_taken, PAIRS)

            def heads_out(tokens, w, done, before_):
                for t in range(NT):
                    m = P if t < NT - 1 else B
                    if t >= 4:
                        pe.wait_ge(o_taken, before_ + t - 3)
                    product(bank(4 + t % 4)[0:m, 0:ED], [(tokens(c, t), w[:, c, :]) for c in range(2)])\
                        .then_inc(done, 1)

            pe.wait_ge(tile_order, 8)
            heads_out(lambda c, t: ctxT[:, c, P * t:P * t + (P if t < NT - 1 else B)], woe, o_mm, 0)
            layernorm(1, gate_w0)

            def turn_shared_weights():
                arrived(pe, "shared")
                for v in range(12):
                    if v >= 2:
                        pe.wait_ge(w_ready, v - 1)
                    for q in range(4):
                        if v < 8:
                            f, m = 4 * (v % 2) + q, v % 4 // 2
                            src = (g_raw if v < 4 else up_raw)[:, f, P * m:P * m + P]
                        else:
                            f, m = 2 * (v - 8) + q // 2, q % 2
                            src = d_raw[:, m, P * f:P * f + P]
                        last = turned(bank(v % 2)[:, P * q:P * q + P], src)
                    last.then_inc(w_mm, 1)
                pe.wait_ge(w_ready, 12)

            def route(l):
                E = e_of[l]
                if l:
                    turn_shared_weights()
                pe.wait_ge(onehot_ready, l + 1)
                oh = onehot[:, :, 0:E]
                rank = bank(5)[:, 0:NT * E].rearrange("p (t e) -> p t e", e=E)
                pe.matmul(rank, before[:], oh, start=True, stop=False)
                for d in range(1, NT):
                    pe.matmul(rank[:, d:NT, :], ones16[:], oh[:, 0:NT - d, :], start=False, stop=d == NT - 1)
                for t in range(NT):
                    last = pe.matmul(bank(6)[:, 0:E], ones16[:], oh[:, t, :], start=t == 0, stop=t == NT - 1)
                last.then_inc(rank_mm, 1)

            route(0)
            pe.wait_ge(slots_ready, 1)
            for n in range(3):
                m = min(4, NT - 4 * n)
                for t in range(4 * n, 4 * n + m):
                    last = turned(bank(5 + n)[0:E0, P * (t - 4 * n):P * (t - 4 * n) + P], onehot_f[:, t, :])
                last.then_inc(ohT_mm, 1)
            pe.wait_ge(ohT_ready, 3)
            for t in range(NT):
                pe.wait_ge(o_taken, NT + max(0, t - 3))
                pe.matmul(bank(4 + t % 4)[:, 0:ED], onehotT[0:E0, t, :], b2[:], start=True, stop=True).then_inc(bias2_mm, 1)
            pe.wait_ge(o_taken, 2 * NT)
            arrived(pe, "w1")
            arrived(pe, "w2")

            expert = {}

            def expert_of(l, use):
                def body(i, s, k):
                    expert[use] = pe.value_load(tile_e[0:1, l, bass.ds(i, 1)], min_val=0, max_val=e_of[l] - 1)
                return body

            def turn_rows(l):
                def body(i, s, k):
                    pe.wait_ge(rows_loaded[l][s], k * 16 + 16)
                    pe.wait_ge(rowsT_ready[l], i)
                    for c in range(KC):
                        last = turned(bank(0)[:, P * c:P * c + P], rows_in[l][:, s, P * c:P * c + P])
                    last.then_inc(rows_mm[l], 1)
                return body

            def hidden0(i, s, k):
                e = expert["hidden"]
                pe.wait_ge(rowsT_ready[0], i + 1)
                for half in range(2):
                    if not (isinstance(i, int) and i == 0):
                        pe.wait_ge(hid_ready[0], i * 2 + (half - 1))
                    product(bank(2 + half), [(rowsT[0][:, s, c, :], w1[:, bass.ds(e * (KC * FF0) + FF0 * c + 512 * half, 512)])
                                             for c in range(KC)]).then_inc(hid_mm[0], 1)

            def turn_hidden0(i, s, k):
                pe.wait_ge(hid_ready[0], i * 2 + 2)
                pe.wait_ge(hidT_ready[0], i * 8)
                for c in range(FF0 // P):
                    last = turned(bank(4, 2)[:, P * c:P * c + P], hid[0][:, s, P * c:P * c + P])
                last.then_inc(hidT_mm[0], 1)

            def out0(i, s, k):
                e = expert["out"]
                pe.wait_ge(hidT_ready[0], i * 8 + 8)
                pe.wait_ge(y_ready[0], i)
                product(bank(6)[:, 0:ED], [(hidT[0][:, s, c, :], w2[:, bass.ds(e * (FF0 // P * ED) + ED * c, ED)])
                                           for c in range(FF0 // P)]).then_inc(y_mm[0], 1)

            pipelined(pe, NT0, (expert_of(0, "hidden"), 1), (expert_of(0, "out"), 2), (turn_rows(0), 0), (turn_hidden0, 2), (hidden0, 1), (out0, 2))

            def latents(v0, v1):
                for v in range(v0, v1):
                    which, bl = LATENTS[v]
                    c0, n = BLOCKS[bl]
                    pe.wait_ge(xT_ready, 2 * NT + (c0 + n + P - 1) // P)
                    if v >= 4:
                        pe.wait_ge(lat_ready, v - 3)
                    product(bank(4 + v % 4)[:, 0:n], [((down_u, down_k)[which][:, k, :], xT[:, k, c0:c0 + n])
                                                      for k in range(KC)]).then_inc(lat_mm, 1)

            pe.wait_ge(y_ready[0], NT0)
            layernorm(2, between=lambda: latents(0, 2))
            latents(2, 6)
            pe.wait_ge(lat_ready, 6)
            for v in range(12):
                c0, n = BLOCKS[v % 3]
                if v >= 4:
                    pe.wait_ge(keys_ready, v - 3)
                pe.matmul(bank(v % 4)[:, 0:n], keyT[:, v // 3, :], lat_k[:, c0:c0 + n], start=True, stop=True)\
                  .then_inc(keys_mm, 1)
            pe.wait_ge(keys_ready, 12)

            def scores1(i, s, k):
                pe.wait_ge(lk_ready, i + 1)
                pe.wait_ge(lv_ready, i * 4)
                turned(bank(6)[:, 0:P], lk_ring[:, s, :]).then_inc(lv_mm, 1)
                pe.wait_ge(u_ready, i * 2 + 2)
                pe.wait_ge(s1_taken, i)
                for j in range(2):
                    last = pe.matmul(bank(s)[:, 4 * S * j:4 * S * j + 4 * S], u_ring[:, s, j, :],
                                     keys[:, :, bass.ds(i * (2 * S) + S * j, S)], start=True, stop=True)
                last.then_inc(s1_mm, 1)

            def turn1(i, s, k):
                pe.wait_ge(p1_norm, i + 2)
                pe.wait_ge(pT1_ready, i)
                for g in range(4):
                    last = turned(bank(4)[:, P * g:P * g + P], p1_ring[:, s, 2 * g:2 * g + 2, :]
                                  .rearrange("p g n -> p (g n)"))
                last.then_inc(t1_mm, 1)

            def context1(i, s, k):
                pe.wait_ge(pT1_ready, i + 1)
                pe.wait_ge(lv_ready, i * 4 + 4)
                pe.wait_ge(c1_taken, i * 2)
                for g in range(4):
                    j, half = g // 2, g % 2
                    last = pe.matmul(bank(7)[64 * half:64 * half + 64, 2 * S * j:2 * S * j + 2 * S],
                                     lat_v[:, s, j, :], pT1[s][:, g, :, :].rearrange("p r n -> p (r n)"),
                                     start=True, stop=True)
                last.then_inc(c1_mm, 1)

            pipelined(pe, PAIRS, (turn1, 2), (scores1, 0), (context1, 2))
            pe.wait_ge(c1_taken, 2 * PAIRS)
            heads_out(lambda c, t: ctx1T[:, c, P * t:P * t + (P if t < NT - 1 else B)], valO, o1_mm, 2 * NT)
            layernorm(3, routerT1)
            route(1)

            def shared_block(bl):
                c0, n = BLOCKS[bl]
                for f in range(SF // P):
                    v = bl * (SF // P) + f
                    if v >= 2:
                        pe.wait_ge(silu_ready, v - 1)
                    product(bank(v % 2)[:, 0:n], [(gT[:, k, P * f:P * f + P], xT[:, k, c0:c0 + n]) for k in range(KC)])\
                        .then_inc(shg_mm, 1)
                    if v >= 2:
                        pe.wait_ge(sT_ready, v - 1)
                    product(bank(2 + v % 2)[:, 0:n], [(upT[:, k, P * f:P * f + P], xT[:, k, c0:c0 + n])
                                                      for k in range(KC)]).then_inc(shu_mm, 1)
                pe.wait_ge(sT_ready, (bl + 1) * (SF // P))
                pe.wait_ge(slots_ready, 2)
                for t in range(c0 // P, (c0 + n + P - 1) // P):
                    m = min(P, TOK - t * P)
                    if t >= 4:
                        pe.wait_ge(sho_taken, t - 3)
                    product(bank(4 + t % 4)[0:m, 0:ED], [(sT[:, f, P * t - c0:P * t - c0 + m], dT[:, f, :])
                                                         for f in range(SF // P)]).then_inc(sho_mm, 1)

            shared_block(0)
            pe.wait_ge(sho_taken, 4)
            arrived(pe, "gate_up")
            arrived(pe, "down")

            def hidden1(i, s, k):
                e = expert["hidden"]
                pe.wait_ge(rowsT_ready[1], i + 1)
                pe.wait_ge(hid_ready[1], i)
                product(bank(2 + s), [(rowsT[1][:, s, c, :], gate_up[:, bass.ds(e * (KC * 2 * FF1) + 2 * FF1 * c, 2 * FF1)])
                                      for c in range(KC)]).then_inc(hid_mm[1], 1)

            def turn_hidden1(i, s, k):
                pe.wait_ge(hid_ready[1], i + 2)
                pe.wait_ge(hidT_ready[1], i)
                for c in range(FF1 // P):
                    last = turned(bank(4)[:, P * c:P * c + P], hid[1][:, s, FF1 + P * c:FF1 + P * c + P])
                last.then_inc(hidT_mm[1], 1)

            def out1(i, s, k):
                e = expert["out"]
                pe.wait_ge(hidT_ready[1], i + 1)
                pe.wait_ge(y_ready[1], i)
                product(bank(6)[:, 0:ED], [(hidT[1][:, s, c, :], down[:, bass.ds(e * (FF1 // P * ED) + ED * c, ED)])
                                           for c in range(FF1 // P)]).then_inc(y_mm[1], 1)

            pipelined(pe, NT1, (expert_of(1, "hidden"), 1), (expert_of(1, "out"), 3), (turn_rows(1), 0), (hidden1, 1), (turn_hidden1, 2), (out1, 3))
            pe.wait_ge(y_ready[1], NT1)
            shared_block(1)
            shared_block(2)


def kernel(**inputs):
    import numpy as np
    import concourse.bacc as bacc
    from concourse.bass_utils import run_bass_kernel_spmd as run

    nc = bacc.Bacc("TRN2", target_bir_lowering=False, num_devices=1)
    arrays, args = {}, {}
    for name, value in inputs.items():
        v = np.ascontiguousarray(value)
        arrays[f"in_{name}"] = v
        args[name] = nc.dram_tensor(f"in_{name}", v.shape, mybir.dt.from_np(v.dtype), kind="ExternalInput").ap()
    out = nc.dram_tensor("out", (B, S, ED), F32, kind="ExternalOutput").ap()
    vit_tower(nc, args, out)
    r = run(nc, [arrays], core_ids=[0])
    return r.results[0]["out"]
```
